# Optimizing a Trainium2 kernel written in Bass

```python
import numpy as np
import jax
import jax.numpy as jnp

def _softmax(x, axis=-1):
    return jax.nn.softmax(x, axis=axis)

def _gelu(x):
    return jax.nn.gelu(x, approximate=True)

def _silu(x):
    return jax.nn.silu(x)

def _sigmoid(x):
    return jax.nn.sigmoid(x)

def _layernorm(x, axis=-1, eps=1e-05):
    m = jnp.mean(x, axis=axis, keepdims=True)
    v = jnp.var(x, axis=axis, keepdims=True)
    return (x - m) / jnp.sqrt(v + eps)

def _scatter_add(tgt, idx, src, axis=0):
    return tgt.at[idx].add(src)

def _segment_sum(src, seg, n):
    return jax.ops.segment_sum(src, seg, n)
kernel_name = 'mk_rec_standalone_d1_rec_r8_a0369a'

def setup_inputs(seed: int=0):
    np.random.seed(seed)
    _w = jnp.asarray

    def _rec_inputs():
        import jax
        import jax.numpy as jnp
        _rk = jax.random.key(seed)
        r_num_feat1 = -0.0580273 + 0.99462 * jax.random.normal(jax.random.fold_in(_rk, 1), (512,), jnp.float32)
        r_num_feat2 = -0.0209273 + 1.04763 * jax.random.normal(jax.random.fold_in(_rk, 2), (512,), jnp.float32)
        r_score = jax.random.uniform(jax.random.fold_in(_rk, 3), (512,), jnp.float32, 0.0, 0.949735)
        r_user_id = jax.random.randint(jax.random.fold_in(_rk, 4), (512,), 52, 99938, jnp.int32)
        r_cand_item_id = jax.random.randint(jax.random.fold_in(_rk, 5), (512,), 110, 99915, jnp.int32)
        r_cand_item_cat = jax.random.randint(jax.random.fold_in(_rk, 6), (512,), 1, 1000, jnp.int32)
        r_exp_item_id = jnp.stack([jax.random.randint(jax.random.fold_in(jax.random.fold_in(_rk, 7), 0), (512,), 124, 12498, jnp.int32), jax.random.randint(jax.random.fold_in(jax.random.fold_in(_rk, 7), 1), (512,), 82, 99347, jnp.int32), jax.random.randint(jax.random.fold_in(jax.random.fold_in(_rk, 7), 2), (512,), 7, 99989, jnp.int32), jax.random.randint(jax.random.fold_in(jax.random.fold_in(_rk, 7), 3), (512,), 167, 99978, jnp.int32), jax.random.randint(jax.random.fold_in(jax.random.fold_in(_rk, 7), 4), (512,), 25, 99999, jnp.int32), jax.random.randint(jax.random.fold_in(jax.random.fold_in(_rk, 7), 5), (512,), 117, 99739, jnp.int32), jax.random.randint(jax.random.fold_in(jax.random.fold_in(_rk, 7), 6), (512,), 151, 99855, jnp.int32), jax.random.randint(jax.random.fold_in(jax.random.fold_in(_rk, 7), 7), (512,), 26, 12500, jnp.int32), jax.random.randint(jax.random.fold_in(jax.random.fold_in(_rk, 7), 8), (512,), 36, 99751, jnp.int32), jax.random.randint(jax.random.fold_in(jax.random.fold_in(_rk, 7), 9), (512,), 40, 99999, jnp.int32), jax.random.randint(jax.random.fold_in(jax.random.fold_in(_rk, 7), 10), (512,), 148, 99826, jnp.int32), jax.random.randint(jax.random.fold_in(jax.random.fold_in(_rk, 7), 11), (512,), 43, 99793, jnp.int32), jax.random.randint(jax.random.fold_in(jax.random.fold_in(_rk, 7), 12), (512,), 53, 99961, jnp.int32), jax.random.randint(jax.random.fold_in(jax.random.fold_in(_rk, 7), 13), (512,), 52, 99973, jnp.int32), jax.random.randint(jax.random.fold_in(jax.random.fold_in(_rk, 7), 14), (512,), 25, 99956, jnp.int32), jax.random.randint(jax.random.fold_in(jax.random.fold_in(_rk, 7), 15), (512,), 72, 99996, jnp.int32), jax.random.randint(jax.random.fold_in(jax.random.fold_in(_rk, 7), 16), (512,), 2, 12485, jnp.int32), jax.random.randint(jax.random.fold_in(jax.random.fold_in(_rk, 7), 17), (512,), 30, 99987, jnp.int32), jax.random.randint(jax.random.fold_in(jax.random.fold_in(_rk, 7), 18), (512,), 174, 12498, jnp.int32), jax.random.randint(jax.random.fold_in(jax.random.fold_in(_rk, 7), 19), (512,), 108, 99957, jnp.int32), jax.random.randint(jax.random.fold_in(jax.random.fold_in(_rk, 7), 20), (512,), 69, 99934, jnp.int32), jax.random.randint(jax.random.fold_in(jax.random.fold_in(_rk, 7), 21), (512,), 76, 99844, jnp.int32), jax.random.randint(jax.random.fold_in(jax.random.fold_in(_rk, 7), 22), (512,), 12, 99862, jnp.int32), jax.random.randint(jax.random.fold_in(jax.random.fold_in(_rk, 7), 23), (512,), 203, 99607, jnp.int32), jax.random.randint(jax.random.fold_in(jax.random.fold_in(_rk, 7), 24), (512,), 52, 12493, jnp.int32), jax.random.randint(jax.random.fold_in(jax.random.fold_in(_rk, 7), 25), (512,), 31, 99841, jnp.int32), jax.random.randint(jax.random.fold_in(jax.random.fold_in(_rk, 7), 26), (512,), 71, 99987, jnp.int32), jax.random.randint(jax.random.fold_in(jax.random.fold_in(_rk, 7), 27), (512,), 63, 99881, jnp.int32), jax.random.randint(jax.random.fold_in(jax.random.fold_in(_rk, 7), 28), (512,), 62, 99903, jnp.int32), jax.random.randint(jax.random.fold_in(jax.random.fold_in(_rk, 7), 29), (512,), 137, 99759, jnp.int32), jax.random.randint(jax.random.fold_in(jax.random.fold_in(_rk, 7), 30), (512,), 60, 99820, jnp.int32), jax.random.randint(jax.random.fold_in(jax.random.fold_in(_rk, 7), 31), (512,), 85, 99675, jnp.int32), jax.random.randint(jax.random.fold_in(jax.random.fold_in(_rk, 7), 32), (512,), 95, 99958, jnp.int32), jax.random.randint(jax.random.fold_in(jax.random.fold_in(_rk, 7), 33), (512,), 222, 99898, jnp.int32), jax.random.randint(jax.random.fold_in(jax.random.fold_in(_rk, 7), 34), (512,), 53, 12468, jnp.int32), jax.random.randint(jax.random.fold_in(jax.random.fold_in(_rk, 7), 35), (512,), 44, 99945, jnp.int32), jax.random.randint(jax.random.fold_in(jax.random.fold_in(_rk, 7), 36), (512,), 82, 99940, jnp.int32), jax.random.randint(jax.random.fold_in(jax.random.fold_in(_rk, 7), 37), (512,), 268, 12500, jnp.int32), jax.random.randint(jax.random.fold_in(jax.random.fold_in(_rk, 7), 38), (512,), 68, 12498, jnp.int32), jax.random.randint(jax.random.fold_in(jax.random.fold_in(_rk, 7), 39), (512,), 16, 99972, jnp.int32), jax.random.randint(jax.random.fold_in(jax.random.fold_in(_rk, 7), 40), (512,), 154, 12494, jnp.int32), jax.random.randint(jax.random.fold_in(jax.random.fold_in(_rk, 7), 41), (512,), 122, 99967, jnp.int32), jax.random.randint(jax.random.fold_in(jax.random.fold_in(_rk, 7), 42), (512,), 241, 99895, jnp.int32), jax.random.randint(jax.random.fold_in(jax.random.fold_in(_rk, 7), 43), (512,), 120, 99755, jnp.int32), jax.random.randint(jax.random.fold_in(jax.random.fold_in(_rk, 7), 44), (512,), 99, 99951, jnp.int32), jax.random.randint(jax.random.fold_in(jax.random.fold_in(_rk, 7), 45), (512,), 103, 99923, jnp.int32), jax.random.randint(jax.random.fold_in(jax.random.fold_in(_rk, 7), 46), (512,), 308, 12493, jnp.int32), jax.random.randint(jax.random.fold_in(jax.random.fold_in(_rk, 7), 47), (512,), 135, 99778, jnp.int32), jax.random.randint(jax.random.fold_in(jax.random.fold_in(_rk, 7), 48), (512,), 15, 12477, jnp.int32), jax.random.randint(jax.random.fold_in(jax.random.fold_in(_rk, 7), 49), (512,), 73, 12500, jnp.int32), jax.random.randint(jax.random.fold_in(jax.random.fold_in(_rk, 7), 50), (512,), 108, 99698, jnp.int32), jax.random.randint(jax.random.fold_in(jax.random.fold_in(_rk, 7), 51), (512,), 125, 99682, jnp.int32), jax.random.randint(jax.random.fold_in(jax.random.fold_in(_rk, 7), 52), (512,), 204, 99980, jnp.int32), jax.random.randint(jax.random.fold_in(jax.random.fold_in(_rk, 7), 53), (512,), 26, 99965, jnp.int32), jax.random.randint(jax.random.fold_in(jax.random.fold_in(_rk, 7), 54), (512,), 20, 99771, jnp.int32), jax.random.randint(jax.random.fold_in(jax.random.fold_in(_rk, 7), 55), (512,), 58, 99676, jnp.int32), jax.random.randint(jax.random.fold_in(jax.random.fold_in(_rk, 7), 56), (512,), 13, 99970, jnp.int32), jax.random.randint(jax.random.fold_in(jax.random.fold_in(_rk, 7), 57), (512,), 12, 99765, jnp.int32), jax.random.randint(jax.random.fold_in(jax.random.fold_in(_rk, 7), 58), (512,), 16, 99949, jnp.int32), jax.random.randint(jax.random.fold_in(jax.random.fold_in(_rk, 7), 59), (512,), 230, 99811, jnp.int32), jax.random.randint(jax.random.fold_in(jax.random.fold_in(_rk, 7), 60), (512,), 82, 99666, jnp.int32), jax.random.randint(jax.random.fold_in(jax.random.fold_in(_rk, 7), 61), (512,), 124, 99877, jnp.int32), jax.random.randint(jax.random.fold_in(jax.random.fold_in(_rk, 7), 62), (512,), 57, 99995, jnp.int32), jax.random.randint(jax.random.fold_in(jax.random.fold_in(_rk, 7), 63), (512,), 164, 99966, jnp.int32), jax.random.randint(jax.random.fold_in(jax.random.fold_in(_rk, 7), 64), (512,), 65, 99955, jnp.int32), jax.random.randint(jax.random.fold_in(jax.random.fold_in(_rk, 7), 65), (512,), 1, 99958, jnp.int32), jax.random.randint(jax.random.fold_in(jax.random.fold_in(_rk, 7), 66), (512,), 69, 99902, jnp.int32), jax.random.randint(jax.random.fold_in(jax.random.fold_in(_rk, 7), 67), (512,), 146, 99685, jnp.int32), jax.random.randint(jax.random.fold_in(jax.random.fold_in(_rk, 7), 68), (512,), 59, 99956, jnp.int32), jax.random.randint(jax.random.fold_in(jax.random.fold_in(_rk, 7), 69), (512,), 72, 99945, jnp.int32), jax.random.randint(jax.random.fold_in(jax.random.fold_in(_rk, 7), 70), (512,), 58, 99870, jnp.int32), jax.random.randint(jax.random.fold_in(jax.random.fold_in(_rk, 7), 71), (512,), 8, 99948, jnp.int32), jax.random.randint(jax.random.fold_in(jax.random.fold_in(_rk, 7), 72), (512,), 53, 99841, jnp.int32), jax.random.randint(jax.random.fold_in(jax.random.fold_in(_rk, 7), 73), (512,), 243, 99998, jnp.int32), jax.random.randint(jax.random.fold_in(jax.random.fold_in(_rk, 7), 74), (512,), 45, 99993, jnp.int32), jax.random.randint(jax.random.fold_in(jax.random.fold_in(_rk, 7), 75), (512,), 71, 99873, jnp.int32), jax.random.randint(jax.random.fold_in(jax.random.fold_in(_rk, 7), 76), (512,), 8, 99717, jnp.int32), jax.random.randint(jax.random.fold_in(jax.random.fold_in(_rk, 7), 77), (512,), 54, 99908, jnp.int32), jax.random.randint(jax.random.fold_in(jax.random.fold_in(_rk, 7), 78), (512,), 66, 99934, jnp.int32), jax.random.randint(jax.random.fold_in(jax.random.fold_in(_rk, 7), 79), (512,), 48, 99956, jnp.int32), jax.random.randint(jax.random.fold_in(jax.random.fold_in(_rk, 7), 80), (512,), 99, 99915, jnp.int32), jax.random.randint(jax.random.fold_in(jax.random.fold_in(_rk, 7), 81), (512,), 108, 99917, jnp.int32), jax.random.randint(jax.random.fold_in(jax.random.fold_in(_rk, 7), 82), (512,), 49, 99639, jnp.int32), jax.random.randint(jax.random.fold_in(jax.random.fold_in(_rk, 7), 83), (512,), 189, 99887, jnp.int32), jax.random.randint(jax.random.fold_in(jax.random.fold_in(_rk, 7), 84), (512,), 160, 99972, jnp.int32), jax.random.randint(jax.random.fold_in(jax.random.fold_in(_rk, 7), 85), (512,), 93, 99974, jnp.int32), jax.random.randint(jax.random.fold_in(jax.random.fold_in(_rk, 7), 86), (512,), 45, 99975, jnp.int32), jax.random.randint(jax.random.fold_in(jax.random.fold_in(_rk, 7), 87), (512,), 16, 99908, jnp.int32), jax.random.randint(jax.random.fold_in(jax.random.fold_in(_rk, 7), 88), (512,), 101, 99892, jnp.int32), jax.random.randint(jax.random.fold_in(jax.random.fold_in(_rk, 7), 89), (512,), 33, 12496, jnp.int32), jax.random.randint(jax.random.fold_in(jax.random.fold_in(_rk, 7), 90), (512,), 11, 99899, jnp.int32), jax.random.randint(jax.random.fold_in(jax.random.fold_in(_rk, 7), 91), (512,), 96, 99924, jnp.int32), jax.random.randint(jax.random.fold_in(jax.random.fold_in(_rk, 7), 92), (512,), 77, 99666, jnp.int32), jax.random.randint(jax.random.fold_in(jax.random.fold_in(_rk, 7), 93), (512,), 30, 99901, jnp.int32), jax.random.randint(jax.random.fold_in(jax.random.fold_in(_rk, 7), 94), (512,), 242, 99991, jnp.int32), jax.random.randint(jax.random.fold_in(jax.random.fold_in(_rk, 7), 95), (512,), 155, 99661, jnp.int32), jax.random.randint(jax.random.fold_in(jax.random.fold_in(_rk, 7), 96), (512,), 17, 99970, jnp.int32), jax.random.randint(jax.random.fold_in(jax.random.fold_in(_rk, 7), 97), (512,), 71, 99882, jnp.int32), jax.random.randint(jax.random.fold_in(jax.random.fold_in(_rk, 7), 98), (512,), 294, 12500, jnp.int32), jax.random.randint(jax.random.fold_in(jax.random.fold_in(_rk, 7), 99), (512,), 19, 99845, jnp.int32), jax.random.randint(jax.random.fold_in(jax.random.fold_in(_rk, 7), 100), (512,), 48, 99918, jnp.int32), jax.random.randint(jax.random.fold_in(jax.random.fold_in(_rk, 7), 101), (512,), 39, 99989, jnp.int32), jax.random.randint(jax.random.fold_in(jax.random.fold_in(_rk, 7), 102), (512,), 44, 99997, jnp.int32), jax.random.randint(jax.random.fold_in(jax.random.fold_in(_rk, 7), 103), (512,), 201, 12488, jnp.int32), jax.random.randint(jax.random.fold_in(jax.random.fold_in(_rk, 7), 104), (512,), 22, 99962, jnp.int32), jax.random.randint(jax.random.fold_in(jax.random.fold_in(_rk, 7), 105), (512,), 195, 99898, jnp.int32), jax.random.randint(jax.random.fold_in(jax.random.fold_in(_rk, 7), 106), (512,), 10, 12499, jnp.int32), jax.random.randint(jax.random.fold_in(jax.random.fold_in(_rk, 7), 107), (512,), 53, 99869, jnp.int32), jax.random.randint(jax.random.fold_in(jax.random.fold_in(_rk, 7), 108), (512,), 124, 99997, jnp.int32), jax.random.randint(jax.random.fold_in(jax.random.fold_in(_rk, 7), 109), (512,), 84, 99955, jnp.int32), jax.random.randint(jax.random.fold_in(jax.random.fold_in(_rk, 7), 110), (512,), 82, 99939, jnp.int32), jax.random.randint(jax.random.fold_in(jax.random.fold_in(_rk, 7), 111), (512,), 125, 99985, jnp.int32), jax.random.randint(jax.random.fold_in(jax.random.fold_in(_rk, 7), 112), (512,), 6, 99997, jnp.int32), jax.random.randint(jax.random.fold_in(jax.random.fold_in(_rk, 7), 113), (512,), 58, 99833, jnp.int32), jax.random.randint(jax.random.fold_in(jax.random.fold_in(_rk, 7), 114), (512,), 70, 99945, jnp.int32), jax.random.randint(jax.random.fold_in(jax.random.fold_in(_rk, 7), 115), (512,), 9, 99763, jnp.int32), jax.random.randint(jax.random.fold_in(jax.random.fold_in(_rk, 7), 116), (512,), 20, 99963, jnp.int32), jax.random.randint(jax.random.fold_in(jax.random.fold_in(_rk, 7), 117), (512,), 173, 99986, jnp.int32), jax.random.randint(jax.random.fold_in(jax.random.fold_in(_rk, 7), 118), (512,), 24, 99938, jnp.int32), jax.random.randint(jax.random.fold_in(jax.random.fold_in(_rk, 7), 119), (512,), 139, 99409, jnp.int32), jax.random.randint(jax.random.fold_in(jax.random.fold_in(_rk, 7), 120), (512,), 7, 99962, jnp.int32), jax.random.randint(jax.random.fold_in(jax.random.fold_in(_rk, 7), 121), (512,), 93, 99973, jnp.int32), jax.random.randint(jax.random.fold_in(jax.random.fold_in(_rk, 7), 122), (512,), 138, 99987, jnp.int32), jax.random.randint(jax.random.fold_in(jax.random.fold_in(_rk, 7), 123), (512,), 121, 99874, jnp.int32), jax.random.randint(jax.random.fold_in(jax.random.fold_in(_rk, 7), 124), (512,), 1, 99945, jnp.int32), jax.random.randint(jax.random.fold_in(jax.random.fold_in(_rk, 7), 125), (512,), 49, 99910, jnp.int32), jax.random.randint(jax.random.fold_in(jax.random.fold_in(_rk, 7), 126), (512,), 373, 99796, jnp.int32), jax.random.randint(jax.random.fold_in(jax.random.fold_in(_rk, 7), 127), (512,), 175, 99915, jnp.int32), jax.random.randint(jax.random.fold_in(jax.random.fold_in(_rk, 7), 128), (512,), 42, 99969, jnp.int32), jax.random.randint(jax.random.fold_in(jax.random.fold_in(_rk, 7), 129), (512,), 91, 12494, jnp.int32), jax.random.randint(jax.random.fold_in(jax.random.fold_in(_rk, 7), 130), (512,), 164, 99963, jnp.int32), jax.random.randint(jax.random.fold_in(jax.random.fold_in(_rk, 7), 131), (512,), 76, 99498, jnp.int32), jax.random.randint(jax.random.fold_in(jax.random.fold_in(_rk, 7), 132), (512,), 7, 99839, jnp.int32), jax.random.randint(jax.random.fold_in(jax.random.fold_in(_rk, 7), 133), (512,), 145, 99851, jnp.int32), jax.random.randint(jax.random.fold_in(jax.random.fold_in(_rk, 7), 134), (512,), 14, 99892, jnp.int32), jax.random.randint(jax.random.fold_in(jax.random.fold_in(_rk, 7), 135), (512,), 10, 99961, jnp.int32), jax.random.randint(jax.random.fold_in(jax.random.fold_in(_rk, 7), 136), (512,), 235, 12486, jnp.int32), jax.random.randint(jax.random.fold_in(jax.random.fold_in(_rk, 7), 137), (512,), 222, 99973, jnp.int32), jax.random.randint(jax.random.fold_in(jax.random.fold_in(_rk, 7), 138), (512,), 96, 99983, jnp.int32), jax.random.randint(jax.random.fold_in(jax.random.fold_in(_rk, 7), 139), (512,), 59, 12490, jnp.int32), jax.random.randint(jax.random.fold_in(jax.random.fold_in(_rk, 7), 140), (512,), 88, 12473, jnp.int32), jax.random.randint(jax.random.fold_in(jax.random.fold_in(_rk, 7), 141), (512,), 15, 99887, jnp.int32), jax.random.randint(jax.random.fold_in(jax.random.fold_in(_rk, 7), 142), (512,), 128, 99798, jnp.int32), jax.random.randint(jax.random.fold_in(jax.random.fold_in(_rk, 7), 143), (512,), 51, 99914, jnp.int32), jax.random.randint(jax.random.fold_in(jax.random.fold_in(_rk, 7), 144), (512,), 24, 12455, jnp.int32), jax.random.randint(jax.random.fold_in(jax.random.fold_in(_rk, 7), 145), (512,), 23, 99961, jnp.int32), jax.random.randint(jax.random.fold_in(jax.random.fold_in(_rk, 7), 146), (512,), 59, 12499, jnp.int32), jax.random.randint(jax.random.fold_in(jax.random.fold_in(_rk, 7), 147), (512,), 208, 99935, jnp.int32), jax.random.randint(jax.random.fold_in(jax.random.fold_in(_rk, 7), 148), (512,), 152, 99740, jnp.int32), jax.random.randint(jax.random.fold_in(jax.random.fold_in(_rk, 7), 149), (512,), 264, 99955, jnp.int32), jax.random.randint(jax.random.fold_in(jax.random.fold_in(_rk, 7), 150), (512,), 33, 99777, jnp.int32), jax.random.randint(jax.random.fold_in(jax.random.fold_in(_rk, 7), 151), (512,), 54, 99871, jnp.int32), jax.random.randint(jax.random.fold_in(jax.random.fold_in(_rk, 7), 152), (512,), 238, 99493, jnp.int32), jax.random.randint(jax.random.fold_in(jax.random.fold_in(_rk, 7), 153), (512,), 69, 99778, jnp.int32), jax.random.randint(jax.random.fold_in(jax.random.fold_in(_rk, 7), 154), (512,), 130, 99654, jnp.int32), jax.random.randint(jax.random.fold_in(jax.random.fold_in(_rk, 7), 155), (512,), 120, 99827, jnp.int32), jax.random.randint(jax.random.fold_in(jax.random.fold_in(_rk, 7), 156), (512,), 120, 12495, jnp.int32), jax.random.randint(jax.random.fold_in(jax.random.fold_in(_rk, 7), 157), (512,), 24, 99994, jnp.int32), jax.random.randint(jax.random.fold_in(jax.random.fold_in(_rk, 7), 158), (512,), 23, 99870, jnp.int32), jax.random.randint(jax.random.fold_in(jax.random.fold_in(_rk, 7), 159), (512,), 10, 99929, jnp.int32), jax.random.randint(jax.random.fold_in(jax.random.fold_in(_rk, 7), 160), (512,), 87, 99838, jnp.int32), jax.random.randint(jax.random.fold_in(jax.random.fold_in(_rk, 7), 161), (512,), 9, 99969, jnp.int32), jax.random.randint(jax.random.fold_in(jax.random.fold_in(_rk, 7), 162), (512,), 83, 99849, jnp.int32), jax.random.randint(jax.random.fold_in(jax.random.fold_in(_rk, 7), 163), (512,), 41, 99926, jnp.int32), jax.random.randint(jax.random.fold_in(jax.random.fold_in(_rk, 7), 164), (512,), 24, 99995, jnp.int32), jax.random.randint(jax.random.fold_in(jax.random.fold_in(_rk, 7), 165), (512,), 124, 99933, jnp.int32), jax.random.randint(jax.random.fold_in(jax.random.fold_in(_rk, 7), 166), (512,), 149, 99789, jnp.int32), jax.random.randint(jax.random.fold_in(jax.random.fold_in(_rk, 7), 167), (512,), 86, 99820, jnp.int32), jax.random.randint(jax.random.fold_in(jax.random.fold_in(_rk, 7), 168), (512,), 6, 99977, jnp.int32), jax.random.randint(jax.random.fold_in(jax.random.fold_in(_rk, 7), 169), (512,), 104, 12496, jnp.int32), jax.random.randint(jax.random.fold_in(jax.random.fold_in(_rk, 7), 170), (512,), 34, 99955, jnp.int32), jax.random.randint(jax.random.fold_in(jax.random.fold_in(_rk, 7), 171), (512,), 22, 99990, jnp.int32), jax.random.randint(jax.random.fold_in(jax.random.fold_in(_rk, 7), 172), (512,), 78, 99495, jnp.int32), jax.random.randint(jax.random.fold_in(jax.random.fold_in(_rk, 7), 173), (512,), 64, 12498, jnp.int32), jax.random.randint(jax.random.fold_in(jax.random.fold_in(_rk, 7), 174), (512,), 123, 99951, jnp.int32), jax.random.randint(jax.random.fold_in(jax.random.fold_in(_rk, 7), 175), (512,), 17, 99932, jnp.int32), jax.random.randint(jax.random.fold_in(jax.random.fold_in(_rk, 7), 176), (512,), 162, 99950, jnp.int32), jax.random.randint(jax.random.fold_in(jax.random.fold_in(_rk, 7), 177), (512,), 48, 12460, jnp.int32), jax.random.randint(jax.random.fold_in(jax.random.fold_in(_rk, 7), 178), (512,), 175, 99364, jnp.int32), jax.random.randint(jax.random.fold_in(jax.random.fold_in(_rk, 7), 179), (512,), 83, 99815, jnp.int32), jax.random.randint(jax.random.fold_in(jax.random.fold_in(_rk, 7), 180), (512,), 51, 99958, jnp.int32), jax.random.randint(jax.random.fold_in(jax.random.fold_in(_rk, 7), 181), (512,), 56, 99575, jnp.int32), jax.random.randint(jax.random.fold_in(jax.random.fold_in(_rk, 7), 182), (512,), 62, 99943, jnp.int32), jax.random.randint(jax.random.fold_in(jax.random.fold_in(_rk, 7), 183), (512,), 170, 99915, jnp.int32), jax.random.randint(jax.random.fold_in(jax.random.fold_in(_rk, 7), 184), (512,), 139, 99946, jnp.int32), jax.random.randint(jax.random.fold_in(jax.random.fold_in(_rk, 7), 185), (512,), 55, 99697, jnp.int32), jax.random.randint(jax.random.fold_in(jax.random.fold_in(_rk, 7), 186), (512,), 378, 99758, jnp.int32), jax.random.randint(jax.random.fold_in(jax.random.fold_in(_rk, 7), 187), (512,), 22, 99954, jnp.int32), jax.random.randint(jax.random.fold_in(jax.random.fold_in(_rk, 7), 188), (512,), 40, 99818, jnp.int32), jax.random.randint(jax.random.fold_in(jax.random.fold_in(_rk, 7), 189), (512,), 25, 99889, jnp.int32), jax.random.randint(jax.random.fold_in(jax.random.fold_in(_rk, 7), 190), (512,), 87, 99855, jnp.int32), jax.random.randint(jax.random.fold_in(jax.random.fold_in(_rk, 7), 191), (512,), 80, 99820, jnp.int32), jax.random.randint(jax.random.fold_in(jax.random.fold_in(_rk, 7), 192), (512,), 33, 99996, jnp.int32), jax.random.randint(jax.random.fold_in(jax.random.fold_in(_rk, 7), 193), (512,), 60, 99956, jnp.int32), jax.random.randint(jax.random.fold_in(jax.random.fold_in(_rk, 7), 194), (512,), 272, 99943, jnp.int32), jax.random.randint(jax.random.fold_in(jax.random.fold_in(_rk, 7), 195), (512,), 72, 99722, jnp.int32), jax.random.randint(jax.random.fold_in(jax.random.fold_in(_rk, 7), 196), (512,), 124, 99981, jnp.int32), jax.random.randint(jax.random.fold_in(jax.random.fold_in(_rk, 7), 197), (512,), 55, 99910, jnp.int32), jax.random.randint(jax.random.fold_in(jax.random.fold_in(_rk, 7), 198), (512,), 136, 99890, jnp.int32), jax.random.randint(jax.random.fold_in(jax.random.fold_in(_rk, 7), 199), (512,), 23, 99955, jnp.int32)], axis=1)
        r_exp_item_cat = jnp.stack([jax.random.randint(jax.random.fold_in(jax.random.fold_in(_rk, 8), 0), (512,), 2, 1000, jnp.int32), jax.random.randint(jax.random.fold_in(jax.random.fold_in(_rk, 8), 1), (512,), 2, 1000, jnp.int32), jax.random.randint(jax.random.fold_in(jax.random.fold_in(_rk, 8), 2), (512,), 0, 999, jnp.int32), jax.random.randint(jax.random.fold_in(jax.random.fold_in(_rk, 8), 3), (512,), 3, 1000, jnp.int32), jax.random.randint(jax.random.fold_in(jax.random.fold_in(_rk, 8), 4), (512,), 3, 1000, jnp.int32), jax.random.randint(jax.random.fold_in(jax.random.fold_in(_rk, 8), 5), (512,), 0, 1000, jnp.int32), jax.random.randint(jax.random.fold_in(jax.random.fold_in(_rk, 8), 6), (512,), 0, 1000, jnp.int32), jax.random.randint(jax.random.fold_in(jax.random.fold_in(_rk, 8), 7), (512,), 0, 1000, jnp.int32), jax.random.randint(jax.random.fold_in(jax.random.fold_in(_rk, 8), 8), (512,), 0, 1000, jnp.int32), jax.random.randint(jax.random.fold_in(jax.random.fold_in(_rk, 8), 9), (512,), 1, 1000, jnp.int32), jax.random.randint(jax.random.fold_in(jax.random.fold_in(_rk, 8), 10), (512,), 0, 1000, jnp.int32), jax.random.randint(jax.random.fold_in(jax.random.fold_in(_rk, 8), 11), (512,), 0, 998, jnp.int32), jax.random.randint(jax.random.fold_in(jax.random.fold_in(_rk, 8), 12), (512,), 1, 1000, jnp.int32), jax.random.randint(jax.random.fold_in(jax.random.fold_in(_rk, 8), 13), (512,), 0, 999, jnp.int32), jax.random.randint(jax.random.fold_in(jax.random.fold_in(_rk, 8), 14), (512,), 0, 1000, jnp.int32), jax.random.randint(jax.random.fold_in(jax.random.fold_in(_rk, 8), 15), (512,), 0, 1000, jnp.int32), jax.random.randint(jax.random.fold_in(jax.random.fold_in(_rk, 8), 16), (512,), 0, 1000, jnp.int32), jax.random.randint(jax.random.fold_in(jax.random.fold_in(_rk, 8), 17), (512,), 0, 1000, jnp.int32), jax.random.randint(jax.random.fold_in(jax.random.fold_in(_rk, 8), 18), (512,), 0, 999, jnp.int32), jax.random.randint(jax.random.fold_in(jax.random.fold_in(_rk, 8), 19), (512,), 0, 1000, jnp.int32), jax.random.randint(jax.random.fold_in(jax.random.fold_in(_rk, 8), 20), (512,), 1, 999, jnp.int32), jax.random.randint(jax.random.fold_in(jax.random.fold_in(_rk, 8), 21), (512,), 0, 999, jnp.int32), jax.random.randint(jax.random.fold_in(jax.random.fold_in(_rk, 8), 22), (512,), 0, 1000, jnp.int32), jax.random.randint(jax.random.fold_in(jax.random.fold_in(_rk, 8), 23), (512,), 1, 1000, jnp.int32), jax.random.randint(jax.random.fold_in(jax.random.fold_in(_rk, 8), 24), (512,), 1, 1000, jnp.int32), jax.random.randint(jax.random.fold_in(jax.random.fold_in(_rk, 8), 25), (512,), 0, 1000, jnp.int32), jax.random.randint(jax.random.fold_in(jax.random.fold_in(_rk, 8), 26), (512,), 2, 999, jnp.int32), jax.random.randint(jax.random.fold_in(jax.random.fold_in(_rk, 8), 27), (512,), 0, 1000, jnp.int32), jax.random.randint(jax.random.fold_in(jax.random.fold_in(_rk, 8), 28), (512,), 0, 1000, jnp.int32), jax.random.randint(jax.random.fold_in(jax.random.fold_in(_rk, 8), 29), (512,), 0, 999, jnp.int32), jax.random.randint(jax.random.fold_in(jax.random.fold_in(_rk, 8), 30), (512,), 0, 999, jnp.int32), jax.random.randint(jax.random.fold_in(jax.random.fold_in(_rk, 8), 31), (512,), 1, 1000, jnp.int32), jax.random.randint(jax.random.fold_in(jax.random.fold_in(_rk, 8), 32), (512,), 0, 1000, jnp.int32), jax.random.randint(jax.random.fold_in(jax.random.fold_in(_rk, 8), 33), (512,), 4, 1000, jnp.int32), jax.random.randint(jax.random.fold_in(jax.random.fold_in(_rk, 8), 34), (512,), 0, 1000, jnp.int32), jax.random.randint(jax.random.fold_in(jax.random.fold_in(_rk, 8), 35), (512,), 0, 1000, jnp.int32), jax.random.randint(jax.random.fold_in(jax.random.fold_in(_rk, 8), 36), (512,), 1, 999, jnp.int32), jax.random.randint(jax.random.fold_in(jax.random.fold_in(_rk, 8), 37), (512,), 0, 999, jnp.int32), jax.random.randint(jax.random.fold_in(jax.random.fold_in(_rk, 8), 38), (512,), 0, 1000, jnp.int32), jax.random.randint(jax.random.fold_in(jax.random.fold_in(_rk, 8), 39), (512,), 2, 1000, jnp.int32), jax.random.randint(jax.random.fold_in(jax.random.fold_in(_rk, 8), 40), (512,), 0, 999, jnp.int32), jax.random.randint(jax.random.fold_in(jax.random.fold_in(_rk, 8), 41), (512,), 0, 1000, jnp.int32), jax.random.randint(jax.random.fold_in(jax.random.fold_in(_rk, 8), 42), (512,), 0, 1000, jnp.int32), jax.random.randint(jax.random.fold_in(jax.random.fold_in(_rk, 8), 43), (512,), 0, 1000, jnp.int32), jax.random.randint(jax.random.fold_in(jax.random.fold_in(_rk, 8), 44), (512,), 0, 1000, jnp.int32), jax.random.randint(jax.random.fold_in(jax.random.fold_in(_rk, 8), 45), (512,), 0, 999, jnp.int32), jax.random.randint(jax.random.fold_in(jax.random.fold_in(_rk, 8), 46), (512,), 3, 998, jnp.int32), jax.random.randint(jax.random.fold_in(jax.random.fold_in(_rk, 8), 47), (512,), 1, 1000, jnp.int32), jax.random.randint(jax.random.fold_in(jax.random.fold_in(_rk, 8), 48), (512,), 0, 1000, jnp.int32), jax.random.randint(jax.random.fold_in(jax.random.fold_in(_rk, 8), 49), (512,), 0, 999, jnp.int32), jax.random.randint(jax.random.fold_in(jax.random.fold_in(_rk, 8), 50), (512,), 0, 1000, jnp.int32), jax.random.randint(jax.random.fold_in(jax.random.fold_in(_rk, 8), 51), (512,), 0, 1000, jnp.int32), jax.random.randint(jax.random.fold_in(jax.random.fold_in(_rk, 8), 52), (512,), 1, 999, jnp.int32), jax.random.randint(jax.random.fold_in(jax.random.fold_in(_rk, 8), 53), (512,), 0, 995, jnp.int32), jax.random.randint(jax.random.fold_in(jax.random.fold_in(_rk, 8), 54), (512,), 0, 998, jnp.int32), jax.random.randint(jax.random.fold_in(jax.random.fold_in(_rk, 8), 55), (512,), 1, 999, jnp.int32), jax.random.randint(jax.random.fold_in(jax.random.fold_in(_rk, 8), 56), (512,), 0, 1000, jnp.int32), jax.random.randint(jax.random.fold_in(jax.random.fold_in(_rk, 8), 57), (512,), 0, 1000, jnp.int32), jax.random.randint(jax.random.fold_in(jax.random.fold_in(_rk, 8), 58), (512,), 2, 1000, jnp.int32), jax.random.randint(jax.random.fold_in(jax.random.fold_in(_rk, 8), 59), (512,), 0, 998, jnp.int32), jax.random.randint(jax.random.fold_in(jax.random.fold_in(_rk, 8), 60), (512,), 1, 999, jnp.int32), jax.random.randint(jax.random.fold_in(jax.random.fold_in(_rk, 8), 61), (512,), 0, 999, jnp.int32), jax.random.randint(jax.random.fold_in(jax.random.fold_in(_rk, 8), 62), (512,), 1, 1000, jnp.int32), jax.random.randint(jax.random.fold_in(jax.random.fold_in(_rk, 8), 63), (512,), 0, 1000, jnp.int32), jax.random.randint(jax.random.fold_in(jax.random.fold_in(_rk, 8), 64), (512,), 2, 1000, jnp.int32), jax.random.randint(jax.random.fold_in(jax.random.fold_in(_rk, 8), 65), (512,), 1, 1000, jnp.int32), jax.random.randint(jax.random.fold_in(jax.random.fold_in(_rk, 8), 66), (512,), 0, 1000, jnp.int32), jax.random.randint(jax.random.fold_in(jax.random.fold_in(_rk, 8), 67), (512,), 0, 1000, jnp.int32), jax.random.randint(jax.random.fold_in(jax.random.fold_in(_rk, 8), 68), (512,), 0, 996, jnp.int32), jax.random.randint(jax.random.fold_in(jax.random.fold_in(_rk, 8), 69), (512,), 0, 1000, jnp.int32), jax.random.randint(jax.random.fold_in(jax.random.fold_in(_rk, 8), 70), (512,), 1, 1000, jnp.int32), jax.random.randint(jax.random.fold_in(jax.random.fold_in(_rk, 8), 71), (512,), 0, 999, jnp.int32), jax.random.randint(jax.random.fold_in(jax.random.fold_in(_rk, 8), 72), (512,), 2, 1000, jnp.int32), jax.random.randint(jax.random.fold_in(jax.random.fold_in(_rk, 8), 73), (512,), 2, 1000, jnp.int32), jax.random.randint(jax.random.fold_in(jax.random.fold_in(_rk, 8), 74), (512,), 3, 999, jnp.int32), jax.random.randint(jax.random.fold_in(jax.random.fold_in(_rk, 8), 75), (512,), 0, 1000, jnp.int32), jax.random.randint(jax.random.fold_in(jax.random.fold_in(_rk, 8), 76), (512,), 4, 999, jnp.int32), jax.random.randint(jax.random.fold_in(jax.random.fold_in(_rk, 8), 77), (512,), 1, 999, jnp.int32), jax.random.randint(jax.random.fold_in(jax.random.fold_in(_rk, 8), 78), (512,), 0, 1000, jnp.int32), jax.random.randint(jax.random.fold_in(jax.random.fold_in(_rk, 8), 79), (512,), 1, 1000, jnp.int32), jax.random.randint(jax.random.fold_in(jax.random.fold_in(_rk, 8), 80), (512,), 0, 1000, jnp.int32), jax.random.randint(jax.random.fold_in(jax.random.fold_in(_rk, 8), 81), (512,), 1, 1000, jnp.int32), jax.random.randint(jax.random.fold_in(jax.random.fold_in(_rk, 8), 82), (512,), 0, 1000, jnp.int32), jax.random.randint(jax.random.fold_in(jax.random.fold_in(_rk, 8), 83), (512,), 0, 1000, jnp.int32), jax.random.randint(jax.random.fold_in(jax.random.fold_in(_rk, 8), 84), (512,), 1, 1000, jnp.int32), jax.random.randint(jax.random.fold_in(jax.random.fold_in(_rk, 8), 85), (512,), 0, 1000, jnp.int32), jax.random.randint(jax.random.fold_in(jax.random.fold_in(_rk, 8), 86), (512,), 0, 1000, jnp.int32), jax.random.randint(jax.random.fold_in(jax.random.fold_in(_rk, 8), 87), (512,), 0, 994, jnp.int32), jax.random.randint(jax.random.fold_in(jax.random.fold_in(_rk, 8), 88), (512,), 0, 1000, jnp.int32), jax.random.randint(jax.random.fold_in(jax.random.fold_in(_rk, 8), 89), (512,), 0, 1000, jnp.int32), jax.random.randint(jax.random.fold_in(jax.random.fold_in(_rk, 8), 90), (512,), 0, 1000, jnp.int32), jax.random.randint(jax.random.fold_in(jax.random.fold_in(_rk, 8), 91), (512,), 0, 999, jnp.int32), jax.random.randint(jax.random.fold_in(jax.random.fold_in(_rk, 8), 92), (512,), 1, 1000, jnp.int32), jax.random.randint(jax.random.fold_in(jax.random.fold_in(_rk, 8), 93), (512,), 0, 1000, jnp.int32), jax.random.randint(jax.random.fold_in(jax.random.fold_in(_rk, 8), 94), (512,), 0, 1000, jnp.int32), jax.random.randint(jax.random.fold_in(jax.random.fold_in(_rk, 8), 95), (512,), 1, 1000, jnp.int32), jax.random.randint(jax.random.fold_in(jax.random.fold_in(_rk, 8), 96), (512,), 0, 1000, jnp.int32), jax.random.randint(jax.random.fold_in(jax.random.fold_in(_rk, 8), 97), (512,), 0, 998, jnp.int32), jax.random.randint(jax.random.fold_in(jax.random.fold_in(_rk, 8), 98), (512,), 0, 1000, jnp.int32), jax.random.randint(jax.random.fold_in(jax.random.fold_in(_rk, 8), 99), (512,), 2, 1000, jnp.int32), jax.random.randint(jax.random.fold_in(jax.random.fold_in(_rk, 8), 100), (512,), 0, 998, jnp.int32), jax.random.randint(jax.random.fold_in(jax.random.fold_in(_rk, 8), 101), (512,), 1, 999, jnp.int32), jax.random.randint(jax.random.fold_in(jax.random.fold_in(_rk, 8), 102), (512,), 0, 1000, jnp.int32), jax.random.randint(jax.random.fold_in(jax.random.fold_in(_rk, 8), 103), (512,), 0, 1000, jnp.int32), jax.random.randint(jax.random.fold_in(jax.random.fold_in(_rk, 8), 104), (512,), 0, 1000, jnp.int32), jax.random.randint(jax.random.fold_in(jax.random.fold_in(_rk, 8), 105), (512,), 0, 1000, jnp.int32), jax.random.randint(jax.random.fold_in(jax.random.fold_in(_rk, 8), 106), (512,), 1, 1000, jnp.int32), jax.random.randint(jax.random.fold_in(jax.random.fold_in(_rk, 8), 107), (512,), 1, 1000, jnp.int32), jax.random.randint(jax.random.fold_in(jax.random.fold_in(_rk, 8), 108), (512,), 0, 996, jnp.int32), jax.random.randint(jax.random.fold_in(jax.random.fold_in(_rk, 8), 109), (512,), 0, 1000, jnp.int32), jax.random.randint(jax.random.fold_in(jax.random.fold_in(_rk, 8), 110), (512,), 0, 1000, jnp.int32), jax.random.randint(jax.random.fold_in(jax.random.fold_in(_rk, 8), 111), (512,), 0, 1000, jnp.int32), jax.random.randint(jax.random.fold_in(jax.random.fold_in(_rk, 8), 112), (512,), 0, 996, jnp.int32), jax.random.randint(jax.random.fold_in(jax.random.fold_in(_rk, 8), 113), (512,), 0, 997, jnp.int32), jax.random.randint(jax.random.fold_in(jax.random.fold_in(_rk, 8), 114), (512,), 0, 999, jnp.int32), jax.random.randint(jax.random.fold_in(jax.random.fold_in(_rk, 8), 115), (512,), 1, 999, jnp.int32), jax.random.randint(jax.random.fold_in(jax.random.fold_in(_rk, 8), 116), (512,), 0, 1000, jnp.int32), jax.random.randint(jax.random.fold_in(jax.random.fold_in(_rk, 8), 117), (512,), 0, 997, jnp.int32), jax.random.randint(jax.random.fold_in(jax.random.fold_in(_rk, 8), 118), (512,), 0, 1000, jnp.int32), jax.random.randint(jax.random.fold_in(jax.random.fold_in(_rk, 8), 119), (512,), 1, 1000, jnp.int32), jax.random.randint(jax.random.fold_in(jax.random.fold_in(_rk, 8), 120), (512,), 1, 1000, jnp.int32), jax.random.randint(jax.random.fold_in(jax.random.fold_in(_rk, 8), 121), (512,), 0, 1000, jnp.int32), jax.random.randint(jax.random.fold_in(jax.random.fold_in(_rk, 8), 122), (512,), 0, 999, jnp.int32), jax.random.randint(jax.random.fold_in(jax.random.fold_in(_rk, 8), 123), (512,), 0, 1000, jnp.int32), jax.random.randint(jax.random.fold_in(jax.random.fold_in(_rk, 8), 124), (512,), 0, 1000, jnp.int32), jax.random.randint(jax.random.fold_in(jax.random.fold_in(_rk, 8), 125), (512,), 1, 999, jnp.int32), jax.random.randint(jax.random.fold_in(jax.random.fold_in(_rk, 8), 126), (512,), 0, 1000, jnp.int32), jax.random.randint(jax.random.fold_in(jax.random.fold_in(_rk, 8), 127), (512,), 0, 1000, jnp.int32), jax.random.randint(jax.random.fold_in(jax.random.fold_in(_rk, 8), 128), (512,), 0, 1000, jnp.int32), jax.random.randint(jax.random.fold_in(jax.random.fold_in(_rk, 8), 129), (512,), 5, 1000, jnp.int32), jax.random.randint(jax.random.fold_in(jax.random.fold_in(_rk, 8), 130), (512,), 1, 1000, jnp.int32), jax.random.randint(jax.random.fold_in(jax.random.fold_in(_rk, 8), 131), (512,), 1, 998, jnp.int32), jax.random.randint(jax.random.fold_in(jax.random.fold_in(_rk, 8), 132), (512,), 0, 1000, jnp.int32), jax.random.randint(jax.random.fold_in(jax.random.fold_in(_rk, 8), 133), (512,), 2, 1000, jnp.int32), jax.random.randint(jax.random.fold_in(jax.random.fold_in(_rk, 8), 134), (512,), 1, 1000, jnp.int32), jax.random.randint(jax.random.fold_in(jax.random.fold_in(_rk, 8), 135), (512,), 0, 1000, jnp.int32), jax.random.randint(jax.random.fold_in(jax.random.fold_in(_rk, 8), 136), (512,), 0, 1000, jnp.int32), jax.random.randint(jax.random.fold_in(jax.random.fold_in(_rk, 8), 137), (512,), 1, 997, jnp.int32), jax.random.randint(jax.random.fold_in(jax.random.fold_in(_rk, 8), 138), (512,), 0, 1000, jnp.int32), jax.random.randint(jax.random.fold_in(jax.random.fold_in(_rk, 8), 139), (512,), 0, 1000, jnp.int32), jax.random.randint(jax.random.fold_in(jax.random.fold_in(_rk, 8), 140), (512,), 0, 1000, jnp.int32), jax.random.randint(jax.random.fold_in(jax.random.fold_in(_rk, 8), 141), (512,), 0, 1000, jnp.int32), jax.random.randint(jax.random.fold_in(jax.random.fold_in(_rk, 8), 142), (512,), 0, 1000, jnp.int32), jax.random.randint(jax.random.fold_in(jax.random.fold_in(_rk, 8), 143), (512,), 0, 999, jnp.int32), jax.random.randint(jax.random.fold_in(jax.random.fold_in(_rk, 8), 144), (512,), 1, 999, jnp.int32), jax.random.randint(jax.random.fold_in(jax.random.fold_in(_rk, 8), 145), (512,), 0, 1000, jnp.int32), jax.random.randint(jax.random.fold_in(jax.random.fold_in(_rk, 8), 146), (512,), 0, 1000, jnp.int32), jax.random.randint(jax.random.fold_in(jax.random.fold_in(_rk, 8), 147), (512,), 0, 1000, jnp.int32), jax.random.randint(jax.random.fold_in(jax.random.fold_in(_rk, 8), 148), (512,), 1, 1000, jnp.int32), jax.random.randint(jax.random.fold_in(jax.random.fold_in(_rk, 8), 149), (512,), 0, 1000, jnp.int32), jax.random.randint(jax.random.fold_in(jax.random.fold_in(_rk, 8), 150), (512,), 1, 1000, jnp.int32), jax.random.randint(jax.random.fold_in(jax.random.fold_in(_rk, 8), 151), (512,), 1, 1000, jnp.int32), jax.random.randint(jax.random.fold_in(jax.random.fold_in(_rk, 8), 152), (512,), 0, 1000, jnp.int32), jax.random.randint(jax.random.fold_in(jax.random.fold_in(_rk, 8), 153), (512,), 3, 1000, jnp.int32), jax.random.randint(jax.random.fold_in(jax.random.fold_in(_rk, 8), 154), (512,), 2, 998, jnp.int32), jax.random.randint(jax.random.fold_in(jax.random.fold_in(_rk, 8), 155), (512,), 0, 1000, jnp.int32), jax.random.randint(jax.random.fold_in(jax.random.fold_in(_rk, 8), 156), (512,), 0, 1000, jnp.int32), jax.random.randint(jax.random.fold_in(jax.random.fold_in(_rk, 8), 157), (512,), 0, 1000, jnp.int32), jax.random.randint(jax.random.fold_in(jax.random.fold_in(_rk, 8), 158), (512,), 0, 999, jnp.int32), jax.random.randint(jax.random.fold_in(jax.random.fold_in(_rk, 8), 159), (512,), 0, 997, jnp.int32), jax.random.randint(jax.random.fold_in(jax.random.fold_in(_rk, 8), 160), (512,), 1, 999, jnp.int32), jax.random.randint(jax.random.fold_in(jax.random.fold_in(_rk, 8), 161), (512,), 0, 1000, jnp.int32), jax.random.randint(jax.random.fold_in(jax.random.fold_in(_rk, 8), 162), (512,), 2, 999, jnp.int32), jax.random.randint(jax.random.fold_in(jax.random.fold_in(_rk, 8), 163), (512,), 1, 1000, jnp.int32), jax.random.randint(jax.random.fold_in(jax.random.fold_in(_rk, 8), 164), (512,), 0, 1000, jnp.int32), jax.random.randint(jax.random.fold_in(jax.random.fold_in(_rk, 8), 165), (512,), 0, 997, jnp.int32), jax.random.randint(jax.random.fold_in(jax.random.fold_in(_rk, 8), 166), (512,), 0, 1000, jnp.int32), jax.random.randint(jax.random.fold_in(jax.random.fold_in(_rk, 8), 167), (512,), 1, 1000, jnp.int32), jax.random.randint(jax.random.fold_in(jax.random.fold_in(_rk, 8), 168), (512,), 0, 1000, jnp.int32), jax.random.randint(jax.random.fold_in(jax.random.fold_in(_rk, 8), 169), (512,), 1, 1000, jnp.int32), jax.random.randint(jax.random.fold_in(jax.random.fold_in(_rk, 8), 170), (512,), 0, 999, jnp.int32), jax.random.randint(jax.random.fold_in(jax.random.fold_in(_rk, 8), 171), (512,), 0, 1000, jnp.int32), jax.random.randint(jax.random.fold_in(jax.random.fold_in(_rk, 8), 172), (512,), 0, 1000, jnp.int32), jax.random.randint(jax.random.fold_in(jax.random.fold_in(_rk, 8), 173), (512,), 1, 1000, jnp.int32), jax.random.randint(jax.random.fold_in(jax.random.fold_in(_rk, 8), 174), (512,), 0, 999, jnp.int32), jax.random.randint(jax.random.fold_in(jax.random.fold_in(_rk, 8), 175), (512,), 2, 1000, jnp.int32), jax.random.randint(jax.random.fold_in(jax.random.fold_in(_rk, 8), 176), (512,), 0, 998, jnp.int32), jax.random.randint(jax.random.fold_in(jax.random.fold_in(_rk, 8), 177), (512,), 0, 1000, jnp.int32), jax.random.randint(jax.random.fold_in(jax.random.fold_in(_rk, 8), 178), (512,), 1, 1000, jnp.int32), jax.random.randint(jax.random.fold_in(jax.random.fold_in(_rk, 8), 179), (512,), 0, 999, jnp.int32), jax.random.randint(jax.random.fold_in(jax.random.fold_in(_rk, 8), 180), (512,), 0, 1000, jnp.int32), jax.random.randint(jax.random.fold_in(jax.random.fold_in(_rk, 8), 181), (512,), 0, 1000, jnp.int32), jax.random.randint(jax.random.fold_in(jax.random.fold_in(_rk, 8), 182), (512,), 0, 998, jnp.int32), jax.random.randint(jax.random.fold_in(jax.random.fold_in(_rk, 8), 183), (512,), 1, 1000, jnp.int32), jax.random.randint(jax.random.fold_in(jax.random.fold_in(_rk, 8), 184), (512,), 0, 1000, jnp.int32), jax.random.randint(jax.random.fold_in(jax.random.fold_in(_rk, 8), 185), (512,), 0, 999, jnp.int32), jax.random.randint(jax.random.fold_in(jax.random.fold_in(_rk, 8), 186), (512,), 0, 999, jnp.int32), jax.random.randint(jax.random.fold_in(jax.random.fold_in(_rk, 8), 187), (512,), 1, 999, jnp.int32), jax.random.randint(jax.random.fold_in(jax.random.fold_in(_rk, 8), 188), (512,), 0, 999, jnp.int32), jax.random.randint(jax.random.fold_in(jax.random.fold_in(_rk, 8), 189), (512,), 0, 1000, jnp.int32), jax.random.randint(jax.random.fold_in(jax.random.fold_in(_rk, 8), 190), (512,), 0, 1000, jnp.int32), jax.random.randint(jax.random.fold_in(jax.random.fold_in(_rk, 8), 191), (512,), 2, 999, jnp.int32), jax.random.randint(jax.random.fold_in(jax.random.fold_in(_rk, 8), 192), (512,), 0, 1000, jnp.int32), jax.random.randint(jax.random.fold_in(jax.random.fold_in(_rk, 8), 193), (512,), 0, 1000, jnp.int32), jax.random.randint(jax.random.fold_in(jax.random.fold_in(_rk, 8), 194), (512,), 1, 1000, jnp.int32), jax.random.randint(jax.random.fold_in(jax.random.fold_in(_rk, 8), 195), (512,), 2, 1000, jnp.int32), jax.random.randint(jax.random.fold_in(jax.random.fold_in(_rk, 8), 196), (512,), 0, 998, jnp.int32), jax.random.randint(jax.random.fold_in(jax.random.fold_in(_rk, 8), 197), (512,), 0, 1000, jnp.int32), jax.random.randint(jax.random.fold_in(jax.random.fold_in(_rk, 8), 198), (512,), 0, 1000, jnp.int32), jax.random.randint(jax.random.fold_in(jax.random.fold_in(_rk, 8), 199), (512,), 1, 998, jnp.int32)], axis=1)
        r_ipv_item_id = jnp.stack([jax.random.randint(jax.random.fold_in(jax.random.fold_in(_rk, 9), 0), (512,), 64, 99938, jnp.int32), jax.random.randint(jax.random.fold_in(jax.random.fold_in(_rk, 9), 1), (512,), 3, 99950, jnp.int32), jax.random.randint(jax.random.fold_in(jax.random.fold_in(_rk, 9), 2), (512,), 18, 99921, jnp.int32), jax.random.randint(jax.random.fold_in(jax.random.fold_in(_rk, 9), 3), (512,), 13, 99873, jnp.int32), jax.random.randint(jax.random.fold_in(jax.random.fold_in(_rk, 9), 4), (512,), 31, 12495, jnp.int32), jax.random.randint(jax.random.fold_in(jax.random.fold_in(_rk, 9), 5), (512,), 10, 99884, jnp.int32), jax.random.randint(jax.random.fold_in(jax.random.fold_in(_rk, 9), 6), (512,), 92, 99990, jnp.int32), jax.random.randint(jax.random.fold_in(jax.random.fold_in(_rk, 9), 7), (512,), 7, 12499, jnp.int32), jax.random.randint(jax.random.fold_in(jax.random.fold_in(_rk, 9), 8), (512,), 44, 12491, jnp.int32), jax.random.randint(jax.random.fold_in(jax.random.fold_in(_rk, 9), 9), (512,), 65, 99923, jnp.int32), jax.random.randint(jax.random.fold_in(jax.random.fold_in(_rk, 9), 10), (512,), 31, 99909, jnp.int32), jax.random.randint(jax.random.fold_in(jax.random.fold_in(_rk, 9), 11), (512,), 331, 99993, jnp.int32), jax.random.randint(jax.random.fold_in(jax.random.fold_in(_rk, 9), 12), (512,), 171, 99975, jnp.int32), jax.random.randint(jax.random.fold_in(jax.random.fold_in(_rk, 9), 13), (512,), 84, 99933, jnp.int32), jax.random.randint(jax.random.fold_in(jax.random.fold_in(_rk, 9), 14), (512,), 5, 99894, jnp.int32), jax.random.randint(jax.random.fold_in(jax.random.fold_in(_rk, 9), 15), (512,), 12, 99821, jnp.int32), jax.random.randint(jax.random.fold_in(jax.random.fold_in(_rk, 9), 16), (512,), 5, 99997, jnp.int32), jax.random.randint(jax.random.fold_in(jax.random.fold_in(_rk, 9), 17), (512,), 162, 12495, jnp.int32), jax.random.randint(jax.random.fold_in(jax.random.fold_in(_rk, 9), 18), (512,), 51, 99900, jnp.int32), jax.random.randint(jax.random.fold_in(jax.random.fold_in(_rk, 9), 19), (512,), 101, 99979, jnp.int32), jax.random.randint(jax.random.fold_in(jax.random.fold_in(_rk, 9), 20), (512,), 381, 99787, jnp.int32), jax.random.randint(jax.random.fold_in(jax.random.fold_in(_rk, 9), 21), (512,), 57, 12478, jnp.int32), jax.random.randint(jax.random.fold_in(jax.random.fold_in(_rk, 9), 22), (512,), 139, 99948, jnp.int32), jax.random.randint(jax.random.fold_in(jax.random.fold_in(_rk, 9), 23), (512,), 47, 99695, jnp.int32), jax.random.randint(jax.random.fold_in(jax.random.fold_in(_rk, 9), 24), (512,), 193, 12495, jnp.int32), jax.random.randint(jax.random.fold_in(jax.random.fold_in(_rk, 9), 25), (512,), 64, 99878, jnp.int32), jax.random.randint(jax.random.fold_in(jax.random.fold_in(_rk, 9), 26), (512,), 5, 99972, jnp.int32), jax.random.randint(jax.random.fold_in(jax.random.fold_in(_rk, 9), 27), (512,), 68, 99965, jnp.int32), jax.random.randint(jax.random.fold_in(jax.random.fold_in(_rk, 9), 28), (512,), 9, 99820, jnp.int32), jax.random.randint(jax.random.fold_in(jax.random.fold_in(_rk, 9), 29), (512,), 30, 99991, jnp.int32), jax.random.randint(jax.random.fold_in(jax.random.fold_in(_rk, 9), 30), (512,), 121, 99843, jnp.int32), jax.random.randint(jax.random.fold_in(jax.random.fold_in(_rk, 9), 31), (512,), 94, 99911, jnp.int32), jax.random.randint(jax.random.fold_in(jax.random.fold_in(_rk, 9), 32), (512,), 38, 99909, jnp.int32), jax.random.randint(jax.random.fold_in(jax.random.fold_in(_rk, 9), 33), (512,), 27, 99996, jnp.int32), jax.random.randint(jax.random.fold_in(jax.random.fold_in(_rk, 9), 34), (512,), 191, 99990, jnp.int32), jax.random.randint(jax.random.fold_in(jax.random.fold_in(_rk, 9), 35), (512,), 51, 12473, jnp.int32), jax.random.randint(jax.random.fold_in(jax.random.fold_in(_rk, 9), 36), (512,), 200, 99935, jnp.int32), jax.random.randint(jax.random.fold_in(jax.random.fold_in(_rk, 9), 37), (512,), 30, 99963, jnp.int32), jax.random.randint(jax.random.fold_in(jax.random.fold_in(_rk, 9), 38), (512,), 181, 99945, jnp.int32), jax.random.randint(jax.random.fold_in(jax.random.fold_in(_rk, 9), 39), (512,), 8, 99999, jnp.int32), jax.random.randint(jax.random.fold_in(jax.random.fold_in(_rk, 9), 40), (512,), 233, 99989, jnp.int32), jax.random.randint(jax.random.fold_in(jax.random.fold_in(_rk, 9), 41), (512,), 70, 99995, jnp.int32), jax.random.randint(jax.random.fold_in(jax.random.fold_in(_rk, 9), 42), (512,), 21, 99924, jnp.int32), jax.random.randint(jax.random.fold_in(jax.random.fold_in(_rk, 9), 43), (512,), 136, 99998, jnp.int32), jax.random.randint(jax.random.fold_in(jax.random.fold_in(_rk, 9), 44), (512,), 12, 99954, jnp.int32), jax.random.randint(jax.random.fold_in(jax.random.fold_in(_rk, 9), 45), (512,), 41, 99956, jnp.int32), jax.random.randint(jax.random.fold_in(jax.random.fold_in(_rk, 9), 46), (512,), 21, 99603, jnp.int32), jax.random.randint(jax.random.fold_in(jax.random.fold_in(_rk, 9), 47), (512,), 67, 99884, jnp.int32), jax.random.randint(jax.random.fold_in(jax.random.fold_in(_rk, 9), 48), (512,), 83, 99991, jnp.int32), jax.random.randint(jax.random.fold_in(jax.random.fold_in(_rk, 9), 49), (512,), 28, 99989, jnp.int32), jax.random.randint(jax.random.fold_in(jax.random.fold_in(_rk, 9), 50), (512,), 63, 99982, jnp.int32), jax.random.randint(jax.random.fold_in(jax.random.fold_in(_rk, 9), 51), (512,), 1, 99636, jnp.int32), jax.random.randint(jax.random.fold_in(jax.random.fold_in(_rk, 9), 52), (512,), 41, 99945, jnp.int32), jax.random.randint(jax.random.fold_in(jax.random.fold_in(_rk, 9), 53), (512,), 196, 99970, jnp.int32), jax.random.randint(jax.random.fold_in(jax.random.fold_in(_rk, 9), 54), (512,), 45, 99999, jnp.int32), jax.random.randint(jax.random.fold_in(jax.random.fold_in(_rk, 9), 55), (512,), 163, 99950, jnp.int32), jax.random.randint(jax.random.fold_in(jax.random.fold_in(_rk, 9), 56), (512,), 91, 99940, jnp.int32), jax.random.randint(jax.random.fold_in(jax.random.fold_in(_rk, 9), 57), (512,), 150, 99965, jnp.int32), jax.random.randint(jax.random.fold_in(jax.random.fold_in(_rk, 9), 58), (512,), 230, 99982, jnp.int32), jax.random.randint(jax.random.fold_in(jax.random.fold_in(_rk, 9), 59), (512,), 64, 99969, jnp.int32), jax.random.randint(jax.random.fold_in(jax.random.fold_in(_rk, 9), 60), (512,), 154, 99884, jnp.int32), jax.random.randint(jax.random.fold_in(jax.random.fold_in(_rk, 9), 61), (512,), 52, 99945, jnp.int32), jax.random.randint(jax.random.fold_in(jax.random.fold_in(_rk, 9), 62), (512,), 3, 99997, jnp.int32), jax.random.randint(jax.random.fold_in(jax.random.fold_in(_rk, 9), 63), (512,), 15, 99925, jnp.int32), jax.random.randint(jax.random.fold_in(jax.random.fold_in(_rk, 9), 64), (512,), 22, 99822, jnp.int32), jax.random.randint(jax.random.fold_in(jax.random.fold_in(_rk, 9), 65), (512,), 91, 99897, jnp.int32), jax.random.randint(jax.random.fold_in(jax.random.fold_in(_rk, 9), 66), (512,), 20, 12488, jnp.int32), jax.random.randint(jax.random.fold_in(jax.random.fold_in(_rk, 9), 67), (512,), 71, 99989, jnp.int32), jax.random.randint(jax.random.fold_in(jax.random.fold_in(_rk, 9), 68), (512,), 79, 99981, jnp.int32), jax.random.randint(jax.random.fold_in(jax.random.fold_in(_rk, 9), 69), (512,), 156, 99986, jnp.int32), jax.random.randint(jax.random.fold_in(jax.random.fold_in(_rk, 9), 70), (512,), 53, 99893, jnp.int32), jax.random.randint(jax.random.fold_in(jax.random.fold_in(_rk, 9), 71), (512,), 52, 99739, jnp.int32), jax.random.randint(jax.random.fold_in(jax.random.fold_in(_rk, 9), 72), (512,), 52, 99943, jnp.int32), jax.random.randint(jax.random.fold_in(jax.random.fold_in(_rk, 9), 73), (512,), 656, 99981, jnp.int32), jax.random.randint(jax.random.fold_in(jax.random.fold_in(_rk, 9), 74), (512,), 44, 99905, jnp.int32), jax.random.randint(jax.random.fold_in(jax.random.fold_in(_rk, 9), 75), (512,), 73, 99810, jnp.int32), jax.random.randint(jax.random.fold_in(jax.random.fold_in(_rk, 9), 76), (512,), 12, 99902, jnp.int32), jax.random.randint(jax.random.fold_in(jax.random.fold_in(_rk, 9), 77), (512,), 2, 99978, jnp.int32), jax.random.randint(jax.random.fold_in(jax.random.fold_in(_rk, 9), 78), (512,), 777, 99573, jnp.int32), jax.random.randint(jax.random.fold_in(jax.random.fold_in(_rk, 9), 79), (512,), 0, 99974, jnp.int32), jax.random.randint(jax.random.fold_in(jax.random.fold_in(_rk, 9), 80), (512,), 74, 99967, jnp.int32), jax.random.randint(jax.random.fold_in(jax.random.fold_in(_rk, 9), 81), (512,), 68, 99891, jnp.int32), jax.random.randint(jax.random.fold_in(jax.random.fold_in(_rk, 9), 82), (512,), 71, 99970, jnp.int32), jax.random.randint(jax.random.fold_in(jax.random.fold_in(_rk, 9), 83), (512,), 8, 99967, jnp.int32), jax.random.randint(jax.random.fold_in(jax.random.fold_in(_rk, 9), 84), (512,), 82, 12498, jnp.int32), jax.random.randint(jax.random.fold_in(jax.random.fold_in(_rk, 9), 85), (512,), 133, 99950, jnp.int32), jax.random.randint(jax.random.fold_in(jax.random.fold_in(_rk, 9), 86), (512,), 7, 99599, jnp.int32), jax.random.randint(jax.random.fold_in(jax.random.fold_in(_rk, 9), 87), (512,), 66, 12487, jnp.int32), jax.random.randint(jax.random.fold_in(jax.random.fold_in(_rk, 9), 88), (512,), 154, 99657, jnp.int32), jax.random.randint(jax.random.fold_in(jax.random.fold_in(_rk, 9), 89), (512,), 156, 99999, jnp.int32), jax.random.randint(jax.random.fold_in(jax.random.fold_in(_rk, 9), 90), (512,), 8, 99969, jnp.int32), jax.random.randint(jax.random.fold_in(jax.random.fold_in(_rk, 9), 91), (512,), 67, 99859, jnp.int32), jax.random.randint(jax.random.fold_in(jax.random.fold_in(_rk, 9), 92), (512,), 311, 99942, jnp.int32), jax.random.randint(jax.random.fold_in(jax.random.fold_in(_rk, 9), 93), (512,), 6, 99898, jnp.int32), jax.random.randint(jax.random.fold_in(jax.random.fold_in(_rk, 9), 94), (512,), 68, 99847, jnp.int32), jax.random.randint(jax.random.fold_in(jax.random.fold_in(_rk, 9), 95), (512,), 7, 99434, jnp.int32), jax.random.randint(jax.random.fold_in(jax.random.fold_in(_rk, 9), 96), (512,), 99, 99995, jnp.int32), jax.random.randint(jax.random.fold_in(jax.random.fold_in(_rk, 9), 97), (512,), 64, 99853, jnp.int32), jax.random.randint(jax.random.fold_in(jax.random.fold_in(_rk, 9), 98), (512,), 110, 99785, jnp.int32), jax.random.randint(jax.random.fold_in(jax.random.fold_in(_rk, 9), 99), (512,), 390, 99868, jnp.int32), jax.random.randint(jax.random.fold_in(jax.random.fold_in(_rk, 9), 100), (512,), 102, 99915, jnp.int32), jax.random.randint(jax.random.fold_in(jax.random.fold_in(_rk, 9), 101), (512,), 60, 99998, jnp.int32), jax.random.randint(jax.random.fold_in(jax.random.fold_in(_rk, 9), 102), (512,), 140, 99948, jnp.int32), jax.random.randint(jax.random.fold_in(jax.random.fold_in(_rk, 9), 103), (512,), 400, 99891, jnp.int32), jax.random.randint(jax.random.fold_in(jax.random.fold_in(_rk, 9), 104), (512,), 11, 99905, jnp.int32), jax.random.randint(jax.random.fold_in(jax.random.fold_in(_rk, 9), 105), (512,), 14, 99978, jnp.int32), jax.random.randint(jax.random.fold_in(jax.random.fold_in(_rk, 9), 106), (512,), 17, 99716, jnp.int32), jax.random.randint(jax.random.fold_in(jax.random.fold_in(_rk, 9), 107), (512,), 44, 99994, jnp.int32), jax.random.randint(jax.random.fold_in(jax.random.fold_in(_rk, 9), 108), (512,), 244, 99917, jnp.int32), jax.random.randint(jax.random.fold_in(jax.random.fold_in(_rk, 9), 109), (512,), 263, 99996, jnp.int32), jax.random.randint(jax.random.fold_in(jax.random.fold_in(_rk, 9), 110), (512,), 14, 99986, jnp.int32), jax.random.randint(jax.random.fold_in(jax.random.fold_in(_rk, 9), 111), (512,), 174, 99908, jnp.int32), jax.random.randint(jax.random.fold_in(jax.random.fold_in(_rk, 9), 112), (512,), 30, 99814, jnp.int32), jax.random.randint(jax.random.fold_in(jax.random.fold_in(_rk, 9), 113), (512,), 4, 99938, jnp.int32), jax.random.randint(jax.random.fold_in(jax.random.fold_in(_rk, 9), 114), (512,), 84, 99854, jnp.int32), jax.random.randint(jax.random.fold_in(jax.random.fold_in(_rk, 9), 115), (512,), 116, 99980, jnp.int32), jax.random.randint(jax.random.fold_in(jax.random.fold_in(_rk, 9), 116), (512,), 45, 99892, jnp.int32), jax.random.randint(jax.random.fold_in(jax.random.fold_in(_rk, 9), 117), (512,), 1, 12499, jnp.int32), jax.random.randint(jax.random.fold_in(jax.random.fold_in(_rk, 9), 118), (512,), 55, 99447, jnp.int32), jax.random.randint(jax.random.fold_in(jax.random.fold_in(_rk, 9), 119), (512,), 86, 99949, jnp.int32), jax.random.randint(jax.random.fold_in(jax.random.fold_in(_rk, 9), 120), (512,), 118, 99956, jnp.int32), jax.random.randint(jax.random.fold_in(jax.random.fold_in(_rk, 9), 121), (512,), 37, 99978, jnp.int32), jax.random.randint(jax.random.fold_in(jax.random.fold_in(_rk, 9), 122), (512,), 33, 99853, jnp.int32), jax.random.randint(jax.random.fold_in(jax.random.fold_in(_rk, 9), 123), (512,), 1, 99795, jnp.int32), jax.random.randint(jax.random.fold_in(jax.random.fold_in(_rk, 9), 124), (512,), 62, 99980, jnp.int32), jax.random.randint(jax.random.fold_in(jax.random.fold_in(_rk, 9), 125), (512,), 26, 99985, jnp.int32), jax.random.randint(jax.random.fold_in(jax.random.fold_in(_rk, 9), 126), (512,), 27, 99958, jnp.int32), jax.random.randint(jax.random.fold_in(jax.random.fold_in(_rk, 9), 127), (512,), 53, 99849, jnp.int32), jax.random.randint(jax.random.fold_in(jax.random.fold_in(_rk, 9), 128), (512,), 5, 99935, jnp.int32), jax.random.randint(jax.random.fold_in(jax.random.fold_in(_rk, 9), 129), (512,), 36, 99895, jnp.int32), jax.random.randint(jax.random.fold_in(jax.random.fold_in(_rk, 9), 130), (512,), 103, 99761, jnp.int32), jax.random.randint(jax.random.fold_in(jax.random.fold_in(_rk, 9), 131), (512,), 41, 99830, jnp.int32), jax.random.randint(jax.random.fold_in(jax.random.fold_in(_rk, 9), 132), (512,), 124, 99879, jnp.int32), jax.random.randint(jax.random.fold_in(jax.random.fold_in(_rk, 9), 133), (512,), 24, 99962, jnp.int32), jax.random.randint(jax.random.fold_in(jax.random.fold_in(_rk, 9), 134), (512,), 148, 99979, jnp.int32), jax.random.randint(jax.random.fold_in(jax.random.fold_in(_rk, 9), 135), (512,), 94, 99894, jnp.int32), jax.random.randint(jax.random.fold_in(jax.random.fold_in(_rk, 9), 136), (512,), 307, 99910, jnp.int32), jax.random.randint(jax.random.fold_in(jax.random.fold_in(_rk, 9), 137), (512,), 61, 99995, jnp.int32), jax.random.randint(jax.random.fold_in(jax.random.fold_in(_rk, 9), 138), (512,), 282, 99985, jnp.int32), jax.random.randint(jax.random.fold_in(jax.random.fold_in(_rk, 9), 139), (512,), 110, 99903, jnp.int32), jax.random.randint(jax.random.fold_in(jax.random.fold_in(_rk, 9), 140), (512,), 154, 99763, jnp.int32), jax.random.randint(jax.random.fold_in(jax.random.fold_in(_rk, 9), 141), (512,), 18, 12473, jnp.int32), jax.random.randint(jax.random.fold_in(jax.random.fold_in(_rk, 9), 142), (512,), 210, 99787, jnp.int32), jax.random.randint(jax.random.fold_in(jax.random.fold_in(_rk, 9), 143), (512,), 55, 99967, jnp.int32), jax.random.randint(jax.random.fold_in(jax.random.fold_in(_rk, 9), 144), (512,), 114, 12492, jnp.int32), jax.random.randint(jax.random.fold_in(jax.random.fold_in(_rk, 9), 145), (512,), 54, 99993, jnp.int32), jax.random.randint(jax.random.fold_in(jax.random.fold_in(_rk, 9), 146), (512,), 30, 99956, jnp.int32), jax.random.randint(jax.random.fold_in(jax.random.fold_in(_rk, 9), 147), (512,), 105, 99998, jnp.int32), jax.random.randint(jax.random.fold_in(jax.random.fold_in(_rk, 9), 148), (512,), 122, 99786, jnp.int32), jax.random.randint(jax.random.fold_in(jax.random.fold_in(_rk, 9), 149), (512,), 10, 12475, jnp.int32), jax.random.randint(jax.random.fold_in(jax.random.fold_in(_rk, 9), 150), (512,), 3, 99892, jnp.int32), jax.random.randint(jax.random.fold_in(jax.random.fold_in(_rk, 9), 151), (512,), 245, 99974, jnp.int32), jax.random.randint(jax.random.fold_in(jax.random.fold_in(_rk, 9), 152), (512,), 219, 99639, jnp.int32), jax.random.randint(jax.random.fold_in(jax.random.fold_in(_rk, 9), 153), (512,), 67, 99846, jnp.int32), jax.random.randint(jax.random.fold_in(jax.random.fold_in(_rk, 9), 154), (512,), 70, 99862, jnp.int32), jax.random.randint(jax.random.fold_in(jax.random.fold_in(_rk, 9), 155), (512,), 144, 12487, jnp.int32), jax.random.randint(jax.random.fold_in(jax.random.fold_in(_rk, 9), 156), (512,), 116, 12469, jnp.int32), jax.random.randint(jax.random.fold_in(jax.random.fold_in(_rk, 9), 157), (512,), 26, 99861, jnp.int32), jax.random.randint(jax.random.fold_in(jax.random.fold_in(_rk, 9), 158), (512,), 15, 99919, jnp.int32), jax.random.randint(jax.random.fold_in(jax.random.fold_in(_rk, 9), 159), (512,), 28, 12482, jnp.int32), jax.random.randint(jax.random.fold_in(jax.random.fold_in(_rk, 9), 160), (512,), 62, 99987, jnp.int32), jax.random.randint(jax.random.fold_in(jax.random.fold_in(_rk, 9), 161), (512,), 103, 99881, jnp.int32), jax.random.randint(jax.random.fold_in(jax.random.fold_in(_rk, 9), 162), (512,), 55, 99985, jnp.int32), jax.random.randint(jax.random.fold_in(jax.random.fold_in(_rk, 9), 163), (512,), 4, 99892, jnp.int32), jax.random.randint(jax.random.fold_in(jax.random.fold_in(_rk, 9), 164), (512,), 13, 99787, jnp.int32), jax.random.randint(jax.random.fold_in(jax.random.fold_in(_rk, 9), 165), (512,), 6, 12464, jnp.int32), jax.random.randint(jax.random.fold_in(jax.random.fold_in(_rk, 9), 166), (512,), 171, 12493, jnp.int32), jax.random.randint(jax.random.fold_in(jax.random.fold_in(_rk, 9), 167), (512,), 269, 99972, jnp.int32), jax.random.randint(jax.random.fold_in(jax.random.fold_in(_rk, 9), 168), (512,), 554, 99985, jnp.int32), jax.random.randint(jax.random.fold_in(jax.random.fold_in(_rk, 9), 169), (512,), 22, 99972, jnp.int32), jax.random.randint(jax.random.fold_in(jax.random.fold_in(_rk, 9), 170), (512,), 9, 99876, jnp.int32), jax.random.randint(jax.random.fold_in(jax.random.fold_in(_rk, 9), 171), (512,), 45, 99890, jnp.int32), jax.random.randint(jax.random.fold_in(jax.random.fold_in(_rk, 9), 172), (512,), 182, 99945, jnp.int32), jax.random.randint(jax.random.fold_in(jax.random.fold_in(_rk, 9), 173), (512,), 110, 99819, jnp.int32), jax.random.randint(jax.random.fold_in(jax.random.fold_in(_rk, 9), 174), (512,), 85, 99981, jnp.int32), jax.random.randint(jax.random.fold_in(jax.random.fold_in(_rk, 9), 175), (512,), 275, 12475, jnp.int32), jax.random.randint(jax.random.fold_in(jax.random.fold_in(_rk, 9), 176), (512,), 114, 99957, jnp.int32), jax.random.randint(jax.random.fold_in(jax.random.fold_in(_rk, 9), 177), (512,), 61, 99954, jnp.int32), jax.random.randint(jax.random.fold_in(jax.random.fold_in(_rk, 9), 178), (512,), 13, 99995, jnp.int32), jax.random.randint(jax.random.fold_in(jax.random.fold_in(_rk, 9), 179), (512,), 78, 99998, jnp.int32), jax.random.randint(jax.random.fold_in(jax.random.fold_in(_rk, 9), 180), (512,), 108, 12498, jnp.int32), jax.random.randint(jax.random.fold_in(jax.random.fold_in(_rk, 9), 181), (512,), 26, 12496, jnp.int32), jax.random.randint(jax.random.fold_in(jax.random.fold_in(_rk, 9), 182), (512,), 200, 99645, jnp.int32), jax.random.randint(jax.random.fold_in(jax.random.fold_in(_rk, 9), 183), (512,), 68, 99932, jnp.int32), jax.random.randint(jax.random.fold_in(jax.random.fold_in(_rk, 9), 184), (512,), 95, 99996, jnp.int32), jax.random.randint(jax.random.fold_in(jax.random.fold_in(_rk, 9), 185), (512,), 30, 99997, jnp.int32), jax.random.randint(jax.random.fold_in(jax.random.fold_in(_rk, 9), 186), (512,), 1, 12485, jnp.int32), jax.random.randint(jax.random.fold_in(jax.random.fold_in(_rk, 9), 187), (512,), 48, 99987, jnp.int32), jax.random.randint(jax.random.fold_in(jax.random.fold_in(_rk, 9), 188), (512,), 19, 12496, jnp.int32), jax.random.randint(jax.random.fold_in(jax.random.fold_in(_rk, 9), 189), (512,), 16, 99953, jnp.int32), jax.random.randint(jax.random.fold_in(jax.random.fold_in(_rk, 9), 190), (512,), 1, 99802, jnp.int32), jax.random.randint(jax.random.fold_in(jax.random.fold_in(_rk, 9), 191), (512,), 8, 99839, jnp.int32), jax.random.randint(jax.random.fold_in(jax.random.fold_in(_rk, 9), 192), (512,), 10, 99779, jnp.int32), jax.random.randint(jax.random.fold_in(jax.random.fold_in(_rk, 9), 193), (512,), 95, 99996, jnp.int32), jax.random.randint(jax.random.fold_in(jax.random.fold_in(_rk, 9), 194), (512,), 94, 12493, jnp.int32), jax.random.randint(jax.random.fold_in(jax.random.fold_in(_rk, 9), 195), (512,), 161, 99902, jnp.int32), jax.random.randint(jax.random.fold_in(jax.random.fold_in(_rk, 9), 196), (512,), 70, 99873, jnp.int32), jax.random.randint(jax.random.fold_in(jax.random.fold_in(_rk, 9), 197), (512,), 264, 99991, jnp.int32), jax.random.randint(jax.random.fold_in(jax.random.fold_in(_rk, 9), 198), (512,), 232, 99947, jnp.int32), jax.random.randint(jax.random.fold_in(jax.random.fold_in(_rk, 9), 199), (512,), 169, 99692, jnp.int32)], axis=1)
        r_ipv_item_cat = jnp.stack([jax.random.randint(jax.random.fold_in(jax.random.fold_in(_rk, 10), 0), (512,), 0, 1000, jnp.int32), jax.random.randint(jax.random.fold_in(jax.random.fold_in(_rk, 10), 1), (512,), 0, 1000, jnp.int32), jax.random.randint(jax.random.fold_in(jax.random.fold_in(_rk, 10), 2), (512,), 1, 1000, jnp.int32), jax.random.randint(jax.random.fold_in(jax.random.fold_in(_rk, 10), 3), (512,), 1, 997, jnp.int32), jax.random.randint(jax.random.fold_in(jax.random.fold_in(_rk, 10), 4), (512,), 2, 999, jnp.int32), jax.random.randint(jax.random.fold_in(jax.random.fold_in(_rk, 10), 5), (512,), 0, 1000, jnp.int32), jax.random.randint(jax.random.fold_in(jax.random.fold_in(_rk, 10), 6), (512,), 2, 1000, jnp.int32), jax.random.randint(jax.random.fold_in(jax.random.fold_in(_rk, 10), 7), (512,), 1, 1000, jnp.int32), jax.random.randint(jax.random.fold_in(jax.random.fold_in(_rk, 10), 8), (512,), 0, 1000, jnp.int32), jax.random.randint(jax.random.fold_in(jax.random.fold_in(_rk, 10), 9), (512,), 2, 999, jnp.int32), jax.random.randint(jax.random.fold_in(jax.random.fold_in(_rk, 10), 10), (512,), 1, 994, jnp.int32), jax.random.randint(jax.random.fold_in(jax.random.fold_in(_rk, 10), 11), (512,), 5, 1000, jnp.int32), jax.random.randint(jax.random.fold_in(jax.random.fold_in(_rk, 10), 12), (512,), 2, 1000, jnp.int32), jax.random.randint(jax.random.fold_in(jax.random.fold_in(_rk, 10), 13), (512,), 0, 1000, jnp.int32), jax.random.randint(jax.random.fold_in(jax.random.fold_in(_rk, 10), 14), (512,), 0, 1000, jnp.int32), jax.random.randint(jax.random.fold_in(jax.random.fold_in(_rk, 10), 15), (512,), 1, 998, jnp.int32), jax.random.randint(jax.random.fold_in(jax.random.fold_in(_rk, 10), 16), (512,), 1, 997, jnp.int32), jax.random.randint(jax.random.fold_in(jax.random.fold_in(_rk, 10), 17), (512,), 0, 999, jnp.int32), jax.random.randint(jax.random.fold_in(jax.random.fold_in(_rk, 10), 18), (512,), 2, 1000, jnp.int32), jax.random.randint(jax.random.fold_in(jax.random.fold_in(_rk, 10), 19), (512,), 1, 1000, jnp.int32), jax.random.randint(jax.random.fold_in(jax.random.fold_in(_rk, 10), 20), (512,), 0, 1000, jnp.int32), jax.random.randint(jax.random.fold_in(jax.random.fold_in(_rk, 10), 21), (512,), 1, 999, jnp.int32), jax.random.randint(jax.random.fold_in(jax.random.fold_in(_rk, 10), 22), (512,), 0, 1000, jnp.int32), jax.random.randint(jax.random.fold_in(jax.random.fold_in(_rk, 10), 23), (512,), 0, 999, jnp.int32), jax.random.randint(jax.random.fold_in(jax.random.fold_in(_rk, 10), 24), (512,), 0, 1000, jnp.int32), jax.random.randint(jax.random.fold_in(jax.random.fold_in(_rk, 10), 25), (512,), 0, 1000, jnp.int32), jax.random.randint(jax.random.fold_in(jax.random.fold_in(_rk, 10), 26), (512,), 1, 999, jnp.int32), jax.random.randint(jax.random.fold_in(jax.random.fold_in(_rk, 10), 27), (512,), 1, 999, jnp.int32), jax.random.randint(jax.random.fold_in(jax.random.fold_in(_rk, 10), 28), (512,), 0, 1000, jnp.int32), jax.random.randint(jax.random.fold_in(jax.random.fold_in(_rk, 10), 29), (512,), 5, 999, jnp.int32), jax.random.randint(jax.random.fold_in(jax.random.fold_in(_rk, 10), 30), (512,), 1, 999, jnp.int32), jax.random.randint(jax.random.fold_in(jax.random.fold_in(_rk, 10), 31), (512,), 0, 999, jnp.int32), jax.random.randint(jax.random.fold_in(jax.random.fold_in(_rk, 10), 32), (512,), 3, 1000, jnp.int32), jax.random.randint(jax.random.fold_in(jax.random.fold_in(_rk, 10), 33), (512,), 1, 1000, jnp.int32), jax.random.randint(jax.random.fold_in(jax.random.fold_in(_rk, 10), 34), (512,), 0, 1000, jnp.int32), jax.random.randint(jax.random.fold_in(jax.random.fold_in(_rk, 10), 35), (512,), 0, 1000, jnp.int32), jax.random.randint(jax.random.fold_in(jax.random.fold_in(_rk, 10), 36), (512,), 0, 1000, jnp.int32), jax.random.randint(jax.random.fold_in(jax.random.fold_in(_rk, 10), 37), (512,), 0, 999, jnp.int32), jax.random.randint(jax.random.fold_in(jax.random.fold_in(_rk, 10), 38), (512,), 1, 999, jnp.int32), jax.random.randint(jax.random.fold_in(jax.random.fold_in(_rk, 10), 39), (512,), 0, 1000, jnp.int32), jax.random.randint(jax.random.fold_in(jax.random.fold_in(_rk, 10), 40), (512,), 0, 1000, jnp.int32), jax.random.randint(jax.random.fold_in(jax.random.fold_in(_rk, 10), 41), (512,), 0, 1000, jnp.int32), jax.random.randint(jax.random.fold_in(jax.random.fold_in(_rk, 10), 42), (512,), 0, 1000, jnp.int32), jax.random.randint(jax.random.fold_in(jax.random.fold_in(_rk, 10), 43), (512,), 0, 1000, jnp.int32), jax.random.randint(jax.random.fold_in(jax.random.fold_in(_rk, 10), 44), (512,), 1, 999, jnp.int32), jax.random.randint(jax.random.fold_in(jax.random.fold_in(_rk, 10), 45), (512,), 0, 997, jnp.int32), jax.random.randint(jax.random.fold_in(jax.random.fold_in(_rk, 10), 46), (512,), 1, 1000, jnp.int32), jax.random.randint(jax.random.fold_in(jax.random.fold_in(_rk, 10), 47), (512,), 0, 999, jnp.int32), jax.random.randint(jax.random.fold_in(jax.random.fold_in(_rk, 10), 48), (512,), 0, 1000, jnp.int32), jax.random.randint(jax.random.fold_in(jax.random.fold_in(_rk, 10), 49), (512,), 1, 1000, jnp.int32), jax.random.randint(jax.random.fold_in(jax.random.fold_in(_rk, 10), 50), (512,), 2, 999, jnp.int32), jax.random.randint(jax.random.fold_in(jax.random.fold_in(_rk, 10), 51), (512,), 1, 1000, jnp.int32), jax.random.randint(jax.random.fold_in(jax.random.fold_in(_rk, 10), 52), (512,), 0, 999, jnp.int32), jax.random.randint(jax.random.fold_in(jax.random.fold_in(_rk, 10), 53), (512,), 0, 1000, jnp.int32), jax.random.randint(jax.random.fold_in(jax.random.fold_in(_rk, 10), 54), (512,), 0, 999, jnp.int32), jax.random.randint(jax.random.fold_in(jax.random.fold_in(_rk, 10), 55), (512,), 0, 1000, jnp.int32), jax.random.randint(jax.random.fold_in(jax.random.fold_in(_rk, 10), 56), (512,), 0, 1000, jnp.int32), jax.random.randint(jax.random.fold_in(jax.random.fold_in(_rk, 10), 57), (512,), 0, 999, jnp.int32), jax.random.randint(jax.random.fold_in(jax.random.fold_in(_rk, 10), 58), (512,), 2, 1000, jnp.int32), jax.random.randint(jax.random.fold_in(jax.random.fold_in(_rk, 10), 59), (512,), 1, 999, jnp.int32), jax.random.randint(jax.random.fold_in(jax.random.fold_in(_rk, 10), 60), (512,), 0, 999, jnp.int32), jax.random.randint(jax.random.fold_in(jax.random.fold_in(_rk, 10), 61), (512,), 0, 999, jnp.int32), jax.random.randint(jax.random.fold_in(jax.random.fold_in(_rk, 10), 62), (512,), 0, 998, jnp.int32), jax.random.randint(jax.random.fold_in(jax.random.fold_in(_rk, 10), 63), (512,), 0, 1000, jnp.int32), jax.random.randint(jax.random.fold_in(jax.random.fold_in(_rk, 10), 64), (512,), 0, 1000, jnp.int32), jax.random.randint(jax.random.fold_in(jax.random.fold_in(_rk, 10), 65), (512,), 0, 998, jnp.int32), jax.random.randint(jax.random.fold_in(jax.random.fold_in(_rk, 10), 66), (512,), 1, 1000, jnp.int32), jax.random.randint(jax.random.fold_in(jax.random.fold_in(_rk, 10), 67), (512,), 2, 1000, jnp.int32), jax.random.randint(jax.random.fold_in(jax.random.fold_in(_rk, 10), 68), (512,), 1, 1000, jnp.int32), jax.random.randint(jax.random.fold_in(jax.random.fold_in(_rk, 10), 69), (512,), 2, 997, jnp.int32), jax.random.randint(jax.random.fold_in(jax.random.fold_in(_rk, 10), 70), (512,), 0, 1000, jnp.int32), jax.random.randint(jax.random.fold_in(jax.random.fold_in(_rk, 10), 71), (512,), 1, 998, jnp.int32), jax.random.randint(jax.random.fold_in(jax.random.fold_in(_rk, 10), 72), (512,), 0, 1000, jnp.int32), jax.random.randint(jax.random.fold_in(jax.random.fold_in(_rk, 10), 73), (512,), 1, 1000, jnp.int32), jax.random.randint(jax.random.fold_in(jax.random.fold_in(_rk, 10), 74), (512,), 0, 998, jnp.int32), jax.random.randint(jax.random.fold_in(jax.random.fold_in(_rk, 10), 75), (512,), 3, 1000, jnp.int32), jax.random.randint(jax.random.fold_in(jax.random.fold_in(_rk, 10), 76), (512,), 1, 999, jnp.int32), jax.random.randint(jax.random.fold_in(jax.random.fold_in(_rk, 10), 77), (512,), 0, 1000, jnp.int32), jax.random.randint(jax.random.fold_in(jax.random.fold_in(_rk, 10), 78), (512,), 0, 1000, jnp.int32), jax.random.randint(jax.random.fold_in(jax.random.fold_in(_rk, 10), 79), (512,), 0, 1000, jnp.int32), jax.random.randint(jax.random.fold_in(jax.random.fold_in(_rk, 10), 80), (512,), 0, 999, jnp.int32), jax.random.randint(jax.random.fold_in(jax.random.fold_in(_rk, 10), 81), (512,), 0, 999, jnp.int32), jax.random.randint(jax.random.fold_in(jax.random.fold_in(_rk, 10), 82), (512,), 0, 1000, jnp.int32), jax.random.randint(jax.random.fold_in(jax.random.fold_in(_rk, 10), 83), (512,), 0, 1000, jnp.int32), jax.random.randint(jax.random.fold_in(jax.random.fold_in(_rk, 10), 84), (512,), 0, 1000, jnp.int32), jax.random.randint(jax.random.fold_in(jax.random.fold_in(_rk, 10), 85), (512,), 1, 1000, jnp.int32), jax.random.randint(jax.random.fold_in(jax.random.fold_in(_rk, 10), 86), (512,), 0, 999, jnp.int32), jax.random.randint(jax.random.fold_in(jax.random.fold_in(_rk, 10), 87), (512,), 0, 998, jnp.int32), jax.random.randint(jax.random.fold_in(jax.random.fold_in(_rk, 10), 88), (512,), 0, 1000, jnp.int32), jax.random.randint(jax.random.fold_in(jax.random.fold_in(_rk, 10), 89), (512,), 0, 997, jnp.int32), jax.random.randint(jax.random.fold_in(jax.random.fold_in(_rk, 10), 90), (512,), 0, 1000, jnp.int32), jax.random.randint(jax.random.fold_in(jax.random.fold_in(_rk, 10), 91), (512,), 0, 1000, jnp.int32), jax.random.randint(jax.random.fold_in(jax.random.fold_in(_rk, 10), 92), (512,), 0, 1000, jnp.int32), jax.random.randint(jax.random.fold_in(jax.random.fold_in(_rk, 10), 93), (512,), 0, 1000, jnp.int32), jax.random.randint(jax.random.fold_in(jax.random.fold_in(_rk, 10), 94), (512,), 0, 1000, jnp.int32), jax.random.randint(jax.random.fold_in(jax.random.fold_in(_rk, 10), 95), (512,), 1, 1000, jnp.int32), jax.random.randint(jax.random.fold_in(jax.random.fold_in(_rk, 10), 96), (512,), 0, 1000, jnp.int32), jax.random.randint(jax.random.fold_in(jax.random.fold_in(_rk, 10), 97), (512,), 0, 1000, jnp.int32), jax.random.randint(jax.random.fold_in(jax.random.fold_in(_rk, 10), 98), (512,), 0, 1000, jnp.int32), jax.random.randint(jax.random.fold_in(jax.random.fold_in(_rk, 10), 99), (512,), 2, 999, jnp.int32), jax.random.randint(jax.random.fold_in(jax.random.fold_in(_rk, 10), 100), (512,), 2, 1000, jnp.int32), jax.random.randint(jax.random.fold_in(jax.random.fold_in(_rk, 10), 101), (512,), 1, 1000, jnp.int32), jax.random.randint(jax.random.fold_in(jax.random.fold_in(_rk, 10), 102), (512,), 1, 1000, jnp.int32), jax.random.randint(jax.random.fold_in(jax.random.fold_in(_rk, 10), 103), (512,), 1, 997, jnp.int32), jax.random.randint(jax.random.fold_in(jax.random.fold_in(_rk, 10), 104), (512,), 0, 1000, jnp.int32), jax.random.randint(jax.random.fold_in(jax.random.fold_in(_rk, 10), 105), (512,), 0, 999, jnp.int32), jax.random.randint(jax.random.fold_in(jax.random.fold_in(_rk, 10), 106), (512,), 2, 1000, jnp.int32), jax.random.randint(jax.random.fold_in(jax.random.fold_in(_rk, 10), 107), (512,), 1, 1000, jnp.int32), jax.random.randint(jax.random.fold_in(jax.random.fold_in(_rk, 10), 108), (512,), 0, 1000, jnp.int32), jax.random.randint(jax.random.fold_in(jax.random.fold_in(_rk, 10), 109), (512,), 0, 999, jnp.int32), jax.random.randint(jax.random.fold_in(jax.random.fold_in(_rk, 10), 110), (512,), 0, 998, jnp.int32), jax.random.randint(jax.random.fold_in(jax.random.fold_in(_rk, 10), 111), (512,), 2, 999, jnp.int32), jax.random.randint(jax.random.fold_in(jax.random.fold_in(_rk, 10), 112), (512,), 1, 999, jnp.int32), jax.random.randint(jax.random.fold_in(jax.random.fold_in(_rk, 10), 113), (512,), 0, 999, jnp.int32), jax.random.randint(jax.random.fold_in(jax.random.fold_in(_rk, 10), 114), (512,), 0, 1000, jnp.int32), jax.random.randint(jax.random.fold_in(jax.random.fold_in(_rk, 10), 115), (512,), 0, 999, jnp.int32), jax.random.randint(jax.random.fold_in(jax.random.fold_in(_rk, 10), 116), (512,), 0, 1000, jnp.int32), jax.random.randint(jax.random.fold_in(jax.random.fold_in(_rk, 10), 117), (512,), 0, 999, jnp.int32), jax.random.randint(jax.random.fold_in(jax.random.fold_in(_rk, 10), 118), (512,), 0, 999, jnp.int32), jax.random.randint(jax.random.fold_in(jax.random.fold_in(_rk, 10), 119), (512,), 0, 1000, jnp.int32), jax.random.randint(jax.random.fold_in(jax.random.fold_in(_rk, 10), 120), (512,), 0, 1000, jnp.int32), jax.random.randint(jax.random.fold_in(jax.random.fold_in(_rk, 10), 121), (512,), 4, 1000, jnp.int32), jax.random.randint(jax.random.fold_in(jax.random.fold_in(_rk, 10), 122), (512,), 0, 1000, jnp.int32), jax.random.randint(jax.random.fold_in(jax.random.fold_in(_rk, 10), 123), (512,), 0, 998, jnp.int32), jax.random.randint(jax.random.fold_in(jax.random.fold_in(_rk, 10), 124), (512,), 0, 1000, jnp.int32), jax.random.randint(jax.random.fold_in(jax.random.fold_in(_rk, 10), 125), (512,), 0, 1000, jnp.int32), jax.random.randint(jax.random.fold_in(jax.random.fold_in(_rk, 10), 126), (512,), 1, 999, jnp.int32), jax.random.randint(jax.random.fold_in(jax.random.fold_in(_rk, 10), 127), (512,), 0, 1000, jnp.int32), jax.random.randint(jax.random.fold_in(jax.random.fold_in(_rk, 10), 128), (512,), 0, 1000, jnp.int32), jax.random.randint(jax.random.fold_in(jax.random.fold_in(_rk, 10), 129), (512,), 0, 1000, jnp.int32), jax.random.randint(jax.random.fold_in(jax.random.fold_in(_rk, 10), 130), (512,), 0, 998, jnp.int32), jax.random.randint(jax.random.fold_in(jax.random.fold_in(_rk, 10), 131), (512,), 0, 1000, jnp.int32), jax.random.randint(jax.random.fold_in(jax.random.fold_in(_rk, 10), 132), (512,), 0, 999, jnp.int32), jax.random.randint(jax.random.fold_in(jax.random.fold_in(_rk, 10), 133), (512,), 1, 1000, jnp.int32), jax.random.randint(jax.random.fold_in(jax.random.fold_in(_rk, 10), 134), (512,), 1, 1000, jnp.int32), jax.random.randint(jax.random.fold_in(jax.random.fold_in(_rk, 10), 135), (512,), 0, 998, jnp.int32), jax.random.randint(jax.random.fold_in(jax.random.fold_in(_rk, 10), 136), (512,), 0, 1000, jnp.int32), jax.random.randint(jax.random.fold_in(jax.random.fold_in(_rk, 10), 137), (512,), 0, 1000, jnp.int32), jax.random.randint(jax.random.fold_in(jax.random.fold_in(_rk, 10), 138), (512,), 0, 998, jnp.int32), jax.random.randint(jax.random.fold_in(jax.random.fold_in(_rk, 10), 139), (512,), 1, 999, jnp.int32), jax.random.randint(jax.random.fold_in(jax.random.fold_in(_rk, 10), 140), (512,), 1, 1000, jnp.int32), jax.random.randint(jax.random.fold_in(jax.random.fold_in(_rk, 10), 141), (512,), 0, 999, jnp.int32), jax.random.randint(jax.random.fold_in(jax.random.fold_in(_rk, 10), 142), (512,), 0, 1000, jnp.int32), jax.random.randint(jax.random.fold_in(jax.random.fold_in(_rk, 10), 143), (512,), 0, 1000, jnp.int32), jax.random.randint(jax.random.fold_in(jax.random.fold_in(_rk, 10), 144), (512,), 0, 999, jnp.int32), jax.random.randint(jax.random.fold_in(jax.random.fold_in(_rk, 10), 145), (512,), 3, 1000, jnp.int32), jax.random.randint(jax.random.fold_in(jax.random.fold_in(_rk, 10), 146), (512,), 1, 1000, jnp.int32), jax.random.randint(jax.random.fold_in(jax.random.fold_in(_rk, 10), 147), (512,), 3, 1000, jnp.int32), jax.random.randint(jax.random.fold_in(jax.random.fold_in(_rk, 10), 148), (512,), 0, 1000, jnp.int32), jax.random.randint(jax.random.fold_in(jax.random.fold_in(_rk, 10), 149), (512,), 0, 1000, jnp.int32), jax.random.randint(jax.random.fold_in(jax.random.fold_in(_rk, 10), 150), (512,), 0, 999, jnp.int32), jax.random.randint(jax.random.fold_in(jax.random.fold_in(_rk, 10), 151), (512,), 2, 1000, jnp.int32), jax.random.randint(jax.random.fold_in(jax.random.fold_in(_rk, 10), 152), (512,), 0, 1000, jnp.int32), jax.random.randint(jax.random.fold_in(jax.random.fold_in(_rk, 10), 153), (512,), 1, 1000, jnp.int32), jax.random.randint(jax.random.fold_in(jax.random.fold_in(_rk, 10), 154), (512,), 1, 1000, jnp.int32), jax.random.randint(jax.random.fold_in(jax.random.fold_in(_rk, 10), 155), (512,), 0, 1000, jnp.int32), jax.random.randint(jax.random.fold_in(jax.random.fold_in(_rk, 10), 156), (512,), 1, 1000, jnp.int32), jax.random.randint(jax.random.fold_in(jax.random.fold_in(_rk, 10), 157), (512,), 0, 999, jnp.int32), jax.random.randint(jax.random.fold_in(jax.random.fold_in(_rk, 10), 158), (512,), 3, 1000, jnp.int32), jax.random.randint(jax.random.fold_in(jax.random.fold_in(_rk, 10), 159), (512,), 0, 1000, jnp.int32), jax.random.randint(jax.random.fold_in(jax.random.fold_in(_rk, 10), 160), (512,), 0, 1000, jnp.int32), jax.random.randint(jax.random.fold_in(jax.random.fold_in(_rk, 10), 161), (512,), 1, 1000, jnp.int32), jax.random.randint(jax.random.fold_in(jax.random.fold_in(_rk, 10), 162), (512,), 1, 1000, jnp.int32), jax.random.randint(jax.random.fold_in(jax.random.fold_in(_rk, 10), 163), (512,), 0, 1000, jnp.int32), jax.random.randint(jax.random.fold_in(jax.random.fold_in(_rk, 10), 164), (512,), 1, 999, jnp.int32), jax.random.randint(jax.random.fold_in(jax.random.fold_in(_rk, 10), 165), (512,), 2, 1000, jnp.int32), jax.random.randint(jax.random.fold_in(jax.random.fold_in(_rk, 10), 166), (512,), 0, 999, jnp.int32), jax.random.randint(jax.random.fold_in(jax.random.fold_in(_rk, 10), 167), (512,), 2, 1000, jnp.int32), jax.random.randint(jax.random.fold_in(jax.random.fold_in(_rk, 10), 168), (512,), 1, 998, jnp.int32), jax.random.randint(jax.random.fold_in(jax.random.fold_in(_rk, 10), 169), (512,), 0, 1000, jnp.int32), jax.random.randint(jax.random.fold_in(jax.random.fold_in(_rk, 10), 170), (512,), 0, 1000, jnp.int32), jax.random.randint(jax.random.fold_in(jax.random.fold_in(_rk, 10), 171), (512,), 0, 997, jnp.int32), jax.random.randint(jax.random.fold_in(jax.random.fold_in(_rk, 10), 172), (512,), 0, 1000, jnp.int32), jax.random.randint(jax.random.fold_in(jax.random.fold_in(_rk, 10), 173), (512,), 0, 999, jnp.int32), jax.random.randint(jax.random.fold_in(jax.random.fold_in(_rk, 10), 174), (512,), 0, 1000, jnp.int32), jax.random.randint(jax.random.fold_in(jax.random.fold_in(_rk, 10), 175), (512,), 0, 999, jnp.int32), jax.random.randint(jax.random.fold_in(jax.random.fold_in(_rk, 10), 176), (512,), 1, 1000, jnp.int32), jax.random.randint(jax.random.fold_in(jax.random.fold_in(_rk, 10), 177), (512,), 0, 1000, jnp.int32), jax.random.randint(jax.random.fold_in(jax.random.fold_in(_rk, 10), 178), (512,), 1, 1000, jnp.int32), jax.random.randint(jax.random.fold_in(jax.random.fold_in(_rk, 10), 179), (512,), 1, 1000, jnp.int32), jax.random.randint(jax.random.fold_in(jax.random.fold_in(_rk, 10), 180), (512,), 1, 1000, jnp.int32), jax.random.randint(jax.random.fold_in(jax.random.fold_in(_rk, 10), 181), (512,), 1, 1000, jnp.int32), jax.random.randint(jax.random.fold_in(jax.random.fold_in(_rk, 10), 182), (512,), 0, 1000, jnp.int32), jax.random.randint(jax.random.fold_in(jax.random.fold_in(_rk, 10), 183), (512,), 1, 1000, jnp.int32), jax.random.randint(jax.random.fold_in(jax.random.fold_in(_rk, 10), 184), (512,), 0, 1000, jnp.int32), jax.random.randint(jax.random.fold_in(jax.random.fold_in(_rk, 10), 185), (512,), 0, 1000, jnp.int32), jax.random.randint(jax.random.fold_in(jax.random.fold_in(_rk, 10), 186), (512,), 2, 1000, jnp.int32), jax.random.randint(jax.random.fold_in(jax.random.fold_in(_rk, 10), 187), (512,), 2, 1000, jnp.int32), jax.random.randint(jax.random.fold_in(jax.random.fold_in(_rk, 10), 188), (512,), 0, 1000, jnp.int32), jax.random.randint(jax.random.fold_in(jax.random.fold_in(_rk, 10), 189), (512,), 0, 1000, jnp.int32), jax.random.randint(jax.random.fold_in(jax.random.fold_in(_rk, 10), 190), (512,), 0, 1000, jnp.int32), jax.random.randint(jax.random.fold_in(jax.random.fold_in(_rk, 10), 191), (512,), 0, 1000, jnp.int32), jax.random.randint(jax.random.fold_in(jax.random.fold_in(_rk, 10), 192), (512,), 0, 996, jnp.int32), jax.random.randint(jax.random.fold_in(jax.random.fold_in(_rk, 10), 193), (512,), 0, 1000, jnp.int32), jax.random.randint(jax.random.fold_in(jax.random.fold_in(_rk, 10), 194), (512,), 1, 1000, jnp.int32), jax.random.randint(jax.random.fold_in(jax.random.fold_in(_rk, 10), 195), (512,), 0, 1000, jnp.int32), jax.random.randint(jax.random.fold_in(jax.random.fold_in(_rk, 10), 196), (512,), 1, 1000, jnp.int32), jax.random.randint(jax.random.fold_in(jax.random.fold_in(_rk, 10), 197), (512,), 0, 999, jnp.int32), jax.random.randint(jax.random.fold_in(jax.random.fold_in(_rk, 10), 198), (512,), 1, 999, jnp.int32), jax.random.randint(jax.random.fold_in(jax.random.fold_in(_rk, 10), 199), (512,), 0, 998, jnp.int32)], axis=1)
        return (r_num_feat1, r_num_feat2, r_score, r_user_id, r_cand_item_id, r_cand_item_cat, r_exp_item_id, r_exp_item_cat, r_ipv_item_id, r_ipv_item_cat)
    r_num_feat1, r_num_feat2, r_score, r_user_id, r_cand_item_id, r_cand_item_cat, r_exp_item_id, r_exp_item_cat, r_ipv_item_id, r_ipv_item_cat = _rec_inputs()

    def _L0_rec_setup():
        import jax, jax.numpy as jnp
        import numpy as np
        B, L = (1024, 200)
        N_ITEM, N_CAT, N_USER = (12500, 1000, 12500)
        D_ID, D_CAT, D_USER = (64, 32, 32)
        D_ITEM = D_ID + D_CAT
        CAT_SIZE = 2 + D_USER + 3 * D_ITEM
        H1, H2 = (200, 80)
        BN_EPS = 1e-05

        def _attention_pool(seq, tgt, w1, b1, w2, b2):
            t = jnp.broadcast_to(tgt[:, None, :], seq.shape)
            cat = jnp.concatenate([seq, t, seq - t, seq * t], axis=-1)
            h = jax.nn.relu(cat @ w1 + b1)
            logits = h @ w2 + b2
            w = jax.nn.softmax(logits, axis=1)
            return jnp.sum(w * seq, axis=1)

        def _bn_eval(x, g, b, m, v):
            return (x - m) * jax.lax.rsqrt(v + BN_EPS) * g + b
        key = jax.random.key(seed)
        ks = jax.random.split(key, 32)
        inp = {}
        inp['num_feat1'] = jax.random.normal(ks[0], (B,), jnp.float32)
        inp['num_feat2'] = jax.random.normal(ks[1], (B,), jnp.float32)
        inp['score'] = jax.random.uniform(ks[2], (B,), jnp.float32, 0.05, 0.95)
        inp['user_id'] = jax.random.randint(ks[3], (B,), 0, N_USER)
        inp['cand_item_id'] = jax.random.randint(ks[4], (B,), 0, N_ITEM)
        inp['cand_item_cat'] = jax.random.randint(ks[5], (B,), 0, N_CAT)
        inp['exp_item_id'] = jax.random.randint(ks[6], (B, L), 0, N_ITEM)
        inp['exp_item_cat'] = jax.random.randint(ks[7], (B, L), 0, N_CAT)
        inp['ipv_item_id'] = jax.random.randint(ks[8], (B, L), 0, N_ITEM)
        inp['ipv_item_cat'] = jax.random.randint(ks[9], (B, L), 0, N_CAT)
        s = 0.02
        inp['emb_item_id'] = jax.random.normal(ks[10], (N_ITEM, D_ID), jnp.float32) * s
        inp['emb_item_cat'] = jax.random.normal(ks[11], (N_CAT, D_CAT), jnp.float32) * s
        inp['emb_user'] = jax.random.normal(ks[12], (N_USER, D_USER), jnp.float32) * s
        inp['att_w1'] = jax.random.normal(ks[13], (4 * D_ITEM, D_ITEM), jnp.float32) * s
        inp['att_b1'] = jnp.zeros((D_ITEM,), jnp.float32)
        inp['att_w2'] = jax.random.normal(ks[14], (D_ITEM, 1), jnp.float32) * s
        inp['att_b2'] = jnp.zeros((1,), jnp.float32)
        inp['fc1_w'] = jax.random.normal(ks[15], (CAT_SIZE, H1), jnp.float32) * s
        inp['fc1_b'] = jnp.zeros((H1,), jnp.float32)
        inp['bn1_g'] = jnp.ones((H1,), jnp.float32)
        inp['bn1_b'] = jnp.zeros((H1,), jnp.float32)
        inp['bn1_m'] = jax.random.normal(ks[16], (H1,), jnp.float32) * 0.1
        inp['bn1_v'] = jax.random.uniform(ks[17], (H1,), jnp.float32, 0.5, 1.5)
        inp['fc2_w'] = jax.random.normal(ks[18], (H1, H2), jnp.float32) * s
        inp['fc2_b'] = jnp.zeros((H2,), jnp.float32)
        inp['bn2_g'] = jnp.ones((H2,), jnp.float32)
        inp['bn2_b'] = jnp.zeros((H2,), jnp.float32)
        inp['bn2_m'] = jax.random.normal(ks[19], (H2,), jnp.float32) * 0.1
        inp['bn2_v'] = jax.random.uniform(ks[20], (H2,), jnp.float32, 0.5, 1.5)
        inp['fc3_w'] = jax.random.normal(ks[21], (H2, 1), jnp.float32) * s
        inp['fc3_b'] = jnp.zeros((1,), jnp.float32)
        return inp
    _L0_rec_all = _L0_rec_setup()
    _L0_rec_in = {k: v for k, v in _L0_rec_all.items() if k in ('emb_item_id', 'emb_item_cat', 'emb_user', 'att_w1', 'att_b1', 'att_w2', 'att_b2', 'fc1_w', 'fc1_b', 'bn1_g', 'bn1_b', 'bn1_m', 'bn1_v', 'fc2_w', 'fc2_b', 'bn2_g', 'bn2_b', 'bn2_m', 'bn2_v', 'fc3_w', 'fc3_b')}
    del _L0_rec_all
    return {'r_num_feat1': r_num_feat1, 'r_num_feat2': r_num_feat2, 'r_score': r_score, 'r_user_id': r_user_id, 'r_cand_item_id': r_cand_item_id, 'r_cand_item_cat': r_cand_item_cat, 'r_exp_item_id': r_exp_item_id, 'r_exp_item_cat': r_exp_item_cat, 'r_ipv_item_id': r_ipv_item_id, 'r_ipv_item_cat': r_ipv_item_cat, 'L0_rec_emb_item_id': _L0_rec_in['emb_item_id'], 'L0_rec_emb_item_cat': _L0_rec_in['emb_item_cat'], 'L0_rec_emb_user': _L0_rec_in['emb_user'], 'L0_rec_att_w1': _L0_rec_in['att_w1'], 'L0_rec_att_b1': _L0_rec_in['att_b1'], 'L0_rec_att_w2': _L0_rec_in['att_w2'], 'L0_rec_att_b2': _L0_rec_in['att_b2'], 'L0_rec_fc1_w': _L0_rec_in['fc1_w'], 'L0_rec_fc1_b': _L0_rec_in['fc1_b'], 'L0_rec_bn1_g': _L0_rec_in['bn1_g'], 'L0_rec_bn1_b': _L0_rec_in['bn1_b'], 'L0_rec_bn1_m': _L0_rec_in['bn1_m'], 'L0_rec_bn1_v': _L0_rec_in['bn1_v'], 'L0_rec_fc2_w': _L0_rec_in['fc2_w'], 'L0_rec_fc2_b': _L0_rec_in['fc2_b'], 'L0_rec_bn2_g': _L0_rec_in['bn2_g'], 'L0_rec_bn2_b': _L0_rec_in['bn2_b'], 'L0_rec_bn2_m': _L0_rec_in['bn2_m'], 'L0_rec_bn2_v': _L0_rec_in['bn2_v'], 'L0_rec_fc3_w': _L0_rec_in['fc3_w'], 'L0_rec_fc3_b': _L0_rec_in['fc3_b']}

def reference(r_num_feat1, r_num_feat2, r_score, r_user_id, r_cand_item_id, r_cand_item_cat, r_exp_item_id, r_exp_item_cat, r_ipv_item_id, r_ipv_item_cat, L0_rec_emb_item_id, L0_rec_emb_item_cat, L0_rec_emb_user, L0_rec_att_w1, L0_rec_att_b1, L0_rec_att_w2, L0_rec_att_b2, L0_rec_fc1_w, L0_rec_fc1_b, L0_rec_bn1_g, L0_rec_bn1_b, L0_rec_bn1_m, L0_rec_bn1_v, L0_rec_fc2_w, L0_rec_fc2_b, L0_rec_bn2_g, L0_rec_bn2_b, L0_rec_bn2_m, L0_rec_bn2_v, L0_rec_fc3_w, L0_rec_fc3_b):
    import jax
    import jax.numpy as jnp

    def _L0_rec_ref(num_feat1, num_feat2, score, emb_item_id, emb_item_cat, emb_user, att_w1, att_b1, att_w2, att_b2, fc1_w, fc1_b, bn1_g, bn1_b, bn1_m, bn1_v, fc2_w, fc2_b, bn2_g, bn2_b, bn2_m, bn2_v, fc3_w, fc3_b, user_id, cand_item_id, cand_item_cat, exp_item_id, exp_item_cat, ipv_item_id, ipv_item_cat):
        import jax, jax.numpy as jnp
        import numpy as np
        B, L = (1024, 200)
        N_ITEM, N_CAT, N_USER = (12500, 1000, 12500)
        D_ID, D_CAT, D_USER = (64, 32, 32)
        D_ITEM = D_ID + D_CAT
        CAT_SIZE = 2 + D_USER + 3 * D_ITEM
        H1, H2 = (200, 80)
        BN_EPS = 1e-05

        def _attention_pool(seq, tgt, w1, b1, w2, b2):
            t = jnp.broadcast_to(tgt[:, None, :], seq.shape)
            cat = jnp.concatenate([seq, t, seq - t, seq * t], axis=-1)
            h = jax.nn.relu(cat @ w1 + b1)
            logits = h @ w2 + b2
            w = jax.nn.softmax(logits, axis=1)
            return jnp.sum(w * seq, axis=1)

        def _bn_eval(x, g, b, m, v):
            return (x - m) * jax.lax.rsqrt(v + BN_EPS) * g + b
        user = emb_user[user_id]
        cand = jnp.concatenate([emb_item_id[cand_item_id], emb_item_cat[cand_item_cat]], axis=-1)
        exp_seq = jnp.concatenate([emb_item_id[exp_item_id], emb_item_cat[exp_item_cat]], axis=-1)
        ipv_seq = jnp.concatenate([emb_item_id[ipv_item_id], emb_item_cat[ipv_item_cat]], axis=-1)
        exp_out = _attention_pool(exp_seq, cand, att_w1, att_b1, att_w2, att_b2)
        ipv_out = _attention_pool(ipv_seq, cand, att_w1, att_b1, att_w2, att_b2)
        x = jnp.concatenate([num_feat1[:, None], num_feat2[:, None], user, cand, exp_out, ipv_out], axis=1)
        h = jax.nn.relu(_bn_eval(x @ fc1_w + fc1_b, bn1_g, bn1_b, bn1_m, bn1_v))
        h = jax.nn.relu(_bn_eval(h @ fc2_w + fc2_b, bn2_g, bn2_b, bn2_m, bn2_v))
        mlp_out = h @ fc3_w + fc3_b
        score_logits = -jnp.log(1.0 / score[:, None] - 1.0)
        return jax.nn.sigmoid(mlp_out + score_logits)
    y = _L0_rec_ref(r_num_feat1, r_num_feat2, r_score, L0_rec_emb_item_id, L0_rec_emb_item_cat, L0_rec_emb_user, L0_rec_att_w1, L0_rec_att_b1, L0_rec_att_w2, L0_rec_att_b2, L0_rec_fc1_w, L0_rec_fc1_b, L0_rec_bn1_g, L0_rec_bn1_b, L0_rec_bn1_m, L0_rec_bn1_v, L0_rec_fc2_w, L0_rec_fc2_b, L0_rec_bn2_g, L0_rec_bn2_b, L0_rec_bn2_m, L0_rec_bn2_v, L0_rec_fc3_w, L0_rec_fc3_b, r_user_id, r_cand_item_id, r_cand_item_cat, r_exp_item_id, r_exp_item_cat, r_ipv_item_id, r_ipv_item_cat)
    return y

_drawn_inputs = setup_inputs


def setup_inputs(seed=0):
    import zlib

    import numpy as np

    out = dict(_drawn_inputs(seed))
    spreads = {'L0_rec_att_b1': (0.0, 2.0),
     'L0_rec_fc1_b': (0.0, 0.8),
     'L0_rec_bn1_g': (1.0, 0.6),
     'L0_rec_bn1_b': (0.0, 0.8),
     'L0_rec_fc2_b': (0.0, 0.8),
     'L0_rec_bn2_g': (1.0, 0.6),
     'L0_rec_bn2_b': (0.0, 0.8)}
    factors = {'r_num_feat1': 8.0,
     'r_num_feat2': 8.0,
     'L0_rec_emb_item_id': 8.0,
     'L0_rec_emb_item_cat': 28.246,
     'L0_rec_emb_user': 8.0,
     'L0_rec_att_w1': 64.0,
     'L0_rec_att_w2': 64.0,
     'L0_rec_fc1_w': 8.0,
     'L0_rec_bn1_m': 8.0,
     'L0_rec_bn1_v': 8.0,
     'L0_rec_fc2_w': 8.0,
     'L0_rec_bn2_m': 8.0,
     'L0_rec_bn2_v': 8.0,
     'L0_rec_fc3_w': 8.0}
    for name, (base, spread) in spreads.items():
        noise = np.random.default_rng([zlib.crc32(name.encode()), seed]).standard_normal(out[name].shape)
        drawn = base * np.exp(spread * noise) if base else spread * noise
        out[name] = jnp.asarray(drawn.astype(out[name].dtype))
    for name, factor in factors.items():
        out[name] = (out[name] * factor).astype(out[name].dtype)
    return out
```

```python
from contextlib import ExitStack

import concourse.bass as bass
from concourse import mybir

ALU = mybir.AluOpType
ACT = mybir.ActivationFunctionType
F32 = mybir.dt.float32
I32 = mybir.dt.int32
U32 = mybir.dt.uint32
AX_X = mybir.AxisListType.X

P = 128
GB = 16
R = P // GB
SEQS = 2
BN_EPS = 1e-05


def recommend(nc, num1, num2, score, user_id, cand_id, cand_cat, exp_id, exp_cat, ipv_id, ipv_cat,
              emb_item, emb_cat, emb_user, att_w1, att_b1, att_w2, att_b2,
              fc1_w, fc1_b, bn1_g, bn1_b, bn1_m, bn1_v, fc2_w, fc2_b, bn2_g, bn2_b, bn2_m, bn2_v,
              fc3_w, fc3_b, out):
    B, L = exp_id.shape
    N_ITEM, D_ID = emb_item.shape
    N_CAT, D_CAT = emb_cat.shape
    N_USER, D_USER = emb_user.shape
    D = D_ID + D_CAT
    H1, H2 = fc2_w.shape
    HC = H1 // 2
    NG = B // GB
    NP = B // P
    T = L // R
    TT = 4
    TB = -(-T // TT)
    NH = GB // 2
    XM = D_USER + 2
    SHIFT = 10
    assert N_CAT <= 1 << SHIFT and N_ITEM << SHIFT < 1 << 24 and T * R == L
    N_WEIGHTS = 23
    CUTS = [0, 4, 6, 7, 8, 9, 11, 14, 18, T]

    with ExitStack() as ctx:
        def sb(name, shape, dt=F32):
            return ctx.enter_context(nc.sbuf_tensor(name, shape, dt))

        def ps(name, shape, dt=F32):
            return ctx.enter_context(nc.psum_tensor(name, shape, dt))

        def sem(name):
            return ctx.enter_context(nc.semaphore(name))

        item_d = nc.dram_tensor("sorted_items", (SEQS, B * R, T), I32, kind="Internal").ap()
        cat_d = nc.dram_tensor("sorted_cats", (SEQS, B * R, T), I32, kind="Internal").ap()
        tiles_d = nc.dram_tensor("tiles_to_gather", (SEQS * NG, 1), I32, kind="Internal").ap()

        ident = sb("ident", [P, P])
        raw_item = sb("raw_item", [P, SEQS, NP, L], I32)
        raw_cat = sb("raw_cat", [P, SEQS, NP, L], I32)
        key = sb("key", [P, SEQS, NP, L])
        key2 = sb("key2", [P, SEQS, NP, L])
        top = sb("top", [P, SEQS * NP, R])
        ranked = sb("ranked", [P, SEQS, NP, R, T])
        ranked_i = raw_item
        srt_item = sb("srt_item", [P, SEQS, NP, L], I32)
        srt_cat = sb("srt_cat", [P, SEQS, NP, L], I32)
        in_range = sb("in_range", [P, SEQS * NP, T])
        n_tiles = sb("n_tiles", [P, SEQS * NP])
        group_tiles = sb("group_tiles", [SEQS * NP, P // GB], I32)

        one_id = sb("one_id", [P, 3, NP], I32)
        one_f = sb("one_f", [P, 3, NP])
        one_neg = sb("one_neg", [P, 3, NP])
        one_idx = sb("one_idx", [P, 3, NP], I32)
        cand_rows = sb("cand_rows", [P, NP, D])
        user_rows = sb("user_rows", [P, NP, D_USER])
        last_index = sb("last_index", [P, 1], I32)
        last_row = sb("last_row", [P, D_ID])
        last_rows = sb("last_rows", [P, T, D_ID])

        w1 = sb("w1", [D, 4, D])
        w_seq = sb("w_seq", [D, D])
        w_tgt = sb("w_tgt", [D, D])
        b1 = sb("b1", [D, 1])
        w2 = sb("w2", [D, 1])
        b2 = sb("b2", [P, 1])
        cand_t = sb("cand_t", [D, B])
        bias_t = sb("bias_t", [D, B])
        misc_t = sb("misc_t", [XM, B])
        pooled_t = [sb(f"pooled_t{s}", [D, B]) for s in range(SEQS)]
        sel = sb("sel", [P, GB])

        items = [sb(f"items{s}", [P, T], I32) for s in range(SEQS)]
        cats = [sb(f"cats{s}", [P, T], I32) for s in range(SEQS)]
        tiles = [sb(f"tiles{s}", [1, 1], I32) for s in range(SEQS)]
        rows = [sb(f"rows{s}", [P, T, D]) for s in range(SEQS)]
        seq_t = [sb(f"seq_t{s}", [D, GB, L]) for s in range(SEQS)]
        cand_g = sb("cand_g", [D, GB])
        bias_g = sb("bias_g", [D, GB])
        mix = sb("mix", [D, GB, D])
        hidden = [sb(f"hidden{s}", [D, T, GB, R]) for s in range(SEQS)]
        logits = [sb(f"logits{s}", [P, T]) for s in range(SEQS)]
        logits_b = [sb(f"logits_b{s}", [GB, L]) for s in range(SEQS)]
        neg_max = [sb(f"neg_max{s}", [GB, 1]) for s in range(SEQS)]
        exps = [sb(f"exps{s}", [GB, L]) for s in range(SEQS)]
        total = [sb(f"total{s}", [GB, 1]) for s in range(SEQS)]
        inv = [sb(f"inv{s}", [GB, 1]) for s in range(SEQS)]
        probs_b = [sb(f"probs_b{s}", [GB, L]) for s in range(SEQS)]
        probs = [sb(f"probs{s}", [P, T]) for s in range(SEQS)]
        spread = [sb(f"spread{s}", [P, T, GB]) for s in range(SEQS)]

        fc1_m = sb("fc1_m", [XM, H1])
        fc1_x = sb("fc1_x", [D, 3, H1])
        fc2 = sb("fc2", [HC, 2, H2])
        fc3 = sb("fc3", [H2, 1])
        bn1 = sb("bn1", [HC, 5, 2])
        bn2 = sb("bn2", [H2, 5, 1])
        bn1_w = sb("bn1_w", [HC, 4, 2])
        bn2_w = sb("bn2_w", [H2, 4, 1])
        fc3_bias = sb("fc3_bias", [1, 1])
        h1 = sb("h1", [HC, 2, B])
        h2 = sb("h2", [H2, B])
        sc = sb("sc", [1, 5, B])

        turned = [ps(f"turned{i}", [P, TT * P]) for i in range(2)]
        pre = [ps(f"pre{i}", [D, 2, 256]) for i in range(2)]
        score_ps = ps("score_ps", [P, 512])
        pool_ps = ps("pool_ps", [D, 512])
        misc_ps = ps("misc_ps", [P, 512])

        ids_loaded = sem("ids_loaded")
        ones_loaded = sem("ones_loaded")
        weights_loaded = sem("weights_loaded")
        ident_set = sem("ident_set")
        step = sem("step")
        top_found = sem("top_found")
        top_cut = sem("top_cut")
        top_kept = sem("top_kept")
        ranked_ready = sem("ranked_ready")
        tiles_turned = sem("tiles_turned")
        tiles_ready = sem("tiles_ready")
        sorted_stored = sem("sorted_stored")
        one_ready = sem("one_ready")
        last_ready = sem("last_ready")
        last_filled = sem("last_filled")
        last_row_in = sem("last_row_in")
        one_gathered = sem("one_gathered")
        head_turned = sem("head_turned")
        head_copied = sem("head_copied")
        index_loaded = [sem(f"index_loaded{s}") for s in range(SEQS)]
        index_seen = [sem(f"index_seen{s}") for s in range(SEQS)]
        tiles_known = [sem(f"tiles_known{s}") for s in range(SEQS)]
        gathered_item = [sem(f"gathered_item{s}") for s in range(SEQS)]
        gathered_cat = [sem(f"gathered_cat{s}") for s in range(SEQS)]
        group_set = sem("group_set")
        mix_ready = sem("mix_ready")
        mixed = sem("mixed")
        turned_ready = sem("turned_ready")
        turned_read = sem("turned_read")
        pre_ready = sem("pre_ready")
        pre_read = sem("pre_read")
        score_ready = sem("score_ready")
        score_read = sem("score_read")
        logits_moved = [sem(f"logits_moved{s}") for s in range(SEQS)]
        max_ready = sem("max_ready")
        max_negated = sem("max_negated")
        exps_ready = sem("exps_ready")
        inv_ready = sem("inv_ready")
        probs_ready = sem("probs_ready")
        probs_moved = [sem(f"probs_moved{s}") for s in range(SEQS)]
        spread_ready = sem("spread_ready")
        pooled_ready = [sem(f"pooled_ready{s}") for s in range(SEQS)]
        pooled_read = sem("pooled_read")
        fc_ready = sem("fc_ready")
        fc_read = sem("fc_read")
        root_ready = sem("root_ready")
        bn_ready = sem("bn_ready")
        score_step = sem("score_step")
        stored = sem("stored")

        block = ctx.enter_context(nc.Block())

        def pre_of(s, k):
            return pre[(s * NH + k) % 2]

        def load_columns(eng, dst, v, p):
            return eng.dma_start(dst, v.rearrange("(c p) -> p c", p=p), allow_slow_non_contiguous=True)

        @block.sync
        def _(sp):
            for s, (item, cat) in enumerate(((exp_id, exp_cat), (ipv_id, ipv_cat))):
                sp.dma_start(raw_item[:, s], item.rearrange("(n p) l -> p n l", p=P)).then_inc(ids_loaded, 16)
                sp.dma_start(raw_cat[:, s], cat.rearrange("(n p) l -> p n l", p=P)).then_inc(ids_loaded, 16)
            for k, v in enumerate((cand_id, cand_cat, user_id)):
                load_columns(sp, one_id[:, k], v, P).then_inc(ones_loaded, 16)
            w = weights_loaded
            sp.dma_start(w1[:], att_w1.rearrange("(k p) n -> p k n", k=4)).then_inc(w, 16)
            load_columns(sp, b1[:], att_b1, D).then_inc(w, 16)
            sp.dma_start(w2[:], att_w2).then_inc(w, 16)
            sp.dma_start(b2[:], bass.AP(att_b2.tensor, 0, [[0, P], [1, 1]])).then_inc(w, 16)
            sp.dma_start(misc_t[D_USER:D_USER + 1, :], num1.rearrange("(a n) -> a n", a=1)).then_inc(w, 16)
            sp.dma_start(misc_t[D_USER + 1:XM, :], num2.rearrange("(a n) -> a n", a=1)).then_inc(w, 16)
            sp.dma_start(fc1_m[D_USER:XM, :], fc1_w[0:2, :]).then_inc(w, 16)
            sp.dma_start(fc1_m[0:D_USER, :], fc1_w[2:XM, :]).then_inc(w, 16)
            sp.dma_start(fc1_x[:], fc1_w[XM:XM + 3 * D, :].rearrange("(k p) n -> p k n", k=3)).then_inc(w, 16)
            sp.dma_start(fc2[:], fc2_w.rearrange("(c p) n -> p c n", c=2)).then_inc(w, 16)
            sp.dma_start(fc3[:], fc3_w).then_inc(w, 16)
            sp.dma_start(fc3_bias[:], fc3_b.rearrange("(a n) -> a n", a=1)).then_inc(w, 16)
            sp.dma_start(sc[:, 0], score.rearrange("(a n) -> a n", a=1)).then_inc(w, 16)
            for k, v in enumerate((fc1_b, bn1_g, bn1_b, bn1_m, bn1_v)):
                load_columns(sp, bn1[:, k], v, HC).then_inc(w, 16)
            for k, v in enumerate((fc2_b, bn2_g, bn2_b, bn2_m, bn2_v)):
                load_columns(sp, bn2[:, k], v, H2).then_inc(w, 16)
            sp.wait_ge(ranked_ready, 2)
            for s in range(SEQS):
                for src, dst in ((srt_item, item_d), (srt_cat, cat_d)):
                    sp.dma_start(dst[s].rearrange("(n p r) t -> p n (r t)", p=P, r=R), src[:, s])\
                        .then_inc(sorted_stored, 16)
            sp.wait_ge(tiles_ready, 1)
            sp.dma_start(tiles_d.rearrange("(a g) o -> a (g o)", a=SEQS * NP), group_tiles[:])\
                .then_inc(sorted_stored, 16)
            sp.wait_ge(sorted_stored, 16 * (2 * SEQS + 1))

            def load_index(s, g):
                sp.dma_start(items[s][:], item_d[s, bass.ds(g * P, P), :]).then_inc(index_loaded[s], 16)
                sp.dma_start(cats[s][:], cat_d[s, bass.ds(g * P, P), :]).then_inc(index_loaded[s], 16)
                sp.dma_start(tiles[s][:], tiles_d[bass.ds(g + s * NG, 1), :]).then_inc(index_loaded[s], 16)

            with sp.Fori(0, NG) as g:
                for s in range(SEQS):
                    sp.wait_ge(gathered_item[s], g * (16 * T))
                    sp.wait_ge(gathered_cat[s], g * (16 * T))
                    sp.wait_ge(tiles_known[s], g)
                    load_index(s, g)

            sp.wait_ge(score_step, 7)
            sp.dma_start(out.rearrange("n o -> o n"), sc[:, 1]).then_inc(stored, 16)
            sp.wait_ge(stored, 16)

        @block.gpsimd
        def _(pool):
            nc.gpsimd.memset(ident[:], 0.0).then_inc(ident_set, 1)
            nc.gpsimd.memset(sel[:], 1.0).then_inc(ident_set, 1)
            pool.wait_ge(ident_set, 2)
            nc.gpsimd.affine_select(out=ident[:], in_=ident[:], compare_op=ALU.not_equal, fill=1.0, base=0,
                                    pattern=[[-1, P]], channel_multiplier=1).then_inc(ident_set, 1)
            nc.gpsimd.affine_select(out=sel[:], in_=sel[:], compare_op=ALU.is_ge, fill=0.0, base=0,
                                    pattern=[[-R, GB]], channel_multiplier=1).then_inc(ident_set, 1)
            pool.wait_ge(ident_set, 4)
            nc.gpsimd.affine_select(out=sel[:], in_=sel[:], compare_op=ALU.is_ge, fill=0.0, base=R - 1,
                                    pattern=[[R, GB]], channel_multiplier=-1).then_inc(ident_set, 1)

            def gather(dst, table, index, done):
                pool.indirect_dma_start(dst, None, table,
                                        bass.IndirectOffsetOnAxis(ap=index.bitcast(U32), axis=0)).then_inc(done, 16)

            pool.wait_ge(last_ready, 1)
            gather(last_row[:], emb_item, last_index[:], last_row_in)
            pool.wait_ge(one_ready, 3)
            for n in range(NP):
                gather(cand_rows[:, n, 0:D_ID], emb_item, one_idx[:, 0, n:n + 1], one_gathered)
                gather(cand_rows[:, n, D_ID:D], emb_cat, one_idx[:, 1, n:n + 1], one_gathered)
                gather(user_rows[:, n], emb_user, one_idx[:, 2, n:n + 1], one_gathered)
            pool.wait_ge(last_filled, 1)

            def gather_tiles(s, c, count):
                lo = CUTS[c]
                if lo == T:
                    return
                with pool.If(count > lo):
                    for t in range(lo, CUTS[c + 1]):
                        gather(rows[s][:, t, 0:D_ID], emb_item, items[s][:, t:t + 1], gathered_item[s])
                    gather_tiles(s, c + 1, count)
                with pool.Else():
                    for a in range(lo, T, 15):
                        e = min(a + 15, T)
                        pool.dma_start(rows[s][:, a:e, 0:D_ID], last_rows[:, a:e, :])\
                            .then_inc(gathered_item[s], 16 * (e - a))

            with pool.Fori(0, NG) as g:
                for s in range(SEQS):
                    pool.wait_ge(pooled_ready[s], g)
                    pool.wait_ge(index_loaded[s], (g + 1) * 48)
                    pool.sem_inc(index_seen[s], 1)
                    count = pool.value_load(tiles[s][0:1, 0:1], min_val=0, max_val=T)
                    pool.sem_inc(tiles_known[s], 1)
                    gather_tiles(s, 0, count)
                    for t in range(T):
                        gather(rows[s][:, t, D_ID:D], emb_cat, cats[s][:, t:t + 1], gathered_cat[s])

        @block.vector
        def _(dve):
            steps = [0]

            def link(ins):
                steps[0] += 1
                ins.then_inc(step, 1)
                dve.wait_ge(step, steps[0])

            v = nc.vector
            link(v.memset(key2[:], 0.0))
            last = v.tensor_scalar(last_index[:], key2[:, 0, 0, 0:1], float(N_ITEM - 1), None, ALU.add)
            last.then_inc(last_ready, 1)
            dve.wait_ge(ones_loaded, 48)
            for k, n in enumerate((N_ITEM, N_CAT, N_USER)):
                link(v.tensor_scalar(one_neg[:, k], one_id[:, k], 0.0, float(n), ALU.is_lt, ALU.mult))
                link(v.tensor_tensor(one_f[:, k], one_id[:, k], one_neg[:, k], ALU.add))
                v.tensor_scalar(one_idx[:, k], one_f[:, k], 0.0, float(n - 1), ALU.max, ALU.min).then_inc(one_ready, 1)
            dve.wait_ge(ids_loaded, 64)
            link(v.tensor_scalar(key[:], raw_item[:], 0.0, float(N_ITEM), ALU.is_lt, ALU.mult))
            link(v.tensor_tensor(key[:], raw_item[:], key[:], ALU.add))
            link(v.tensor_scalar(key[:], key[:], 0.0, float(N_ITEM - 1), ALU.max, ALU.min))
            link(v.tensor_scalar(key[:], key[:], -float(1 << SHIFT), float((N_ITEM - 1) << SHIFT), ALU.mult, ALU.add))
            link(v.tensor_scalar(key2[:], raw_cat[:], 0.0, float(N_CAT), ALU.is_lt, ALU.mult))
            link(v.tensor_tensor(key2[:], raw_cat[:], key2[:], ALU.add))
            link(v.tensor_scalar(key2[:], key2[:], 0.0, float(N_CAT - 1), ALU.max, ALU.min))
            link(v.tensor_tensor(key[:], key[:], key2[:], ALU.add))
            kf = key[:].rearrange("p s n l -> p (s n) l")
            rk = ranked[:].rearrange("p s n r t -> p (s n) r t")
            for t in range(T):
                if t:
                    dve.wait_ge(top_kept, t)
                for q in range(SEQS * NP):
                    if t:
                        dve.wait_ge(top_cut, (t - 1) * (SEQS * NP) + q + 1)
                    v.max(top[:, q, :], kf[:, q, :]).then_inc(top_found, 1)
                for q in range(SEQS * NP):
                    dve.wait_ge(top_found, t * (SEQS * NP) + (q + 1))
                    v.match_replace(kf[:, q, :], top[:, q, :], kf[:, q, :], -1.0).then_inc(top_cut, 1)
                v.tensor_copy(rk[:, :, :, t:t + 1], top[:].rearrange("p q (r o) -> p q r o", o=1)).then_inc(top_kept, 1)
            dve.wait_ge(top_kept, T)
            link(v.tensor_scalar(in_range[:], rk[:, :, 0, :], float(1 << SHIFT), None, ALU.is_ge))
            v.reduce_sum(n_tiles[:], in_range[:], AX_X).then_inc(ranked_ready, 1)
            ri = ranked_i[:].rearrange("p s n l -> p (s n l)")
            link(v.tensor_copy(ri, ranked[:].rearrange("p s n r t -> p (s n r t)")))
            si = srt_item[:].rearrange("p s n l -> p (s n l)")
            link(v.tensor_scalar(srt_cat[:].rearrange("p s n l -> p (s n l)"), ri, (1 << SHIFT) - 1, None, ALU.bitwise_and))
            link(v.tensor_scalar(si, ri, SHIFT, None, ALU.logical_shift_right))
            v.tensor_scalar(si, si, -1.0, float(N_ITEM - 1), ALU.mult, ALU.add).then_inc(ranked_ready, 1)
            dve.wait_ge(tiles_turned, 1)
            v.tensor_reduce(group_tiles[:], misc_ps[0:SEQS * NP, 0:P].rearrange("a (g b) -> a g b", b=GB),
                            AX_X, ALU.max).then_inc(tiles_ready, 1)
            dve.wait_ge(last_row_in, 16)
            v.tensor_copy(last_rows[:], last_row[:].rearrange("p (o d) -> p o d", o=1).broadcast_to([P, T, D_ID]))\
                .then_inc(last_filled, 1)
            dve.wait_ge(weights_loaded, 16 * N_WEIGHTS)
            v.tensor_tensor(w_seq[:], w1[:, 0], w1[:, 2], ALU.add).then_inc(head_copied, 1)
            v.tensor_tensor(w_tgt[:], w1[:, 1], w1[:, 2], ALU.subtract).then_inc(head_copied, 1)
            dve.wait_ge(head_turned, 1)
            v.tensor_copy(cand_t[:], turned[0][0:D, :]).then_inc(head_copied, 1)
            v.tensor_copy(misc_t[0:D_USER, :], turned[1][0:D_USER, :]).then_inc(head_copied, 1)
            dve.wait_ge(head_turned, 2)
            v.tensor_scalar(bias_t[:], misc_ps[0:D, :], b1[:, 0:1], None, ALU.add).then_inc(head_copied, 1)
            dve.wait_ge(head_copied, 5)

            with dve.Fori(0, NG) as g:
                dve.wait_ge(pre_ready, g * (SEQS * NH))
                dve.wait_ge(pre_read, g * (2 * NH))
                v.tensor_copy(cand_g[:], cand_t[:, bass.ds(g * GB, GB)]).then_inc(group_set, 1)
                v.tensor_copy(bias_g[:], bias_t[:, bass.ds(g * GB, GB)]).then_inc(group_set, 1)
                dve.wait_ge(group_set, (g + 1) * 2)
                for b in range(GB):
                    ins = v.scalar_tensor_tensor(out=mix[:, b, :], in0=w1[:, 3], scalar=cand_g[:, b:b + 1], in1=w_seq[:],
                                                 op0=ALU.mult, op1=ALU.add)
                ins.then_inc(mix_ready, 1)

                def turn_out(s):
                    for k in range(TB):
                        n = min(TT, T - k * TT)
                        dve.wait_ge(turned_ready, g * (SEQS * TB) + (s * TB + k + 1))
                        src = turned[(s * TB + k) % 2][0:D, 0:n * P].rearrange("d (t b r) -> d t b r", t=n, b=GB)
                        dst = seq_t[s][:, :, k * TT * R:(k * TT + n) * R].rearrange("d b (t r) -> d t b r", t=n)
                        v.tensor_copy(dst, src).then_inc(turned_read, 1)

                def score_out(s):
                    dve.wait_ge(score_ready, g * SEQS + (s + 1))
                    v.tensor_scalar(logits[s][:], score_ps[:, 0:T], b2[:, 0:1], None, ALU.add).then_inc(score_read, 1)

                def softmax(s):
                    at = g * SEQS + (s + 1)
                    dve.wait_ge(logits_moved[s], (g + 1) * 16)
                    v.tensor_reduce(neg_max[s][:], logits_b[s][:], AX_X, ALU.max, negate=True).then_inc(max_ready, 1)
                    dve.wait_ge(exps_ready, at)
                    v.reciprocal(inv[s][:], total[s][:]).then_inc(inv_ready, 1)
                    dve.wait_ge(inv_ready, at)
                    v.tensor_scalar(probs_b[s][:], exps[s][:], inv[s][:, 0:1], None, ALU.mult).then_inc(probs_ready, 1)

                def spread_out(s):
                    dve.wait_ge(probs_moved[s], (g + 1) * 16)
                    v.tensor_tensor(spread[s][:],
                                    probs[s][:].rearrange("p (t o) -> p t o", o=1).broadcast_to([P, T, GB]),
                                    sel[:].rearrange("p (o b) -> p o b", o=1).broadcast_to([P, T, GB]),
                                    ALU.mult).then_inc(spread_ready, 1)

                def pool_out(s):
                    dve.wait_ge(pooled_ready[s], g + 1)
                    v.tensor_copy(pooled_t[s][:, bass.ds(g * GB, GB)], pool_ps[:, 0:GB]).then_inc(pooled_read, 1)

                turn_out(0)
                score_out(0)
                softmax(0)
                turn_out(1)
                spread_out(0)
                score_out(1)
                pool_out(0)
                softmax(1)
                spread_out(1)
                pool_out(1)
            dve.wait_ge(pooled_read, NG * SEQS)

            for k, (bn, w) in enumerate(((bn1, bn1_w), (bn2, bn2_w))):
                link(v.tensor_scalar(w[:, 0], bn[:, 4], BN_EPS, None, ALU.add))
                v.tensor_tensor(w[:, 3], bn[:, 0], bn[:, 3], ALU.subtract).then_inc(bn_ready, 1)
                dve.wait_ge(root_ready, k + 1)
                link(v.reciprocal(w[:, 2], w[:, 1]))
                link(v.tensor_tensor(w[:, 2], w[:, 2], bn[:, 1], ALU.mult))
                dve.wait_ge(bn_ready, 2 * k + 1)
                link(v.tensor_tensor(w[:, 3], w[:, 3], w[:, 2], ALU.mult))
                v.tensor_tensor(w[:, 3], w[:, 3], bn[:, 2], ALU.add).then_inc(bn_ready, 1)
            v.reciprocal(sc[:, 1], sc[:, 0]).then_inc(score_step, 1)
            dve.wait_ge(score_step, 1)
            v.tensor_scalar(sc[:, 2], sc[:, 1], -1.0, None, ALU.add).then_inc(score_step, 1)
            dve.wait_ge(score_step, 4)
            v.tensor_tensor(sc[:, 1], sc[:, 3], sc[:, 4], ALU.subtract).then_inc(score_step, 1)
            dve.wait_ge(score_step, 6)
            link(v.tensor_scalar(sc[:, 3], sc[:, 2], 1.0, None, ALU.add))
            v.reciprocal(sc[:, 1], sc[:, 3]).then_inc(score_step, 1)

        @block.scalar
        def _(act):
            with act.Fori(0, NG) as g:
                act.wait_ge(group_set, (g + 1) * 2)

                def relu_out(s):
                    for k in range(NH):
                        act.wait_ge(pre_ready, g * (SEQS * NH) + (s * NH + k + 1))
                        if k == 0:
                            act.wait_ge(score_ready, g * SEQS)
                        for j in range(2):
                            b = 2 * k + j
                            ins = nc.scalar.activation(hidden[s][:, :, b, :],
                                                       pre_of(s, k)[:, j, 0:L].rearrange("d (t r) -> d t r", r=R),
                                                       ACT.Relu, bias=bias_g[:, b:b + 1])
                        ins.then_inc(pre_read, 1)

                def move_logits(s):
                    act.wait_ge(score_read, g * SEQS + (s + 1))
                    act.dma_start(logits_b[s][:].rearrange("b (r t) -> b r t", r=R),
                                  logits[s][:]).then_inc(logits_moved[s], 16)

                def exp_out(s):
                    act.wait_ge(max_ready, g * SEQS + (s + 1))
                    nc.scalar.activation(exps[s][:], logits_b[s][:], ACT.Exp, bias=neg_max[s][:, 0:1],
                                         accum_out=total[s][:]).then_inc(exps_ready, 1)
                    act.wait_ge(probs_ready, g * SEQS + (s + 1))
                    act.dma_start(probs[s][:], probs_b[s][:].rearrange("b (r t) -> b r t", r=R))\
                        .then_inc(probs_moved[s], 16)

                relu_out(0)
                move_logits(0)
                exp_out(0)
                relu_out(1)
                move_logits(1)
                exp_out(1)

            act.wait_ge(bn_ready, 1)
            for k, (w, n) in enumerate(((bn1_w, 1), (bn2_w, 3))):
                act.wait_ge(bn_ready, n)
                nc.scalar.activation(w[:, 1], w[:, 0], ACT.Sqrt).then_inc(root_ready, 1)
            act.wait_ge(score_step, 2)
            nc.scalar.activation(sc[:, 3], sc[:, 2], ACT.Ln).then_inc(score_step, 1)
            act.wait_ge(bn_ready, 4)
            for c in range(2):
                act.wait_ge(fc_ready, c + 1)
                nc.scalar.activation(h1[:, c], turned[c][0:HC, :], ACT.Relu, bias=bn1_w[:, 3, c:c + 1],
                                     scale=bn1_w[:, 2, c:c + 1]).then_inc(fc_read, 1)
            act.wait_ge(fc_ready, 3)
            nc.scalar.activation(h2[:], score_ps[0:H2, :], ACT.Relu, bias=bn2_w[:, 3, 0:1],
                                 scale=bn2_w[:, 2, 0:1]).then_inc(fc_read, 1)
            act.wait_ge(fc_ready, 4)
            act.wait_ge(score_step, 3)
            nc.scalar.activation(sc[:, 4], misc_ps[0:1, :], ACT.Identity, bias=fc3_bias[:, 0:1]).then_inc(score_step, 1)
            act.wait_ge(score_step, 5)
            nc.scalar.activation(sc[:, 2], sc[:, 1], ACT.Exp).then_inc(score_step, 1)

        @block.tensor
        def _(pe):
            mm = nc.tensor.matmul
            pe.wait_ge(ident_set, 5)
            pe.wait_ge(ranked_ready, 1)
            nc.tensor.transpose(misc_ps[0:SEQS * NP, 0:P], n_tiles[:], ident[:]).then_inc(tiles_turned, 1)
            pe.wait_ge(one_gathered, 16 * 3 * NP)
            for n in range(NP):
                nc.tensor.transpose(turned[0][0:D, n * P:(n + 1) * P], cand_rows[:, n, :], ident[:])
                ins = nc.tensor.transpose(turned[1][0:D_USER, n * P:(n + 1) * P], user_rows[:, n, :], ident[:])
            ins.then_inc(head_turned, 1)
            pe.wait_ge(head_copied, 4)
            pe.wait_ge(tiles_ready, 1)
            mm(misc_ps[0:D, :], w_tgt[:], cand_t[:], start=True, stop=True).then_inc(head_turned, 1)
            pe.wait_ge(head_copied, 5)

            with pe.Fori(0, NG) as g:
                def turn(s):
                    pe.wait_ge(gathered_item[s], (g + 1) * (16 * T))
                    pe.wait_ge(gathered_cat[s], (g + 1) * (16 * T))
                    for k in range(TB):
                        n = s * TB + k
                        if n >= 2:
                            pe.wait_ge(turned_read, g * (SEQS * TB) + (n - 1))
                        else:
                            pe.wait_ge(turned_read, g * (SEQS * TB))
                        for j in range(min(TT, T - k * TT)):
                            t = k * TT + j
                            ins = nc.tensor.transpose(turned[n % 2][0:D, j * P:(j + 1) * P], rows[s][:, t, :], ident[:])
                        ins.then_inc(turned_ready, 1)

                def hide(s):
                    pe.wait_ge(turned_read, g * (SEQS * TB) + (s + 1) * TB)
                    pe.wait_ge(mix_ready, g + 1)
                    for k in range(NH):
                        n = s * NH + k
                        if n >= 2:
                            pe.wait_ge(pre_read, g * (SEQS * NH) + (n - 1))
                        else:
                            pe.wait_ge(pre_read, g * (SEQS * NH))
                        for j in range(2):
                            b = 2 * k + j
                            ins = mm(pre_of(s, k)[:, j, 0:L], mix[:, b, :], seq_t[s][:, b, :], start=True, stop=True)
                        ins.then_inc(pre_ready, 1)

                def score(s):
                    pe.wait_ge(pre_read, g * (SEQS * NH) + (s + 1) * NH)
                    pe.wait_ge(score_read, g * SEQS + s)
                    for t in range(T):
                        ins = mm(score_ps[:, t:t + 1], hidden[s][:, t].rearrange("d b r -> d (b r)"), w2[:],
                                 start=True, stop=True)
                    ins.then_inc(score_ready, 1)

                def pool_rows(s):
                    pe.wait_ge(spread_ready, g * SEQS + (s + 1))
                    pe.wait_ge(pooled_read, g * SEQS + s)
                    for t in range(T):
                        ins = mm(pool_ps[:, 0:GB], rows[s][:, t, :], spread[s][:, t, :],
                                 start=(t == 0), stop=(t == T - 1))
                    ins.then_inc(pooled_ready[s], 1)

                turn(0)
                hide(0)
                score(0)
                turn(1)
                hide(1)
                score(1)
                pool_rows(0)
                pool_rows(1)

            pe.wait_ge(pooled_read, NG * SEQS)
            for c in range(2):
                cols = slice(c * HC, (c + 1) * HC)
                o = turned[c][0:HC, :]
                mm(o, fc1_m[:, cols], misc_t[:], start=True, stop=False)
                mm(o, fc1_x[:, 0, cols], cand_t[:], start=False, stop=False)
                mm(o, fc1_x[:, 1, cols], pooled_t[0][:], start=False, stop=False)
                mm(o, fc1_x[:, 2, cols], pooled_t[1][:], start=False, stop=True).then_inc(fc_ready, 1)
            pe.wait_ge(fc_read, 2)
            for c in range(2):
                ins = mm(score_ps[0:H2, :], fc2[:, c], h1[:, c], start=(c == 0), stop=(c == 1))
            ins.then_inc(fc_ready, 1)
            pe.wait_ge(fc_read, 3)
            mm(misc_ps[0:1, :], fc3[:], h2[:], start=True, stop=True).then_inc(fc_ready, 1)


_INS = ['r_num_feat1', 'r_num_feat2', 'r_score', 'r_user_id', 'r_cand_item_id', 'r_cand_item_cat',
        'r_exp_item_id', 'r_exp_item_cat', 'r_ipv_item_id', 'r_ipv_item_cat',
        'L0_rec_emb_item_id', 'L0_rec_emb_item_cat', 'L0_rec_emb_user',
        'L0_rec_att_w1', 'L0_rec_att_b1', 'L0_rec_att_w2', 'L0_rec_att_b2',
        'L0_rec_fc1_w', 'L0_rec_fc1_b', 'L0_rec_bn1_g', 'L0_rec_bn1_b', 'L0_rec_bn1_m', 'L0_rec_bn1_v',
        'L0_rec_fc2_w', 'L0_rec_fc2_b', 'L0_rec_bn2_g', 'L0_rec_bn2_b', 'L0_rec_bn2_m', 'L0_rec_bn2_v',
        'L0_rec_fc3_w', 'L0_rec_fc3_b']
_OUTS = [((512, 1), 'float32')]


def kernel(**inputs):
    import numpy as _np
    import concourse.bacc as _bacc
    from concourse import mybir as _mybir
    from concourse.bass_utils import run_bass_kernel_spmd as _run

    nc = _bacc.Bacc("TRN2", target_bir_lowering=False, num_devices=1)
    arrays, args = {}, []
    for name in _INS:
        a = _np.ascontiguousarray(inputs[name])
        arrays[f"in_{name}_dram"] = a
        args.append(nc.dram_tensor(f"in_{name}_dram", a.shape, _mybir.dt.from_np(a.dtype), kind="ExternalInput").ap())
    for i, (shape, dtype) in enumerate(_OUTS):
        dt = _mybir.dt.from_np(_np.dtype(dtype))
        args.append(nc.dram_tensor(f"out_{i}_dram", shape, dt, kind="ExternalOutput").ap())
    recommend(nc, *args)
    r = _run(nc, [arrays], core_ids=[0])
    return r.results[0]["out_0_dram"]
```

```python
from contextlib import ExitStack

import concourse.bass as bass
from concourse import mybir

ALU = mybir.AluOpType
ACT = mybir.ActivationFunctionType
F32 = mybir.dt.float32
I32 = mybir.dt.int32
F16 = mybir.dt.float16
BF16 = mybir.dt.bfloat16
U32 = mybir.dt.uint32
AX_X = mybir.AxisListType.X

P = 128
GB = 16
R = P // GB
SEQS = 2
UNITS = 4
Q = 32
HOT_CHUNK = 4
HOT_CHUNKS = 4
HOT = HOT_CHUNK * HOT_CHUNKS
BN_EPS = 1e-05


def recommend(nc, num1, num2, score, user_id, cand_id, cand_cat, exp_id, exp_cat, ipv_id, ipv_cat,
              emb_item, emb_cat, emb_user, att_w1, att_b1, att_w2, att_b2,
              fc1_w, fc1_b, bn1_g, bn1_b, bn1_m, bn1_v, fc2_w, fc2_b, bn2_g, bn2_b, bn2_m, bn2_v,
              fc3_w, fc3_b, out):
    B, L = exp_id.shape
    N_ITEM, D_ID = emb_item.shape
    N_CAT, D_CAT = emb_cat.shape
    N_USER, D_USER = emb_user.shape
    D = D_ID + D_CAT
    H1, H2 = fc2_w.shape
    HC = H1 // 2
    NG = B // GB
    NP = B // P
    T = L // R
    TT = 4
    TB = -(-T // TT)
    NH = GB // 2
    XM = D_USER + 2
    SHIFT = 10
    assert N_CAT <= 1 << SHIFT and N_ITEM << SHIFT < 1 << 24 and T * R == L
    N_WEIGHTS = 23
    COLD = T - HOT
    CK = -(-N_CAT // P)
    TURNS = NG * SEQS // UNITS
    BANKS = UNITS * TB
    PRES = UNITS * NH
    PRE_RING = 3
    TURN_RING = 2 + PRE_RING
    HOT_RING = HOT_CHUNKS
    HOTS = UNITS * HOT_CHUNKS
    NQ = P // Q
    QB = GB // NQ
    CUTS = [0, 4, 6, 7, 8, 9, 11, 14, 18, T]

    with ExitStack() as ctx:
        def sb(name, shape, dt=F32):
            return ctx.enter_context(nc.sbuf_tensor(name, shape, dt))

        def ps(name, shape, dt=F32):
            return ctx.enter_context(nc.psum_tensor(name, shape, dt))

        def sem(name):
            return ctx.enter_context(nc.semaphore(name))

        item_d = nc.dram_tensor("sorted_items", (SEQS, B * R, T), I32, kind="Internal").ap()
        cat_d = nc.dram_tensor("sorted_cats", (SEQS, B * R, T), I32, kind="Internal").ap()
        tiles_d = nc.dram_tensor("tiles_to_gather", (SEQS * NG, 1), I32, kind="Internal").ap()

        hot_cat_d = nc.dram_tensor("hot_cats", (SEQS, NG, HOT, P), F16, kind="Internal").ap()

        ident = sb("ident", [P, P])
        SORT = SEQS * NP * L
        arena = sb("arena", [P, 4 * SORT])

        def sort_part(i):
            return arena[:, i * SORT:(i + 1) * SORT].rearrange("p (s n l) -> p s n l", s=SEQS, n=NP)

        raw_item = sort_part(0).bitcast(I32)
        raw_cat = sort_part(1).bitcast(I32)
        key = sort_part(2)
        ranked = sort_part(3).rearrange("p s n (r t) -> p s n r t", r=R)
        key2 = sort_part(3)
        srt_item, srt_cat, srt_cat_f = raw_item, raw_cat, key
        in_range = sb("in_range", [P, NP, SEQS, T])
        n_tiles = sb("n_tiles", [P, NP, SEQS])
        group_tiles = sb("group_tiles", [SEQS, NP, P // GB], I32)

        one_id = sb("one_id", [P, 3, NP], I32)
        one_f = sb("one_f", [P, 3, NP])
        one_neg = sb("one_neg", [P, 3, NP])
        one_idx = sb("one_idx", [P, 3, NP], I32)
        cand_rows = sb("cand_rows", [P, NP, D])
        user_rows = sb("user_rows", [P, NP, D_USER])
        last_index = sb("last_index", [P, 1], I32)
        last_row = sb("last_row", [P, D_ID])
        last_rows = sb("last_rows", [P, T, D_ID])

        w1 = sb("w1", [D, 4, D])
        w_seq = sb("w_seq", [D, D])
        w_tgt = sb("w_tgt", [D, D])
        b1 = sb("b1", [D, 1])
        w2 = sb("w2", [D, 1])
        b2 = sb("b2", [P, 1])
        cand_t = sb("cand_t", [D, B])
        bias_t = sb("bias_t", [D, B])
        misc_t = sb("misc_t", [XM, B])
        pooled_t = [sb(f"pooled_t{s}", [D, B]) for s in range(SEQS)]
        sel = sb("sel", [P, GB])
        fold_sel = sb("fold_sel", [P, GB])
        w2_wide = sb("w2_wide", [D, 2 * Q - 1])

        cat_f = sb("cat_f", [P, CK, D_CAT])
        cat_rest = sb("cat_rest", [P, CK, D_CAT])
        cat_parts = sb("cat_parts", [P, CK, 3, D_CAT], BF16)
        cat_no_i = sb("cat_no_i", [P, CK], I32)
        cat_no = sb("cat_no", [P, CK])
        hot_cat = sb("hot_cat", [HOT, NP, SEQS, P, R], F16)

        items = [sb(f"items{u}", [P, T], I32) for u in range(UNITS)]
        cats = [sb(f"cats{u}", [P, T], I32) for u in range(UNITS)]
        tiles = [sb(f"tiles{u}", [1, 1], I32) for u in range(UNITS)]
        rows = [sb(f"rows{u}", [P, T, D]) for u in range(UNITS)]
        cand_g = [sb(f"cand_g{i}", [D, GB]) for i in range(2)]
        bias_g = [sb(f"bias_g{i}", [D, GB]) for i in range(2)]
        mix = [sb(f"mix{i}", [D, GB, D]) for i in range(2)]
        hot_ids = [sb(f"hot_ids{s}", [P, HOT * P], F16) for s in range(SEQS)]
        HOT_WORDS = CK * HOT_CHUNK * P // 2
        one_hot = [arena[:, i * HOT_WORDS:(i + 1) * HOT_WORDS].bitcast(BF16)
                   .rearrange("p (c x) -> p c x", c=CK) if (i + 1) * HOT_WORDS <= 4 * SORT
                   else sb(f"one_hot{i}", [P, CK, HOT_CHUNK * P], BF16)[:] for i in range(HOT_RING)]
        seq_t = [sb(f"seq_t{s}", [D, GB, L]) for s in range(SEQS)]
        hidden = [sb(f"hidden{s}", [D, GB, L]) for s in range(SEQS)]
        logits = [sb(f"logits{s}", [P, L]) for s in range(SEQS)]
        neg_max = [sb(f"neg_max{s}", [P, 1]) for s in range(SEQS)]
        exps = [sb(f"exps{s}", [P, L]) for s in range(SEQS)]
        total = [sb(f"total{s}", [P, 1]) for s in range(SEQS)]
        inv = [sb(f"inv{s}", [P, 1]) for s in range(SEQS)]
        probs = [sb(f"probs{s}", [P, T]) for s in range(SEQS)]
        spread = [sb(f"spread{s}", [P, T, GB]) for s in range(SEQS)]
        pooled_rows = sb("pooled_rows", [P, D])

        fc1_m = sb("fc1_m", [XM, H1])
        fc1_x = sb("fc1_x", [D, 3, H1])
        fc2 = sb("fc2", [HC, 2, H2])
        fc3 = sb("fc3", [H2, 1])
        bn1 = sb("bn1", [HC, 5, 2])
        bn2 = sb("bn2", [H2, 5, 1])
        bn1_w = sb("bn1_w", [HC, 4, 2])
        bn2_w = sb("bn2_w", [H2, 4, 1])
        fc3_bias = sb("fc3_bias", [1, 1])
        h1 = arena[0:HC, 0:2 * B].rearrange("h (c b) -> h c b", c=2)
        h2 = arena[0:H2, 2 * B:3 * B]
        fin = [sb("score_row", [1, B])[:], *(arena[0:1, k * B:(k + 1) * B] for k in range(3, 6)),
               sb("mlp_row", [1, B])[:]]

        turned = [ps(f"turned{i}", [P, TT * P]) for i in range(2)]
        pre = [ps(f"pre{i}", [D, 2, 256]) for i in range(PRE_RING)]
        turn_ring = [t[0:D, :] for t in turned] + [p[:].rearrange("d j l -> d (j l)") for p in pre]
        pool_bank = ps("pool_bank", [P, 512])
        score_ps, pool_ps, fold_ps = pool_bank[:, 0:L], pool_bank[:, 256:256 + D], pool_bank[0:D, 384:384 + GB]
        hot_ps = [ps(f"hot_ps{i}", [P, 512]) for i in range(2)]
        misc_ps = hot_ps[0]

        ids_loaded = sem("ids_loaded")
        ones_loaded = sem("ones_loaded")
        weights_loaded = sem("weights_loaded")
        ident_set = sem("ident_set")
        step = sem("step")
        top_found = sem("top_found")
        top_cut = sem("top_cut")
        top_kept = sem("top_kept")
        ranked_ready = sem("ranked_ready")
        tiles_turned = sem("tiles_turned")
        tiles_ready = sem("tiles_ready")
        stored_block = [sem(f"stored_block{n}") for n in range(NP)]
        pool_cleared = sem("pool_cleared")
        one_ready = sem("one_ready")
        last_ready = sem("last_ready")
        last_filled = sem("last_filled")
        last_row_in = sem("last_row_in")
        one_gathered = sem("one_gathered")
        head_turned = sem("head_turned")
        head_copied = sem("head_copied")
        cat_loaded = sem("cat_loaded")
        cat_split = sem("cat_split")
        cat_numbered = sem("cat_numbered")
        hot_turned = sem("hot_turned")
        hot_copied = sem("hot_copied")
        index_loaded = [sem(f"index_loaded{u}") for u in range(UNITS)]
        gathered = [sem(f"gathered{u}") for u in range(UNITS)]
        probs_moved = [sem(f"probs_moved{u}") for u in range(UNITS)]
        hot_loaded = [sem(f"hot_loaded{u}") for u in range(UNITS)]
        slot_free = sem("slot_free")
        index_seen = sem("index_seen")
        tiles_known = sem("tiles_known")
        rows_seen = sem("rows_seen")
        mix_scaled = sem("mix_scaled")
        mix_ready = sem("mix_ready")
        group_set = sem("group_set")
        one_hot_ready = sem("one_hot_ready")
        hot_ready = sem("hot_ready")
        hot_summed = sem("hot_summed")
        turned_ready = sem("turned_ready")
        turned_read = sem("turned_read")
        pre_ready = sem("pre_ready")
        pre_read = sem("pre_read")
        score_ready = sem("score_ready")
        score_read = sem("score_read")
        max_ready = sem("max_ready")
        exps_ready = sem("exps_ready")
        inv_ready = sem("inv_ready")
        probs_ready = sem("probs_ready")
        spread_ready = sem("spread_ready")
        pooled_ready = sem("pooled_ready")
        pooled_copied = sem("pooled_copied")
        folded = sem("folded")
        pooled_read = sem("pooled_read")
        fc_ready = sem("fc_ready")
        fc_read = sem("fc_read")
        root_ready = sem("root_ready")
        bn_ready = sem("bn_ready")
        score_step = sem("score_step")
        stored = sem("stored")

        block = ctx.enter_context(nc.Block())

        def nth(turn, n, each):
            return turn * each + (each + n + 1)

        def landed(turn, v):
            return turn * 16 + (v // UNITS + 1) * 16

        def landed_probs(turn, v):
            return (turn + v // UNITS + 1) * (16 * NQ)

        def group_of(turn, v):
            return turn * (UNITS // SEQS) + v // SEQS

        def turns(eng, body):
            body(0, True, False)
            with eng.Fori(1, TURNS - 1) as turn:
                body(turn, False, False)
            body(TURNS - 1, False, True)

        def load_columns(eng, dst, v, p):
            return eng.dma_start(dst, v.rearrange("(c p) -> p c", p=p), allow_slow_non_contiguous=True)

        @block.sync
        def _(sp):
            for s, (item, cat) in enumerate(((exp_id, exp_cat), (ipv_id, ipv_cat))):
                sp.dma_start(raw_item[:, s], item.rearrange("(n p) l -> p n l", p=P)).then_inc(ids_loaded, 16)
                sp.dma_start(raw_cat[:, s], cat.rearrange("(n p) l -> p n l", p=P)).then_inc(ids_loaded, 16)
            for k, v in enumerate((cand_id, cand_cat, user_id)):
                load_columns(sp, one_id[:, k], v, P).then_inc(ones_loaded, 16)
            w = weights_loaded
            sp.dma_start(w1[:], att_w1.rearrange("(k p) n -> p k n", k=4)).then_inc(w, 16)
            load_columns(sp, b1[:], att_b1, D).then_inc(w, 16)
            sp.dma_start(w2[:], att_w2).then_inc(w, 16)
            sp.dma_start(b2[:], bass.AP(att_b2.tensor, 0, [[0, P], [1, 1]])).then_inc(w, 16)
            sp.dma_start(misc_t[D_USER:D_USER + 1, :], num1.rearrange("(a n) -> a n", a=1)).then_inc(w, 16)
            sp.dma_start(misc_t[D_USER + 1:XM, :], num2.rearrange("(a n) -> a n", a=1)).then_inc(w, 16)
            sp.dma_start(fc1_m[D_USER:XM, :], fc1_w[0:2, :]).then_inc(w, 16)
            sp.dma_start(fc1_m[0:D_USER, :], fc1_w[2:XM, :]).then_inc(w, 16)
            sp.dma_start(fc1_x[:], fc1_w[XM:XM + 3 * D, :].rearrange("(k p) n -> p k n", k=3)).then_inc(w, 16)
            sp.dma_start(fc2[:], fc2_w.rearrange("(c p) n -> p c n", c=2)).then_inc(w, 16)
            sp.dma_start(fc3[:], fc3_w).then_inc(w, 16)
            sp.dma_start(fc3_bias[:], fc3_b.rearrange("(a n) -> a n", a=1)).then_inc(w, 16)
            sp.dma_start(fin[0], score.rearrange("(a n) -> a n", a=1)).then_inc(w, 16)
            for k, v in enumerate((fc1_b, bn1_g, bn1_b, bn1_m, bn1_v)):
                load_columns(sp, bn1[:, k], v, HC).then_inc(w, 16)
            for k, v in enumerate((fc2_b, bn2_g, bn2_b, bn2_m, bn2_v)):
                load_columns(sp, bn2[:, k], v, H2).then_inc(w, 16)
            full = N_CAT // P
            sp.dma_start(cat_f[:, 0:full], emb_cat[0:full * P, :].rearrange("(c p) d -> p c d", p=P)).then_inc(cat_loaded, 16)
            sp.wait_ge(cat_split, 1)
            sp.dma_start(cat_f[0:N_CAT - full * P, full], emb_cat[full * P:N_CAT, :]).then_inc(cat_loaded, 16)

            def load_index(turn, v):
                g, s = group_of(turn, v), v % SEQS
                done = index_loaded[v % UNITS]
                sp.dma_start(items[v % UNITS][:], item_d[s, bass.ds(g * P, P), :]).then_inc(done, 16)
                sp.dma_start(cats[v % UNITS][:], cat_d[s, bass.ds(g * P, P), :]).then_inc(done, 16)
                sp.dma_start(tiles[v % UNITS][:], tiles_d[bass.ds(g + s * NG, 1), :]).then_inc(done, 16)

            def load_hot(turn, v):
                sp.dma_start(hot_ids[v % SEQS][:], hot_cat_d[v % SEQS, bass.ds(group_of(turn, v), 1), :, :]
                             .rearrange("g t x -> g (t x)").broadcast_to([P, HOT * P])).then_inc(hot_loaded[v % UNITS], 16)

            def move_probs(turn, v):
                sp.wait_ge(probs_ready, nth(turn, v, UNITS))
                for q in range(NQ):
                    sp.dma_start(probs[v % SEQS][q * Q:(q + 1) * Q, :],
                                 exps[v % SEQS][q * Q:q * Q + QB, :].rearrange("b (r t) -> b r t", r=R))\
                        .then_inc(probs_moved[v % UNITS], 16)

            sp.wait_ge(stored_block[0], 16 * 5)
            for v in range(UNITS):
                load_index(0, v)
            for v in range(SEQS):
                load_hot(0, v)
            for n in range(1, NP):
                sp.wait_ge(stored_block[n], 16 * 5)

            def body(turn, first, last):
                for u in range(UNITS):
                    if not (first and u == 0):
                        move_probs(turn, u - 1)
                    if not last:
                        sp.wait_ge(rows_seen, nth(turn, u, UNITS))
                        sp.wait_ge(tiles_known, nth(turn, u, UNITS))
                        sp.sem_inc(slot_free, 1)
                        load_index(turn, u + UNITS)
                    if not last or u + SEQS < UNITS:
                        sp.wait_ge(one_hot_ready, nth(turn, (u + 1) * HOT_CHUNKS - 1, HOTS))
                        sp.sem_inc(slot_free, 1)
                        load_hot(turn, u + SEQS)

            turns(sp, body)
            move_probs(TURNS - 1, UNITS - 1)
            sp.wait_ge(score_step, 7)
            sp.dma_start(out.rearrange("n o -> o n"), fin[1]).then_inc(stored, 16)
            sp.wait_ge(stored, 16)

        @block.gpsimd
        def _(pool):
            nc.gpsimd.memset(ident[:], 0.0).then_inc(ident_set, 1)
            nc.gpsimd.memset(sel[:], 1.0).then_inc(ident_set, 1)
            pool.wait_ge(ident_set, 2)
            nc.gpsimd.affine_select(out=ident[:], in_=ident[:], compare_op=ALU.not_equal, fill=1.0, base=0,
                                    pattern=[[-1, P]], channel_multiplier=1).then_inc(ident_set, 1)
            nc.gpsimd.affine_select(out=sel[:], in_=sel[:], compare_op=ALU.is_ge, fill=0.0, base=0,
                                    pattern=[[-R, GB]], channel_multiplier=1).then_inc(ident_set, 1)
            nc.gpsimd.iota(cat_no_i[:], pattern=[[P, CK]], base=0, channel_multiplier=1).then_inc(cat_numbered, 1)
            pool.wait_ge(ident_set, 4)
            nc.gpsimd.affine_select(out=sel[:], in_=sel[:], compare_op=ALU.is_ge, fill=0.0, base=R - 1,
                                    pattern=[[R, GB]], channel_multiplier=-1).then_inc(ident_set, 1)

            nc.gpsimd.memset(fold_sel[:], 0.0).then_inc(ident_set, 1)
            for q in range(NQ):
                pool.wait_ge(ident_set, 6 + q)
                nc.gpsimd.affine_select(out=fold_sel[:], in_=fold_sel[:], compare_op=ALU.not_equal, fill=1.0,
                                        base=-q * Q, pattern=[[-1, GB]], channel_multiplier=1).then_inc(ident_set, 1)

            def gather(dst, table, index, done):
                pool.indirect_dma_start(dst, None, table,
                                        bass.IndirectOffsetOnAxis(ap=index.bitcast(U32), axis=0)).then_inc(done, 16)

            pool.wait_ge(last_ready, 1)
            gather(last_row[:], emb_item, last_index[:], last_row_in)
            pool.wait_ge(one_ready, 3)
            for n in range(NP):
                gather(cand_rows[:, n, 0:D_ID], emb_item, one_idx[:, 0, n:n + 1], one_gathered)
                gather(cand_rows[:, n, D_ID:D], emb_cat, one_idx[:, 1, n:n + 1], one_gathered)
                gather(user_rows[:, n], emb_user, one_idx[:, 2, n:n + 1], one_gathered)
            pool.wait_ge(last_filled, 1)

            def gather_cat(u, t, tiles_done=1):
                pool.indirect_dma_start(rows[u][:, t, D_ID:D], None, emb_cat,
                                        bass.IndirectOffsetOnAxis(ap=cats[u][:, t:t + 1].bitcast(U32), axis=0))\
                    .then_inc(gathered[u], 16 * tiles_done)

            def gather_tiles(u, c, count):
                lo = CUTS[c]
                if lo == T:
                    gather_cat(u, 0)
                    return
                with pool.If(count > lo):
                    for t in range(lo, CUTS[c + 1]):
                        gather(rows[u][:, t, 0:D_ID], emb_item, items[u][:, t:t + 1], gathered[u])
                    gather_tiles(u, c + 1, count)
                with pool.Else():
                    filled = min(T - lo, 15)
                    pool.dma_start(rows[u][:, lo:T, 0:D_ID], last_rows[:, lo:T, :]).then_inc(gathered[u], 16 * filled)
                    gather_cat(u, 0, 1 + T - lo - filled)

            pool.sem_inc(tiles_known, UNITS)
            pool.sem_inc(index_seen, UNITS)
            with pool.Fori(0, TURNS) as turn:
                for u in range(UNITS):
                    pool.wait_ge(pooled_ready, nth(turn, u - UNITS, UNITS))
                    pool.wait_ge(index_loaded[u], (turn + 1) * 48)
                    pool.sem_inc(index_seen, 1)
                    count = pool.value_load(tiles[u][0:1, 0:1], min_val=0, max_val=T)
                    pool.sem_inc(tiles_known, 1)
                    gather_tiles(u, 0, count)
                    for t in range(1, COLD):
                        gather_cat(u, t)

        @block.vector
        def _(dve):
            steps = [0]

            def link(ins):
                steps[0] += 1
                ins.then_inc(step, 1)
                dve.wait_ge(step, steps[0])

            v = nc.vector
            v.memset(cat_f[:, CK - 1], 0.0).then_inc(cat_split, 1)
            link(v.memset(key2, 0.0))
            last = v.tensor_scalar(last_index[:], key2[:, 0, 0, 0:1], float(N_ITEM - 1), None, ALU.add)
            last.then_inc(last_ready, 1)
            dve.wait_ge(ones_loaded, 48)
            for k, n in enumerate((N_ITEM, N_CAT, N_USER)):
                link(v.tensor_scalar(one_neg[:, k], one_id[:, k], 0.0, float(n), ALU.is_lt, ALU.mult))
                link(v.tensor_tensor(one_f[:, k], one_id[:, k], one_neg[:, k], ALU.add))
                v.tensor_scalar(one_idx[:, k], one_f[:, k], 0.0, float(n - 1), ALU.max, ALU.min).then_inc(one_ready, 1)
            dve.wait_ge(ids_loaded, 64)

            def sort_block(n):
                k, k2 = key[:, :, n, :], key2[:, :, n, :]
                item, cat = raw_item[:, :, n, :], raw_cat[:, :, n, :]
                link(v.tensor_scalar(k, item, 0.0, float(N_ITEM), ALU.is_lt, ALU.mult))
                link(v.tensor_tensor(k, item, k, ALU.add))
                link(v.tensor_scalar(k, k, 0.0, float(N_ITEM - 1), ALU.max, ALU.min))
                link(v.tensor_scalar(k, k, -float(1 << SHIFT), float((N_ITEM - 1) << SHIFT), ALU.mult, ALU.add))
                link(v.tensor_scalar(k2, cat, 0.0, float(N_CAT), ALU.is_lt, ALU.mult))
                link(v.tensor_tensor(k2, cat, k2, ALU.add))
                link(v.tensor_scalar(k2, k2, 0.0, float(N_CAT - 1), ALU.max, ALU.min))
                link(v.tensor_tensor(k, k, k2, ALU.add))
                for t in range(T):
                    for s in range(SEQS):
                        at = (n * T + t) * SEQS + s
                        if t:
                            dve.wait_ge(top_cut, at - SEQS + 1)
                        v.max(ranked[:, s, n, :, t], key[:, s, n, :]).then_inc(top_found, 1)
                    for s in range(SEQS):
                        at = (n * T + t) * SEQS + s
                        dve.wait_ge(top_found, at + 1)
                        v.match_replace(key[:, s, n, :], ranked[:, s, n, :, t], key[:, s, n, :], -1.0)\
                            .then_inc(top_cut, 1)
                link(v.tensor_scalar(in_range[:, n], ranked[:, :, n, 0, :], float(1 << SHIFT), None, ALU.is_ge))
                v.reduce_sum(n_tiles[:, n], in_range[:, n], AX_X).then_inc(ranked_ready, 1)
                dve.wait_ge(top_cut, (n + 1) * T * SEQS)
                rank = ranked[:, :, n].rearrange("p s r t -> p s (r t)")
                link(v.tensor_copy(item, rank))
                link(v.tensor_scalar(cat, item, (1 << SHIFT) - 1, None, ALU.bitwise_and))
                v.tensor_copy(k, cat).then_inc(ranked_ready, 1)
                link(v.tensor_scalar(item, item, SHIFT, None, ALU.logical_shift_right))
                v.tensor_scalar(item, item, -1.0, float(N_ITEM - 1), ALU.mult, ALU.add).then_inc(ranked_ready, 1)
                dve.wait_ge(tiles_turned, n + 1)
                v.tensor_reduce(group_tiles[:, n, :], misc_ps[0:SEQS, 0:P].rearrange("a (g b) -> a g b", b=GB),
                                AX_X, ALU.max).then_inc(tiles_ready, 1)
                for s in range(SEQS):
                    for h in range(2):
                        dve.wait_ge(hot_turned, (n * SEQS + s) * 2 + h + 1)
                        half = slice(h * (R // 2), (h + 1) * (R // 2))
                        v.tensor_copy(hot_cat[:, n, s, :, half].rearrange("t x r -> t r x"),
                                      turned[h][0:HOT, :].rearrange("t (r x) -> t r x", x=P)).then_inc(hot_copied, 1)

            sort_block(0)
            dve.wait_ge(cat_loaded, 32)
            link(v.tensor_copy(cat_parts[:, :, 0], cat_f[:]))
            link(v.tensor_tensor(cat_rest[:], cat_f[:], cat_parts[:, :, 0], ALU.subtract))
            link(v.tensor_copy(cat_parts[:, :, 1], cat_rest[:]))
            link(v.tensor_tensor(cat_f[:], cat_rest[:], cat_parts[:, :, 1], ALU.subtract))
            v.tensor_copy(cat_parts[:, :, 2], cat_f[:]).then_inc(cat_split, 1)
            dve.wait_ge(cat_numbered, 1)
            link(v.tensor_copy(cat_no[:], cat_no_i[:]))
            dve.wait_ge(last_row_in, 16)
            v.tensor_copy(last_rows[:], last_row[:].rearrange("p (o d) -> p o d", o=1).broadcast_to([P, T, D_ID]))\
                .then_inc(last_filled, 1)
            dve.wait_ge(weights_loaded, 16 * N_WEIGHTS)
            v.tensor_tensor(w_seq[:], w1[:, 0], w1[:, 2], ALU.add).then_inc(head_copied, 1)
            v.tensor_tensor(w_tgt[:], w1[:, 1], w1[:, 2], ALU.subtract).then_inc(head_copied, 1)
            dve.wait_ge(head_turned, 1)
            v.tensor_copy(cand_t[:], turned[0][0:D, :]).then_inc(head_copied, 1)
            v.tensor_copy(misc_t[0:D_USER, :], turned[1][0:D_USER, :]).then_inc(head_copied, 1)
            dve.wait_ge(head_turned, 2)
            v.tensor_scalar(bias_t[:], misc_ps[0:D, :], b1[:, 0:1], None, ALU.add).then_inc(head_copied, 1)
            dve.wait_ge(head_copied, 5)
            link(v.memset(w2_wide[:], 0.0))
            link(v.tensor_copy(w2_wide[:, Q - 1:Q], w2[:]))
            v.memset(pool_ps, 0.0).then_inc(pool_cleared, 1)
            for n in range(1, NP):
                sort_block(n)

            for n in range(NP):
                dve.wait_ge(stored_block[n], 16 * 5)
            for done, each in ((group_set, UNITS), (one_hot_ready, HOTS), (hot_summed, HOTS),
                               (score_read, UNITS), (max_ready, UNITS), (inv_ready, UNITS), (probs_ready, UNITS),
                               (spread_ready, UNITS), (mix_scaled, UNITS // SEQS), (mix_ready, UNITS // SEQS)):
                dve.sem_inc(done, each)

            def body(turn, first, last):
                def mix_out(u):
                    i = u // SEQS
                    g = group_of(turn, u)
                    dve.wait_ge(pre_read, nth(turn, (u + SEQS - UNITS) * NH - 1, PRES))
                    v.tensor_copy(cand_g[i][:], cand_t[:, bass.ds(g * GB, GB)]).then_inc(group_set, 1)
                    v.tensor_copy(bias_g[i][:], bias_t[:, bass.ds(g * GB, GB)]).then_inc(group_set, 1)
                    dve.wait_ge(group_set, nth(turn, 2 * i + 1, UNITS))
                    v.tensor_tensor(mix[i][:], w1[:, 3:4].broadcast_to([D, GB, D]),
                                    cand_g[i][:].rearrange("d (b o) -> d b o", o=1).broadcast_to([D, GB, D]),
                                    ALU.mult).then_inc(mix_scaled, 1)
                    dve.wait_ge(mix_scaled, nth(turn, i, UNITS // SEQS))
                    v.tensor_tensor(mix[i][:], mix[i][:],
                                    w_seq[:].rearrange("d (o n) -> d o n", o=1).broadcast_to([D, GB, D]),
                                    ALU.add).then_inc(mix_ready, 1)

                def one_hot_out(u, c):
                    n = u * HOT_CHUNKS + c
                    if c == 0:
                        dve.wait_ge(hot_loaded[u % UNITS], landed(turn, u))
                    dve.wait_ge(hot_ready, nth(turn, n - HOT_RING, HOTS))
                    for k in range(CK):
                        ins = v.tensor_scalar(one_hot[n % HOT_RING][:, k, :],
                                              hot_ids[u % SEQS][:, c * HOT_CHUNK * P:(c + 1) * HOT_CHUNK * P],
                                              cat_no[:, k:k + 1], None, ALU.is_equal)
                    ins.then_inc(one_hot_ready, 1)

                def hot_sum(u, c):
                    n = u * HOT_CHUNKS + c
                    t = COLD + c * HOT_CHUNK
                    if c == 0:
                        dve.wait_ge(pooled_ready, nth(turn, u - UNITS, UNITS))
                    dve.wait_ge(hot_ready, nth(turn, n, HOTS))
                    v.tensor_reduce(rows[u % UNITS][:, t:t + HOT_CHUNK, D_ID:D],
                                    hot_ps[n % 2][:, 0:HOT_CHUNK * D].rearrange("p (t k d) -> p t d k", k=3, d=D_CAT),
                                    AX_X, ALU.add).then_inc(hot_summed, 1)

                def score_out(u):
                    s = u % SEQS
                    dve.wait_ge(score_ready, nth(turn, u, UNITS))
                    v.tensor_scalar(logits[s][:], score_ps, b2[:, 0:1], None, ALU.add).then_inc(score_read, 1)

                def max_out(u):
                    s = u % SEQS
                    dve.wait_ge(score_read, nth(turn, u, UNITS))
                    v.tensor_reduce(neg_max[s][:], logits[s][:], AX_X, ALU.max, negate=True).then_inc(max_ready, 1)

                def probs_out(u):
                    s = u % SEQS
                    dve.wait_ge(exps_ready, nth(turn, u, UNITS))
                    v.reciprocal(inv[s][:], total[s][:]).then_inc(inv_ready, 1)
                    dve.wait_ge(inv_ready, nth(turn, u, UNITS))
                    v.tensor_scalar(exps[s][:], exps[s][:], inv[s][:, 0:1], None, ALU.mult).then_inc(probs_ready, 1)

                def spread_out(u):
                    s = u % SEQS
                    dve.wait_ge(pooled_ready, nth(turn, u - 2, UNITS))
                    dve.wait_ge(probs_moved[u % UNITS], landed_probs(turn, u))
                    v.tensor_tensor(spread[s][:],
                                    probs[s][:].rearrange("p (t o) -> p t o", o=1).broadcast_to([P, T, GB]),
                                    sel[:].rearrange("p (o b) -> p o b", o=1).broadcast_to([P, T, GB]),
                                    ALU.mult).then_inc(spread_ready, 1)

                def hot_out(u, after, between):
                    one_hot_out(u, 1)
                    one_hot_out(u, 2)
                    between()
                    hot_sum(u, 0)
                    for c in range(3, HOT_CHUNKS):
                        one_hot_out(u, c)
                        hot_sum(u, c - 2)
                    if after:
                        one_hot_out(u + 1, 0)
                    hot_sum(u, HOT_CHUNKS - 2)
                    hot_sum(u, HOT_CHUNKS - 1)

                if first:
                    one_hot_out(0, 0)
                    hot_out(0, True, lambda: None)
                for u in range(UNITS):
                    behind = not (first and u == 0)
                    if behind:
                        score_out(u - 1)
                        max_out(u - 1)
                    if u % SEQS == 0:
                        mix_out(u)
                    if behind:
                        probs_out(u - 1)
                    if last and u == UNITS - 1:
                        spread_out(u - 1)
                    else:
                        hot_out(u + 1, not (last and u == UNITS - 2), (lambda: spread_out(u - 1)) if behind else (lambda: None))
                if last:
                    score_out(UNITS - 1)
                    max_out(UNITS - 1)
                    probs_out(UNITS - 1)
                    spread_out(UNITS - 1)

            turns(dve, body)
            dve.wait_ge(pooled_read, UNITS + NG * SEQS)

            for k, (bn, w) in enumerate(((bn1, bn1_w), (bn2, bn2_w))):
                link(v.tensor_scalar(w[:, 0], bn[:, 4], BN_EPS, None, ALU.add))
                v.tensor_tensor(w[:, 3], bn[:, 0], bn[:, 3], ALU.subtract).then_inc(bn_ready, 1)
                dve.wait_ge(root_ready, k + 1)
                link(v.reciprocal(w[:, 2], w[:, 1]))
                link(v.tensor_tensor(w[:, 2], w[:, 2], bn[:, 1], ALU.mult))
                dve.wait_ge(bn_ready, 2 * k + 1)
                link(v.tensor_tensor(w[:, 3], w[:, 3], w[:, 2], ALU.mult))
                v.tensor_tensor(w[:, 3], w[:, 3], bn[:, 2], ALU.add).then_inc(bn_ready, 1)
            v.reciprocal(fin[1], fin[0]).then_inc(score_step, 1)
            dve.wait_ge(score_step, 1)
            v.tensor_scalar(fin[2], fin[1], -1.0, None, ALU.add).then_inc(score_step, 1)
            dve.wait_ge(score_step, 4)
            v.tensor_tensor(fin[1], fin[3], fin[4], ALU.subtract).then_inc(score_step, 1)
            dve.wait_ge(score_step, 6)
            link(v.tensor_scalar(fin[3], fin[2], 1.0, None, ALU.add))
            v.reciprocal(fin[1], fin[3]).then_inc(score_step, 1)

        @block.scalar
        def _(act):
            for n in range(NP):
                done = stored_block[n]
                groups = slice(n * (P // GB), (n + 1) * (P // GB))
                act.wait_ge(ranked_ready, 3 * n + 3)
                for src, dst in ((srt_item, item_d), (srt_cat, cat_d)):
                    act.dma_start(dst.rearrange("s (n p r) t -> n p s (r t)", p=P, r=R)[n], src[:, :, n, :])\
                        .then_inc(done, 16)
                act.wait_ge(tiles_ready, n + 1)
                act.dma_start(tiles_d.rearrange("(s g) o -> s (g o)", s=SEQS)[:, groups], group_tiles[:, n, :])\
                    .then_inc(done, 16)
                act.wait_ge(hot_copied, (n + 1) * SEQS * 2)
                for s in range(SEQS):
                    act.dma_start(hot_cat_d[s, groups].rearrange("g t x -> t g x"),
                                  hot_cat[:, n, s].rearrange("t (g b) r -> t g (b r)", b=GB)).then_inc(done, 16)

            for done, each in ((pre_read, PRES), (exps_ready, UNITS), (turned_read, BANKS), (pooled_copied, UNITS),
                               (pooled_read, UNITS)):
                act.sem_inc(done, each)

            def body(turn, first, last):
                def turn_out(u, after_three):
                    act.wait_ge(pre_ready, nth(turn, (u - 2 + 1) * NH - 1, PRES))
                    for k in range(TB):
                        n = min(TT, T - k * TT)
                        act.wait_ge(turned_ready, nth(turn, u * TB + k, BANKS))
                        src = turn_ring[k % TURN_RING][:, 0:n * P].rearrange("d (t b r) -> d t b r", t=n, b=GB)
                        dst = seq_t[u % SEQS][:].rearrange("d b (r t) -> d t b r", r=R)[:, k * TT:k * TT + n]
                        nc.scalar.activation(dst, src, ACT.Copy).then_inc(turned_read, 1)
                        if k == 2:
                            after_three()

                def relu_out(u):
                    s, i = u % SEQS, u // SEQS
                    act.wait_ge(group_set, nth(turn, 2 * i + 1, UNITS))
                    act.wait_ge(score_ready, nth(turn, u - 2, UNITS))
                    for k in range(NH):
                        n = u * NH + k
                        act.wait_ge(pre_ready, nth(turn, n, PRES))
                        for j in range(2):
                            b = 2 * k + j
                            ins = nc.scalar.activation(hidden[s][:, b, :], pre[k % PRE_RING][:, j, 0:L], ACT.Relu,
                                                       bias=bias_g[i][:, b:b + 1])
                        ins.then_inc(pre_read, 1)

                def exp_out(u):
                    s = u % SEQS
                    act.wait_ge(max_ready, nth(turn, u, UNITS))
                    nc.scalar.activation(exps[s][:], logits[s][:], ACT.Exp, bias=neg_max[s][:, 0:1],
                                         accum_out=total[s][:]).then_inc(exps_ready, 1)

                def pool_copy(u):
                    act.wait_ge(pooled_ready, nth(turn, u, UNITS))
                    nc.scalar.activation(pooled_rows[:], pool_ps, ACT.Copy).then_inc(pooled_copied, 1)

                def fold_out(u):
                    act.wait_ge(folded, nth(turn, u, UNITS))
                    nc.scalar.activation(pooled_t[u % SEQS][:, bass.ds(group_of(turn, u) * GB, GB)],
                                         fold_ps, ACT.Copy).then_inc(pooled_read, 1)

                for u in range(UNITS):
                    behind = not (first and u == 0)
                    turn_out(u, (lambda: exp_out(u - 1)) if behind else (lambda: None))
                    relu_out(u)
                    if behind:
                        pool_copy(u - 1)
                        fold_out(u - 1)
                if last:
                    exp_out(UNITS - 1)
                    pool_copy(UNITS - 1)
                    fold_out(UNITS - 1)

            turns(act, body)

            act.wait_ge(bn_ready, 1)
            for k, (w, n) in enumerate(((bn1_w, 1), (bn2_w, 3))):
                act.wait_ge(bn_ready, n)
                nc.scalar.activation(w[:, 1], w[:, 0], ACT.Sqrt).then_inc(root_ready, 1)
            act.wait_ge(score_step, 2)
            nc.scalar.activation(fin[3], fin[2], ACT.Ln).then_inc(score_step, 1)
            act.wait_ge(bn_ready, 4)
            for c in range(2):
                act.wait_ge(fc_ready, c + 1)
                nc.scalar.activation(h1[:, c], turned[c][0:HC, :], ACT.Relu, bias=bn1_w[:, 3, c:c + 1],
                                     scale=bn1_w[:, 2, c:c + 1]).then_inc(fc_read, 1)
            act.wait_ge(fc_ready, 3)
            nc.scalar.activation(h2, pool_bank[0:H2, :], ACT.Relu, bias=bn2_w[:, 3, 0:1],
                                 scale=bn2_w[:, 2, 0:1]).then_inc(fc_read, 1)
            act.wait_ge(fc_ready, 4)
            act.wait_ge(score_step, 3)
            nc.scalar.activation(fin[4], misc_ps[0:1, :], ACT.Identity, bias=fc3_bias[:, 0:1]).then_inc(score_step, 1)
            act.wait_ge(score_step, 5)
            nc.scalar.activation(fin[2], fin[1], ACT.Exp).then_inc(score_step, 1)

        @block.tensor
        def _(pe):
            mm = nc.tensor.matmul
            for done, each in ((rows_seen, UNITS), (hot_ready, HOTS), (turned_ready, BANKS), (pre_ready, PRES),
                               (score_ready, UNITS), (pooled_ready, UNITS), (folded, UNITS)):
                pe.sem_inc(done, each)
            pe.wait_ge(ident_set, 10)

            def turn_block(n):
                pe.wait_ge(ranked_ready, 3 * n + 1)
                nc.tensor.transpose(misc_ps[0:SEQS, 0:P], n_tiles[:, n], ident[:]).then_inc(tiles_turned, 1)
                pe.wait_ge(ranked_ready, 3 * n + 2)
                for s in range(SEQS):
                    for h in range(2):
                        k = (n * SEQS + s) * 2 + h
                        if k >= 2:
                            pe.wait_ge(hot_copied, k - 1)
                        for j in range(R // 2):
                            r = h * (R // 2) + j
                            ins = nc.tensor.transpose(turned[h][0:HOT, j * P:(j + 1) * P],
                                                      srt_cat_f[:, s, n, r * T + COLD:(r + 1) * T], ident[:])
                        ins.then_inc(hot_turned, 1)

            turn_block(0)
            pe.wait_ge(hot_copied, SEQS * 2)
            pe.wait_ge(one_gathered, 16 * 3 * NP)
            for n in range(NP):
                nc.tensor.transpose(turned[0][0:D, n * P:(n + 1) * P], cand_rows[:, n, :], ident[:])
                ins = nc.tensor.transpose(turned[1][0:D_USER, n * P:(n + 1) * P], user_rows[:, n, :], ident[:])
            ins.then_inc(head_turned, 1)
            pe.wait_ge(head_copied, 4)
            pe.wait_ge(tiles_ready, 1)
            mm(misc_ps[0:D, :], w_tgt[:], cand_t[:], start=True, stop=True).then_inc(head_turned, 1)
            pe.wait_ge(head_copied, 5)
            for n in range(1, NP):
                turn_block(n)
            pe.wait_ge(tiles_ready, NP)
            pe.wait_ge(hot_copied, NP * SEQS * 2)
            pe.wait_ge(pool_cleared, 1)

            pe.wait_ge(cat_split, 2)

            def body(turn, first, last):
                def hot(u, chunks, before_last):
                    for c in chunks:
                        if c == HOT_CHUNKS - 1:
                            before_last()
                        n = u * HOT_CHUNKS + c
                        pe.wait_ge(hot_summed, nth(turn, n - 2, HOTS))
                        pe.wait_ge(one_hot_ready, nth(turn, n, HOTS))
                        for t in range(HOT_CHUNK):
                            for k in range(CK):
                                ins = mm(hot_ps[n % 2][:, t * D:(t + 1) * D], one_hot[n % HOT_RING][:, k, t * P:(t + 1) * P],
                                         cat_parts[:, k].rearrange("p k d -> p (k d)"), start=(k == 0), stop=(k == CK - 1))
                        ins.then_inc(hot_ready, 1)

                def turn_rows(u):
                    pe.wait_ge(gathered[u], (turn + 1) * (16 * (T + COLD)))
                    pe.wait_ge(hot_summed, nth(turn, (u + 1) * HOT_CHUNKS - 1, HOTS))
                    pe.wait_ge(turned_read, nth(turn, u * TB - 1, BANKS))
                    pe.wait_ge(pre_read, nth(turn, u * NH - 1, PRES))
                    for k in range(TB):
                        if k >= TURN_RING:
                            pe.wait_ge(turned_read, nth(turn, u * TB + k - TURN_RING, BANKS))
                        for j in range(min(TT, T - k * TT)):
                            ins = nc.tensor.transpose(turn_ring[k % TURN_RING][:, j * P:(j + 1) * P], rows[u][:, k * TT + j, :],
                                                      ident[:])
                        ins.then_inc(turned_ready, 1)
                    pe.sem_inc(rows_seen, 1)

                def hide(u):
                    pe.wait_ge(turned_read, nth(turn, (u + 1) * TB - 1, BANKS))
                    pe.wait_ge(mix_ready, nth(turn, u // SEQS, UNITS // SEQS))
                    for k in range(NH):
                        n = u * NH + k
                        if k >= PRE_RING:
                            pe.wait_ge(pre_read, nth(turn, n - PRE_RING, PRES))
                        for j in range(2):
                            b = 2 * k + j
                            ins = mm(pre[k % PRE_RING][:, j, 0:L], mix[u // SEQS][:, b, :], seq_t[u % SEQS][:, b, :],
                                     start=True, stop=True)
                        ins.then_inc(pre_ready, 1)

                def score(u):
                    pe.wait_ge(pre_read, nth(turn, (u + 1) * NH - 1, PRES))
                    pe.wait_ge(score_read, nth(turn, u - 1, UNITS))
                    pe.wait_ge(pooled_read, nth(turn, u - 1, UNITS))
                    for i in range(QB):
                        for q in range(NQ):
                            ins = mm(score_ps[q * Q:(q + 1) * Q, :], w2_wide[:, Q - 1 - i:2 * Q - 1 - i],
                                     hidden[u % SEQS][:, q * QB + i, :], start=(i == 0), stop=(i == QB - 1))
                    ins.then_inc(score_ready, 1)

                def pool_rows(u):
                    pe.wait_ge(spread_ready, nth(turn, u, UNITS))
                    for t in range(T):
                        q = t % NQ
                        ins = mm(pool_ps[q * Q:q * Q + GB, :], spread[u % SEQS][:, t, :], rows[u % UNITS][:, t, :],
                                 start=(t < NQ), stop=(t + NQ >= T))
                    ins.then_inc(pooled_ready, 1)

                def fold(u):
                    pe.wait_ge(pooled_copied, nth(turn, u, UNITS))
                    mm(fold_ps, pooled_rows[:], fold_sel[:], start=True, stop=True).then_inc(folded, 1)

                if first:
                    hot(0, range(HOT_CHUNKS), lambda: None)
                for u in range(UNITS):
                    behind = not (first and u == 0)
                    fold_behind = (lambda: fold(u - 1)) if behind else (lambda: None)
                    turn_rows(u)
                    if not (last and u == UNITS - 1):
                        hot(u + 1, range(1), lambda: None)
                    hide(u)
                    if behind:
                        pool_rows(u - 1)
                    if last and u == UNITS - 1:
                        fold_behind()
                    else:
                        hot(u + 1, range(1, HOT_CHUNKS), fold_behind)
                    score(u)
                if last:
                    pool_rows(UNITS - 1)
                    fold(UNITS - 1)

            turns(pe, body)

            pe.wait_ge(pooled_read, UNITS + NG * SEQS)
            for c in range(2):
                cols = slice(c * HC, (c + 1) * HC)
                o = turned[c][0:HC, :]
                mm(o, fc1_m[:, cols], misc_t[:], start=True, stop=False)
                mm(o, fc1_x[:, 0, cols], cand_t[:], start=False, stop=False)
                mm(o, fc1_x[:, 1, cols], pooled_t[0][:], start=False, stop=False)
                mm(o, fc1_x[:, 2, cols], pooled_t[1][:], start=False, stop=True).then_inc(fc_ready, 1)
            pe.wait_ge(fc_read, 2)
            for c in range(2):
                ins = mm(pool_bank[0:H2, :], fc2[:, c], h1[:, c], start=(c == 0), stop=(c == 1))
            ins.then_inc(fc_ready, 1)
            pe.wait_ge(fc_read, 3)
            mm(misc_ps[0:1, :], fc3[:], h2, start=True, stop=True).then_inc(fc_ready, 1)


_INS = ['r_num_feat1', 'r_num_feat2', 'r_score', 'r_user_id', 'r_cand_item_id', 'r_cand_item_cat',
        'r_exp_item_id', 'r_exp_item_cat', 'r_ipv_item_id', 'r_ipv_item_cat',
        'L0_rec_emb_item_id', 'L0_rec_emb_item_cat', 'L0_rec_emb_user',
        'L0_rec_att_w1', 'L0_rec_att_b1', 'L0_rec_att_w2', 'L0_rec_att_b2',
        'L0_rec_fc1_w', 'L0_rec_fc1_b', 'L0_rec_bn1_g', 'L0_rec_bn1_b', 'L0_rec_bn1_m', 'L0_rec_bn1_v',
        'L0_rec_fc2_w', 'L0_rec_fc2_b', 'L0_rec_bn2_g', 'L0_rec_bn2_b', 'L0_rec_bn2_m', 'L0_rec_bn2_v',
        'L0_rec_fc3_w', 'L0_rec_fc3_b']
_OUTS = [((512, 1), 'float32')]


def kernel(**inputs):
    import numpy as _np
    import concourse.bacc as _bacc
    from concourse import mybir as _mybir
    from concourse.bass_utils import run_bass_kernel_spmd as _run

    nc = _bacc.Bacc("TRN2", target_bir_lowering=False, num_devices=1)
    arrays, args = {}, []
    for name in _INS:
        a = _np.ascontiguousarray(inputs[name])
        arrays[f"in_{name}_dram"] = a
        args.append(nc.dram_tensor(f"in_{name}_dram", a.shape, _mybir.dt.from_np(a.dtype), kind="ExternalInput").ap())
    for i, (shape, dtype) in enumerate(_OUTS):
        dt = _mybir.dt.from_np(_np.dtype(dtype))
        args.append(nc.dram_tensor(f"out_{i}_dram", shape, dt, kind="ExternalOutput").ap())
    recommend(nc, *args)
    r = _run(nc, [arrays], core_ids=[0])
    return r.results[0]["out_0_dram"]
```

```python
from contextlib import ExitStack

import concourse.bass as bass
from concourse import mybir

ALU = mybir.AluOpType
ACT = mybir.ActivationFunctionType
F32 = mybir.dt.float32
I32 = mybir.dt.int32
F16 = mybir.dt.float16
BF16 = mybir.dt.bfloat16
U32 = mybir.dt.uint32
AX_X = mybir.AxisListType.X

P = 128
GB = 16
R = P // GB
SEQS = 2
UNITS = 4
Q = 32
HOT_TILES = ((5, 4, 4, 4), (5, 4, 5, 4))
HOT_CHUNKS = len(HOT_TILES[0])
HOT = max(map(sum, HOT_TILES))
HALVES = 2
PER_HALF = HOT_CHUNKS // HALVES
CHUNK_AT = [[HOT - sum(chunks[c:]) for c in range(HOT_CHUNKS + 1)] for chunks in HOT_TILES]
HALF_AT = [at[::PER_HALF] for at in CHUNK_AT]
BN_EPS = 1e-05


def recommend(nc, num1, num2, score, user_id, cand_id, cand_cat, exp_id, exp_cat, ipv_id, ipv_cat,
              emb_item, emb_cat, emb_user, att_w1, att_b1, att_w2, att_b2,
              fc1_w, fc1_b, bn1_g, bn1_b, bn1_m, bn1_v, fc2_w, fc2_b, bn2_g, bn2_b, bn2_m, bn2_v,
              fc3_w, fc3_b, out):
    B, L = exp_id.shape
    N_ITEM, D_ID = emb_item.shape
    N_CAT, D_CAT = emb_cat.shape
    N_USER, D_USER = emb_user.shape
    D = D_ID + D_CAT
    H1, H2 = fc2_w.shape
    HC = H1 // 2
    NG = B // GB
    NP = B // P
    T = L // R
    TT = 4
    TB = -(-T // TT)
    PIECES = D // Q
    PIECE = [(*divmod(i, P // Q), *divmod(i, PIECES)) for i in range(P // Q * PIECES)]
    ROUNDS = GB * PIECES * Q // P
    NH = ROUNDS // 2
    XM = D_USER + 2
    SHIFT = 10
    assert N_CAT <= 1 << SHIFT and N_ITEM << SHIFT < 1 << 24 and T * R == L
    N_WEIGHTS = 23
    HOT_FROM = T - HOT
    COLD = [HOT_FROM + at[0] for at in CHUNK_AT]
    CK = -(-N_CAT // P)
    TURNS = NG * SEQS // UNITS
    BLOCK_TURNS = TURNS // NP
    BANKS = UNITS * TB
    PRES = UNITS * NH
    PRE_RING = 3
    TURN_RING = 1 + PRE_RING
    BUILDS = UNITS * HALVES
    HOTS = UNITS * HOT_CHUNKS
    NQ = P // Q
    QB = GB // NQ
    assert QB == NQ and PIECES * Q == D
    CUTS = [0, 4, 6, 7, 8, 9, 11, 14, 18, T]

    with ExitStack() as ctx:
        def sb(name, shape, dt=F32):
            return ctx.enter_context(nc.sbuf_tensor(name, shape, dt))

        def ps(name, shape, dt=F32):
            return ctx.enter_context(nc.psum_tensor(name, shape, dt))

        def sem(name):
            return ctx.enter_context(nc.semaphore(name))

        item_d = nc.dram_tensor("sorted_items", (SEQS, B * R, T), I32, kind="Internal").ap()
        cat_d = nc.dram_tensor("sorted_cats", (SEQS, B * R, T), I32, kind="Internal").ap()
        counts_d = nc.dram_tensor("tiles_to_gather", (SEQS, B), F32, kind="Internal").ap()

        hot_cat_d = nc.dram_tensor("hot_cats", (NG, SEQS, HOT, P), F16, kind="Internal").ap()

        ident = sb("ident", [P, P])
        raw_item = sb("raw_item", [P, SEQS, L], I32)
        raw_cat = sb("raw_cat", [P, SEQS, L], I32)
        key = sb("key", [P, SEQS, L])
        MAX_ROUNDS = T + BLOCK_TURNS - 1
        sort_mem = sb("sort_mem", [P, SEQS * R * MAX_ROUNDS])
        ranked = sort_mem[:].rearrange("p (s r t) -> p s r t", s=SEQS, r=R)
        key2 = sort_mem[:, 0:SEQS * L].rearrange("p (s l) -> p s l", s=SEQS)
        tops = sb("tops", [P, SEQS, R, -(-T // (BLOCK_TURNS - 1))])
        srt_item = sb("srt_item", [P, SEQS, L], I32)
        srt_cat = sb("srt_cat", [P, SEQS, L], I32)
        hot_cat = sb("hot_cat", [P, SEQS, HOT, R], F16)
        in_range = sb("in_range", [P, SEQS, T])
        n_tiles = sb("n_tiles", [P, SEQS])

        one_id = sb("one_id", [P, 3, NP], I32)
        one_f = sb("one_f", [P, 3, NP])
        one_neg = sb("one_neg", [P, 3, NP])
        one_idx = sb("one_idx", [P, 3, NP], I32)
        cand_rows = sb("cand_rows", [P, NP, D])
        user_rows = sb("user_rows", [P, NP, D_USER])
        last_index = sb("last_index", [P, 1], I32)
        last_row = sb("last_row", [P, D_ID])
        last_rows = sb("last_rows", [P, T, D_ID])

        w1 = sb("w1", [D, 4, D])
        w_seq = sb("w_seq", [D, D])
        w_tgt = sb("w_tgt", [D, D])
        b2 = sb("b2", [P, 1])
        cand_t = sb("cand_t", [D, B])
        bias_q = sb("bias_q", [P, B // QB, PIECES])
        b1_w2 = sb("b1_w2", [D, 2])
        b1_w2_q = sb("b1_w2_q", [P, PIECES, 2])
        misc_t = sb("misc_t", [XM, B])
        pooled_t = [sb(f"pooled_t{s}", [D, B]) for s in range(SEQS)]
        sel = sb("sel", [P, GB])
        fold_sel = sb("fold_sel", [P, GB])
        w2_q = sb("w2_q", [P, PIECES, Q])

        cat_f = sb("cat_f", [P, CK, D_CAT])
        cat_rest = sb("cat_rest", [P, CK, D_CAT])
        cat_parts = sb("cat_parts", [P, CK, 3, D_CAT], BF16)
        cat_no_i = sb("cat_no_i", [P, CK], I32)
        cat_no = sb("cat_no", [P, CK])

        items = [sb(f"items{u}", [P, T], I32) for u in range(UNITS)]
        cats = [sb(f"cats{u}", [P, T], I32) for u in range(UNITS)]
        counts = [sb(f"counts{u}", [1, GB]) for u in range(UNITS)]
        tiles = [sb(f"tiles{u}", [1, 1], I32) for u in range(UNITS)]
        rows = [sb(f"rows{u}", [P, T, D]) for u in range(UNITS)]
        cand_g = [sb(f"cand_g{i}", [D, GB]) for i in range(2)]
        bias_g = [sb(f"bias_g{i}", [P, ROUNDS]) for i in range(2)]
        mix = [sb(f"mix{i}", [D, GB, D]) for i in range(2)]
        hot_ids = [sb(f"hot_ids{s}", [P, HOT * P], F16) for s in range(SEQS)]
        TILE_WORDS = CK * P // 2
        half_tiles = max(end - at for halves in HALF_AT for at, end in zip(halves, halves[1:]))
        arena = sb("arena", [P, HALVES, half_tiles * TILE_WORDS])
        one_hot = [[arena[:, half, 0:(halves[half + 1] - halves[half]) * TILE_WORDS].bitcast(BF16)
                    .rearrange("p (c x) -> p c x", c=CK) for half in range(HALVES)] for halves in HALF_AT]
        seq_t = [sb(f"seq_t{s}", [D, GB, L]) for s in range(SEQS)]
        hidden = [sb(f"hidden{s}", [P, ROUNDS, L]) for s in range(SEQS)]
        logits = [sb(f"logits{s}", [P, L]) for s in range(SEQS)]
        neg_max = [sb(f"neg_max{s}", [P, 1]) for s in range(SEQS)]
        exps = [sb(f"exps{s}", [P, L]) for s in range(SEQS)]
        total = [sb(f"total{s}", [P, 1]) for s in range(SEQS)]
        inv = [sb(f"inv{s}", [P, 1]) for s in range(SEQS)]
        probs = [sb(f"probs{s}", [P, T]) for s in range(SEQS)]
        spread = [sb(f"spread{s}", [P, T, GB]) for s in range(SEQS)]
        pooled_rows = sb("pooled_rows", [P, D])

        fc1_m = sb("fc1_m", [XM, H1])
        fc1_x = sb("fc1_x", [D, 3, H1])
        fc2 = sb("fc2", [HC, 2, H2])
        fc3 = sb("fc3", [H2, 1])
        bn1 = sb("bn1", [HC, 5, 2])
        bn2 = sb("bn2", [H2, 5, 1])
        bn1_w = sb("bn1_w", [HC, 4, 2])
        bn2_w = sb("bn2_w", [H2, 4, 1])
        fc3_bias = sb("fc3_bias", [P, 1])
        h1 = arena[0:HC, 0, 0:2 * B].rearrange("h (c b) -> h c b", c=2)
        h2 = arena[0:H2, 0, 2 * B:3 * B]
        fin = [sb(f"final{i}", [P, NP])[:] for i in range(9)]
        PARTS = [slice(0, B - GB), slice(B - GB, B)]

        turned = [ps(f"turned{i}", [P, TT * P]) for i in range(2)]
        pre = [ps(f"pre{i}", [P, 2, 256]) for i in range(PRE_RING)]
        turn_ring = [t[0:D, :] for t in turned] + [p[0:D].rearrange("d j l -> d (j l)") for p in pre[:-1]]
        pool_bank = ps("pool_bank", [P, 512])
        pool_ps, fold_ps = pool_bank[:, 0:D], pool_bank[0:D, 256:256 + GB]
        score_ps = pre[PRE_RING - 1][:, 0, 0:L]
        hot_ps = [ps(f"hot_ps{i}", [P, 512]) for i in range(2)]
        misc_ps = hot_ps[0]
        fc2_ps = turn_ring[2][0:H2, :]

        ids_loaded = sem("ids_loaded")
        ids_used = sem("ids_used")
        ones_loaded = sem("ones_loaded")
        weights_loaded = sem("weights_loaded")
        ident_set = sem("ident_set")
        step = sem("step")
        top_found = sem("top_found")
        top_cut = sem("top_cut")
        tops_kept = sem("tops_kept")
        sort_wait = sem("sort_wait")
        ranked_ready = sem("ranked_ready")
        tiles_counted = sem("tiles_counted")
        stored_ids = sem("stored_ids")
        stored_hot = [sem(f"stored_hot{n}") for n in range(NP)]
        pool_cleared = sem("pool_cleared")
        one_ready = sem("one_ready")
        last_ready = sem("last_ready")
        last_filled = sem("last_filled")
        last_row_in = sem("last_row_in")
        one_gathered = sem("one_gathered")
        head_turned = sem("head_turned")
        head_copied = sem("head_copied")
        cat_loaded = sem("cat_loaded")
        cat_split = sem("cat_split")
        cat_numbered = sem("cat_numbered")
        index_loaded = [sem(f"index_loaded{u}") for u in range(UNITS)]
        gathered = [sem(f"gathered{u}") for u in range(UNITS)]
        probs_moved = [sem(f"probs_moved{u}") for u in range(UNITS)]
        hot_loaded = [sem(f"hot_loaded{u}") for u in range(UNITS)]
        slot_free = sem("slot_free")
        index_seen = sem("index_seen")
        tiles_known = sem("tiles_known")
        rows_seen = sem("rows_seen")
        mix_scaled = sem("mix_scaled")
        mix_ready = sem("mix_ready")
        group_set = sem("group_set")
        one_hot_ready = sem("one_hot_ready")
        hot_ready = sem("hot_ready")
        hot_summed = sem("hot_summed")
        turned_ready = sem("turned_ready")
        turned_read = sem("turned_read")
        pre_ready = sem("pre_ready")
        pre_read = sem("pre_read")
        score_ready = sem("score_ready")
        score_read = sem("score_read")
        max_ready = sem("max_ready")
        exps_ready = sem("exps_ready")
        inv_ready = sem("inv_ready")
        probs_ready = sem("probs_ready")
        spread_ready = sem("spread_ready")
        pooled_ready = sem("pooled_ready")
        pooled_copied = sem("pooled_copied")
        folded = sem("folded")
        pooled_read = sem("pooled_read")
        fc_ready = sem("fc_ready")
        fc_read = sem("fc_read")
        root_ready = sem("root_ready")
        bn_ready = sem("bn_ready")
        score_step = sem("score_step")
        logit_ready = sem("logit_ready")
        exp_ready = sem("exp_ready")
        out_ready = sem("out_ready")
        stored = sem("stored")

        block = ctx.enter_context(nc.Block())

        def nth(turn, n, each):
            return turn * each + (each + n + 1)

        def landed(turn, v):
            return turn * 16 + (v // UNITS + 1) * 16

        def landed_probs(turn, v):
            return (turn + v // UNITS + 1) * (16 * NQ)

        def group_of(turn, v):
            return turn * (UNITS // SEQS) + v // SEQS

        def share(n):
            start, stop = max(0, n * BLOCK_TURNS - 1), (n + 1) * BLOCK_TURNS - 1
            return (start, stop, -(-T // (stop - start))) if n < NP - 1 else (start, TURNS, 0)

        def turns(eng, body, next_block=lambda n: None):
            for n in range(NP):
                start, stop, _ = share(n)
                if n == 0:
                    body(0, n, True, False)
                    start = 1
                if n < NP - 1:
                    with eng.Fori(start, stop) as turn:
                        body(turn, n, False, False)
                    next_block(n + 1)
                else:
                    with eng.Fori(start, stop - 1) as turn:
                        body(turn, n, False, False)
                    body(TURNS - 1, n, False, True)

        def load_columns(eng, dst, v, p):
            return eng.dma_start(dst, v.rearrange("(c p) -> p c", p=p), allow_slow_non_contiguous=True)

        @block.sync
        def _(sp):
            def load_ids(n):
                for s, (item, cat) in enumerate(((exp_id, exp_cat), (ipv_id, ipv_cat))):
                    sp.dma_start(raw_item[:, s], item[n * P:(n + 1) * P, :]).then_inc(ids_loaded, 16)
                    sp.dma_start(raw_cat[:, s], cat[n * P:(n + 1) * P, :]).then_inc(ids_loaded, 16)

            load_ids(0)
            for k, v in enumerate((cand_id, cand_cat, user_id)):
                load_columns(sp, one_id[:, k], v, P).then_inc(ones_loaded, 16)
            w = weights_loaded
            sp.dma_start(w1[:], att_w1.rearrange("(k p) n -> p k n", k=4)).then_inc(w, 16)
            load_columns(sp, b1_w2[:, 0:1], att_b1, D).then_inc(w, 16)
            sp.dma_start(b1_w2[:, 1:2], att_w2).then_inc(w, 16)
            sp.dma_start(b2[:], bass.AP(att_b2.tensor, 0, [[0, P], [1, 1]])).then_inc(w, 16)
            sp.dma_start(misc_t[D_USER:D_USER + 1, :], num1.rearrange("(a n) -> a n", a=1)).then_inc(w, 16)
            sp.dma_start(misc_t[D_USER + 1:XM, :], num2.rearrange("(a n) -> a n", a=1)).then_inc(w, 16)
            sp.dma_start(fc1_m[D_USER:XM, :], fc1_w[0:2, :]).then_inc(w, 16)
            sp.dma_start(fc1_m[0:D_USER, :], fc1_w[2:XM, :]).then_inc(w, 16)
            sp.dma_start(fc1_x[:], fc1_w[XM:XM + 3 * D, :].rearrange("(k p) n -> p k n", k=3)).then_inc(w, 16)
            sp.dma_start(fc2[:], fc2_w.rearrange("(c p) n -> p c n", c=2)).then_inc(w, 16)
            sp.dma_start(fc3[:], fc3_w).then_inc(w, 16)
            sp.dma_start(fc3_bias[:], bass.AP(fc3_b.tensor, 0, [[0, P], [1, 1]])).then_inc(w, 16)
            load_columns(sp, fin[0], score, P).then_inc(w, 16)
            for k, v in enumerate((fc1_b, bn1_g, bn1_b, bn1_m, bn1_v)):
                load_columns(sp, bn1[:, k], v, HC).then_inc(w, 16)
            for k, v in enumerate((fc2_b, bn2_g, bn2_b, bn2_m, bn2_v)):
                load_columns(sp, bn2[:, k], v, H2).then_inc(w, 16)
            full = N_CAT // P
            sp.dma_start(cat_f[:, 0:full], emb_cat[0:full * P, :].rearrange("(c p) d -> p c d", p=P)).then_inc(cat_loaded, 16)
            sp.wait_ge(cat_split, 1)
            sp.dma_start(cat_f[0:N_CAT - full * P, full], emb_cat[full * P:N_CAT, :]).then_inc(cat_loaded, 16)

            def store_ids(n):
                sp.wait_ge(ranked_ready, 3 * n + 3)
                for src, dst in ((srt_item, item_d), (srt_cat, cat_d)):
                    sp.dma_start(dst.rearrange("s (n p r) t -> n p s (r t)", p=P, r=R)[n], src[:]).then_inc(stored_ids, 16)
                sp.dma_start(counts_d.rearrange("s (n p) -> n p s", p=P)[n], n_tiles[:], allow_slow_non_contiguous=True)\
                    .then_inc(stored_ids, 16)

            def store_hot(n):
                for g in range(P // GB):
                    sp.dma_start(hot_cat_d[n * (P // GB) + g].rearrange("s t (b r) -> b (s t) r", r=R),
                                 hot_cat[g * GB:(g + 1) * GB].rearrange("b s t r -> b (s t) r")).then_inc(stored_hot[n], 16)

            def load_index(turn, v):
                g, s = group_of(turn, v), v % SEQS
                done = index_loaded[v % UNITS]
                sp.dma_start(items[v % UNITS][:], item_d[s, bass.ds(g * P, P), :]).then_inc(done, 16)
                sp.dma_start(cats[v % UNITS][:], cat_d[s, bass.ds(g * P, P), :]).then_inc(done, 16)
                sp.dma_start(counts[v % UNITS][:], counts_d[s:s + 1, bass.ds(g * GB, GB)]).then_inc(done, 16)

            def load_hot(turn, v):
                sp.dma_start(hot_ids[v % SEQS][:], hot_cat_d[bass.ds(group_of(turn, v), 1), v % SEQS, :, :]
                             .rearrange("g t x -> g (t x)").broadcast_to([P, HOT * P])).then_inc(hot_loaded[v % UNITS], 16)

            def move_probs(turn, v):
                sp.wait_ge(probs_ready, nth(turn, v, UNITS))
                for q in range(NQ):
                    sp.dma_start(probs[v % SEQS][q * Q:(q + 1) * Q, :],
                                 exps[v % SEQS][q * Q:q * Q + QB, :].rearrange("b (r t) -> b r t", r=R))\
                        .then_inc(probs_moved[v % UNITS], 16)

            sp.wait_ge(ids_used, 1)
            load_ids(1)
            store_ids(0)
            sp.wait_ge(stored_ids, 16 * 3)
            for v in range(UNITS):
                load_index(0, v)
            store_hot(0)
            sp.wait_ge(stored_hot[0], 16 * (P // GB))
            for v in range(SEQS):
                load_hot(0, v)
            sp.wait_ge(ids_used, 2)
            load_ids(2)

            def body(turn, n_block, first, last):
                for u in range(UNITS):
                    if not (first and u == 0):
                        move_probs(turn, u - 1)
                    if u == 0:
                        sp.wait_ge(stored_ids, 16 * 3 * (n_block + 1))
                        sp.wait_ge(stored_hot[n_block], 16 * (P // GB))
                    if not last:
                        sp.wait_ge(rows_seen, nth(turn, u, UNITS))
                        sp.wait_ge(tiles_counted, nth(turn, u, UNITS))
                        sp.sem_inc(slot_free, 1)
                        load_index(turn, u + UNITS)
                    if not last or u + SEQS < UNITS:
                        sp.wait_ge(one_hot_ready, nth(turn, (u + 1) * HALVES - 1, BUILDS))
                        sp.sem_inc(slot_free, 1)
                        load_hot(turn, u + SEQS)

            def next_block(n):
                store_ids(n)
                store_hot(n)
                if n + 2 < NP:
                    sp.wait_ge(ids_used, n + 2)
                    load_ids(n + 2)

            turns(sp, body, next_block)
            move_probs(TURNS - 1, UNITS - 1)
            sp.wait_ge(out_ready, 1)
            sp.dma_start(out.rearrange("(n p) o -> p (n o)", p=P), fin[8], allow_slow_non_contiguous=True)\
                .then_inc(stored, 16)
            sp.wait_ge(stored, 16)

        @block.gpsimd
        def _(pool):
            nc.gpsimd.memset(ident[:], 0.0).then_inc(ident_set, 1)
            nc.gpsimd.memset(sel[:], 1.0).then_inc(ident_set, 1)
            pool.wait_ge(ident_set, 2)
            nc.gpsimd.affine_select(out=ident[:], in_=ident[:], compare_op=ALU.not_equal, fill=1.0, base=0,
                                    pattern=[[-1, P]], channel_multiplier=1).then_inc(ident_set, 1)
            nc.gpsimd.affine_select(out=sel[:], in_=sel[:], compare_op=ALU.is_ge, fill=0.0, base=0,
                                    pattern=[[-R, GB]], channel_multiplier=1).then_inc(ident_set, 1)
            nc.gpsimd.iota(cat_no_i[:], pattern=[[P, CK]], base=0, channel_multiplier=1).then_inc(cat_numbered, 1)
            pool.wait_ge(ident_set, 4)
            nc.gpsimd.affine_select(out=sel[:], in_=sel[:], compare_op=ALU.is_ge, fill=0.0, base=R - 1,
                                    pattern=[[R, GB]], channel_multiplier=-1).then_inc(ident_set, 1)

            nc.gpsimd.memset(fold_sel[:], 0.0).then_inc(ident_set, 1)
            for q in range(NQ):
                pool.wait_ge(ident_set, 6 + q)
                nc.gpsimd.affine_select(out=fold_sel[:], in_=fold_sel[:], compare_op=ALU.not_equal, fill=1.0,
                                        base=-q * Q, pattern=[[-1, GB]], channel_multiplier=1).then_inc(ident_set, 1)

            def gather(dst, table, index, done):
                pool.indirect_dma_start(dst, None, table,
                                        bass.IndirectOffsetOnAxis(ap=index.bitcast(U32), axis=0)).then_inc(done, 16)

            pool.wait_ge(last_ready, 1)
            gather(last_row[:], emb_item, last_index[:], last_row_in)
            pool.wait_ge(one_ready, 3)
            for n in range(NP):
                gather(cand_rows[:, n, 0:D_ID], emb_item, one_idx[:, 0, n:n + 1], one_gathered)
                gather(cand_rows[:, n, D_ID:D], emb_cat, one_idx[:, 1, n:n + 1], one_gathered)
                gather(user_rows[:, n], emb_user, one_idx[:, 2, n:n + 1], one_gathered)
            pool.wait_ge(last_filled, 1)

            def gather_cat(u, t, tiles_done=1):
                pool.indirect_dma_start(rows[u][:, t, D_ID:D], None, emb_cat,
                                        bass.IndirectOffsetOnAxis(ap=cats[u][:, t:t + 1].bitcast(U32), axis=0))\
                    .then_inc(gathered[u], 16 * tiles_done)

            def gather_tiles(u, c, count):
                lo = CUTS[c]
                if lo == T:
                    gather_cat(u, 0)
                    return
                with pool.If(count > lo):
                    for t in range(lo, CUTS[c + 1]):
                        gather(rows[u][:, t, 0:D_ID], emb_item, items[u][:, t:t + 1], gathered[u])
                    gather_tiles(u, c + 1, count)
                with pool.Else():
                    filled = min(T - lo, 15)
                    pool.dma_start(rows[u][:, lo:T, 0:D_ID], last_rows[:, lo:T, :]).then_inc(gathered[u], 16 * filled)
                    gather_cat(u, 0, 1 + T - lo - filled)

            pool.sem_inc(tiles_known, UNITS)
            pool.sem_inc(index_seen, UNITS)
            with pool.Fori(0, TURNS) as turn:
                for u in range(UNITS):
                    pool.wait_ge(pooled_ready, nth(turn, u - UNITS, UNITS))
                    pool.wait_ge(index_loaded[u], (turn + 1) * 48)
                    pool.wait_ge(tiles_counted, nth(turn, u, UNITS))
                    pool.sem_inc(index_seen, 1)
                    count = pool.value_load(tiles[u][0:1, 0:1], min_val=0, max_val=T)
                    pool.sem_inc(tiles_known, 1)
                    gather_tiles(u, 0, count)
                    for t in range(1, COLD[u % SEQS]):
                        gather_cat(u, t)

        @block.vector
        def _(dve):
            steps = [0]

            def link(ins):
                steps[0] += 1
                ins.then_inc(step, 1)
                dve.wait_ge(step, steps[0])

            v = nc.vector
            v.memset(cat_f[:, CK - 1], 0.0).then_inc(cat_split, 1)
            link(v.memset(key2, 0.0))
            last = v.tensor_scalar(last_index[:], key2[:, 0, 0:1], float(N_ITEM - 1), None, ALU.add)
            last.then_inc(last_ready, 1)
            dve.wait_ge(ones_loaded, 48)
            for k, n in enumerate((N_ITEM, N_CAT, N_USER)):
                link(v.tensor_scalar(one_neg[:, k], one_id[:, k], 0.0, float(n), ALU.is_lt, ALU.mult))
                link(v.tensor_tensor(one_f[:, k], one_id[:, k], one_neg[:, k], ALU.add))
                v.tensor_scalar(one_idx[:, k], one_f[:, k], 0.0, float(n - 1), ALU.max, ALU.min).then_inc(one_ready, 1)

            def rounds_before(n):
                return T + sum((stop - start) * rounds for start, stop, rounds in map(share, range(n - 1)))

            def make_keys(n):
                k = key[:]
                dve.wait_ge(ids_loaded, 64 * (n + 1))
                link(v.tensor_scalar(k, raw_item[:], 0.0, float(N_ITEM), ALU.is_lt, ALU.mult))
                link(v.tensor_tensor(k, raw_item[:], k, ALU.add))
                link(v.tensor_scalar(k, k, 0.0, float(N_ITEM - 1), ALU.max, ALU.min))
                link(v.tensor_scalar(k, k, -float(1 << SHIFT), float((N_ITEM - 1) << SHIFT), ALU.mult, ALU.add))
                link(v.tensor_scalar(key2, raw_cat[:], 0.0, float(N_CAT), ALU.is_lt, ALU.mult))
                link(v.tensor_tensor(key2, raw_cat[:], key2, ALU.add))
                link(v.tensor_scalar(key2, key2, 0.0, float(N_CAT - 1), ALU.max, ALU.min))
                link(v.tensor_tensor(k, k, key2, ALU.add))
                dve.sem_inc(ids_used, 1)

            def sort_round(at, top):
                for s in range(SEQS):
                    if not isinstance(at, int) or at > 0:
                        dve.wait_ge(top_cut, at * SEQS + (s + 1 - SEQS))
                        dve.sem_inc(sort_wait, 1)
                    v.max(top(s), key[:, s, :]).then_inc(top_found, 1)
                for s in range(SEQS):
                    dve.wait_ge(top_found, at * SEQS + (s + 1))
                    dve.sem_inc(sort_wait, 1)
                    v.match_replace(key[:, s, :], top(s), key[:, s, :], -1.0).then_inc(top_cut, 1)

            def finish_block(n, rounds):
                if n > 0:
                    dve.wait_ge(stored_ids, 16 * 3 * n)
                    dve.wait_ge(stored_hot[n - 1], 16 * (P // GB))
                dve.wait_ge(top_cut, rounds * SEQS)
                link(v.tensor_scalar(in_range[:], ranked[:, :, 0, 0:T], float(1 << SHIFT), None, ALU.is_ge))
                v.reduce_sum(n_tiles[:], in_range[:], AX_X).then_inc(ranked_ready, 1)
                item, cat = srt_item[:], srt_cat[:]
                link(v.tensor_copy(item.rearrange("p s (r t) -> p s r t", r=R), ranked[:, :, :, 0:T]))
                link(v.tensor_scalar(cat, item, (1 << SHIFT) - 1, None, ALU.bitwise_and))
                v.tensor_copy(hot_cat[:], cat.rearrange("p s (r t) -> p s t r", r=R)[:, :, HOT_FROM:T]).then_inc(ranked_ready, 1)
                link(v.tensor_scalar(item, item, SHIFT, None, ALU.logical_shift_right))
                v.tensor_scalar(item, item, -1.0, float(N_ITEM - 1), ALU.mult, ALU.add).then_inc(ranked_ready, 1)

            def count_out(turn, v):
                dve.wait_ge(index_loaded[v % UNITS], landed(turn, v) * 3)
                dve.wait_ge(tiles_known, nth(turn, v - UNITS, UNITS))
                nc.vector.tensor_reduce(tiles[v % UNITS][:], counts[v % UNITS][:], AX_X, ALU.max).then_inc(tiles_counted, 1)

            make_keys(0)
            for t in range(T):
                sort_round(t, lambda s: ranked[:, s, :, t])
            finish_block(0, T)
            dve.sem_inc(tiles_counted, UNITS)
            dve.wait_ge(weights_loaded, 16 * N_WEIGHTS)
            for k, (bn, w) in enumerate(((bn1, bn1_w), (bn2, bn2_w))):
                link(v.tensor_scalar(w[:, 0], bn[:, 4], BN_EPS, None, ALU.add))
                v.tensor_tensor(w[:, 3], bn[:, 0], bn[:, 3], ALU.subtract).then_inc(bn_ready, 1)
                dve.wait_ge(root_ready, k + 1)
                link(v.reciprocal(w[:, 2], w[:, 1]))
                link(v.tensor_tensor(w[:, 2], w[:, 2], bn[:, 1], ALU.mult))
                dve.wait_ge(bn_ready, 2 * k + 1)
                link(v.tensor_tensor(w[:, 3], w[:, 3], w[:, 2], ALU.mult))
                v.tensor_tensor(w[:, 3], w[:, 3], bn[:, 2], ALU.add).then_inc(bn_ready, 1)
            v.reciprocal(fin[1], fin[0]).then_inc(score_step, 1)
            dve.wait_ge(score_step, 1)
            v.tensor_scalar(fin[2], fin[1], -1.0, None, ALU.add).then_inc(score_step, 1)
            dve.wait_ge(cat_loaded, 32)
            link(v.tensor_copy(cat_parts[:, :, 0], cat_f[:]))
            link(v.tensor_tensor(cat_rest[:], cat_f[:], cat_parts[:, :, 0], ALU.subtract))
            link(v.tensor_copy(cat_parts[:, :, 1], cat_rest[:]))
            link(v.tensor_tensor(cat_f[:], cat_rest[:], cat_parts[:, :, 1], ALU.subtract))
            v.tensor_copy(cat_parts[:, :, 2], cat_f[:]).then_inc(cat_split, 1)
            dve.wait_ge(cat_numbered, 1)
            link(v.tensor_copy(cat_no[:], cat_no_i[:]))
            count_out(0, 0)
            v.tensor_tensor(w_seq[:], w1[:, 0], w1[:, 2], ALU.add).then_inc(head_copied, 1)
            v.tensor_tensor(w_tgt[:], w1[:, 1], w1[:, 2], ALU.subtract).then_inc(head_copied, 1)
            dve.wait_ge(head_turned, 1)
            v.tensor_copy(cand_t[:], turned[0][0:D, :]).then_inc(head_copied, 1)
            v.tensor_copy(misc_t[0:D_USER, :], turned[1][0:D_USER, :]).then_inc(head_copied, 1)
            for u in range(1, UNITS):
                count_out(0, u)
            dve.wait_ge(head_turned, 2)
            link(v.tensor_copy(b1_w2_q[:], turned[0][:, 0:PIECES * 2].rearrange("p (r k) -> p r k", k=2)))
            for r in range(PIECES):
                v.tensor_scalar(bias_q[:, :, r], misc_ps[:, r * (B // QB):(r + 1) * (B // QB)], b1_w2_q[:, r, 0:1], None,
                                ALU.add).then_inc(head_copied, 1)
            dve.wait_ge(head_copied, 4 + PIECES)
            link(v.memset(w2_q[:], 0.0))
            for r, q, b, _ in PIECE:
                ins = v.tensor_copy(w2_q[q * Q:(q + 1) * Q, r, b:b + 1], b1_w2_q[q * Q:(q + 1) * Q, r, 1:2])
            link(ins)
            v.memset(pool_ps, 0.0).then_inc(pool_cleared, 1)
            for done, each in ((group_set, UNITS), (one_hot_ready, BUILDS), (hot_summed, HOTS),
                               (score_read, UNITS), (max_ready, UNITS), (inv_ready, UNITS), (probs_ready, UNITS),
                               (spread_ready, UNITS), (mix_scaled, UNITS // SEQS), (mix_ready, UNITS // SEQS)):
                dve.sem_inc(done, each)

            def body(turn, n_block, first, last):
                def mix_out(u):
                    i = u // SEQS
                    g = group_of(turn, u)
                    cand, bias, m = cand_g[i % 2], bias_g[i % 2], mix[i % 2]
                    dve.wait_ge(pre_read, nth(turn, (u + SEQS - UNITS) * NH - 1, PRES))
                    v.tensor_copy(cand[:], cand_t[:, bass.ds(g * GB, GB)]).then_inc(group_set, 1)
                    v.tensor_copy(bias[:], bias_q[:].rearrange("p f r -> p (f r)")[:, bass.ds(g * ROUNDS, ROUNDS)]).then_inc(group_set, 1)
                    dve.wait_ge(group_set, nth(turn, 2 * i + 1, UNITS))
                    v.tensor_tensor(m[:], w1[:, 3:4].broadcast_to([D, GB, D]),
                                    cand[:].rearrange("d (b o) -> d b o", o=1).broadcast_to([D, GB, D]),
                                    ALU.mult).then_inc(mix_scaled, 1)

                def mix_add(u):
                    i = u // SEQS
                    m = mix[i % 2]
                    dve.wait_ge(mix_scaled, nth(turn, i, UNITS // SEQS))
                    v.tensor_tensor(m[:], m[:],
                                    w_seq[:].rearrange("d (o n) -> d o n", o=1).broadcast_to([D, GB, D]),
                                    ALU.add).then_inc(mix_ready, 1)

                def one_hot_out(u, half, chunks=range(CK)):
                    if chunks[0] == 0:
                        if half == 0:
                            dve.wait_ge(hot_loaded[u % UNITS], landed(turn, u))
                        dve.wait_ge(hot_ready, nth(turn, (u - 1) * HOT_CHUNKS + (half + 1) * PER_HALF - 1, HOTS))
                    columns = slice(HALF_AT[u % SEQS][half] * P, HALF_AT[u % SEQS][half + 1] * P)
                    for k in chunks:
                        ins = v.tensor_scalar(one_hot[u % SEQS][half][:, k, :],
                                              hot_ids[u % SEQS][:, columns],
                                              cat_no[:, k:k + 1], None, ALU.is_equal)
                    if chunks[-1] == CK - 1:
                        ins.then_inc(one_hot_ready, 1)

                def hot_sum(u, c):
                    n = u * HOT_CHUNKS + c
                    t, tiles = HOT_FROM + CHUNK_AT[u % SEQS][c], HOT_TILES[u % SEQS][c]
                    if c == 0:
                        dve.wait_ge(pooled_ready, nth(turn, u - UNITS, UNITS))
                    dve.wait_ge(hot_ready, nth(turn, n, HOTS))
                    v.tensor_reduce(rows[u % UNITS][:, t:t + tiles, D_ID:D],
                                    hot_ps[n % 2][:, 0:tiles * D].rearrange("p (t k d) -> p t d k", k=3, d=D_CAT),
                                    AX_X, ALU.add).then_inc(hot_summed, 1)

                def score_out(u):
                    s = u % SEQS
                    dve.wait_ge(score_ready, nth(turn, u, UNITS))
                    v.tensor_scalar(logits[s][:], score_ps, b2[:, 0:1], None, ALU.add).then_inc(score_read, 1)

                def max_out(u):
                    s = u % SEQS
                    dve.wait_ge(score_read, nth(turn, u, UNITS))
                    v.tensor_reduce(neg_max[s][:], logits[s][:], AX_X, ALU.max, negate=True).then_inc(max_ready, 1)

                def probs_out(u):
                    s = u % SEQS
                    dve.wait_ge(exps_ready, nth(turn, u, UNITS))
                    v.reciprocal(inv[s][:], total[s][:]).then_inc(inv_ready, 1)
                    dve.wait_ge(inv_ready, nth(turn, u, UNITS))
                    v.tensor_scalar(exps[s][:], exps[s][:], inv[s][:, 0:1], None, ALU.mult).then_inc(probs_ready, 1)

                def spread_out(u):
                    s = u % SEQS
                    dve.wait_ge(pooled_ready, nth(turn, u - 2, UNITS))
                    dve.wait_ge(probs_moved[u % UNITS], landed_probs(turn, u))
                    v.tensor_tensor(spread[s][:],
                                    probs[s][:].rearrange("p (t o) -> p t o", o=1).broadcast_to([P, T, GB]),
                                    sel[:].rearrange("p (o b) -> p o b", o=1).broadcast_to([P, T, GB]),
                                    ALU.mult).then_inc(spread_ready, 1)

                def hot_out(u, after, late, between, later):
                    one_hot_out(u, 1)
                    hot_sum(u, 0)
                    late()
                    between()
                    hot_sum(u, 1)
                    later()
                    part = -(-CK // (HOT_CHUNKS - PER_HALF + 1))
                    for i in range(0, CK, part):
                        if after:
                            one_hot_out(u + 1, 0, range(i, min(i + part, CK)))
                        if i // part < HOT_CHUNKS - PER_HALF:
                            hot_sum(u, PER_HALF + i // part)

                start, _, rounds = share(n_block)
                slots = [0, 2, 4, 6, 1, 5, 1, 5, 1, 5]
                assert rounds <= len(slots)
                slots = sorted(slots[:rounds])

                def sort_rounds(slot):
                    for i in range(rounds):
                        if slots[i] == slot:
                            sort_round((turn - start) * rounds + (rounds_before(n_block + 1) + i),
                                       lambda s: tops[:, s, :, i])

                if first:
                    one_hot_out(0, 0)
                    hot_out(0, True, lambda: None, lambda: None, lambda: None)
                    mix_out(0)
                    mix_add(0)
                    make_keys(1)
                for u in range(UNITS):
                    behind = not (first and u == 0)

                    def late():
                        if u % SEQS == SEQS - 1:
                            mix_out(u + 1)
                        sort_rounds(2 * u + 1)

                    def later():
                        if u % SEQS == SEQS - 1:
                            mix_add(u + 1)

                    sort_rounds(2 * u)
                    if behind:
                        probs_out(u - 1)
                    if last and u == UNITS - 1:
                        spread_out(u - 1)
                    else:
                        hot_out(u + 1, not (last and u == UNITS - 2),
                                late, (lambda: spread_out(u - 1)) if behind else (lambda: None), later)
                    if not last:
                        count_out(turn, u + UNITS)
                    if rounds and u == UNITS - 1:
                        dve.wait_ge(top_found, ((turn - start + 1) * rounds + rounds_before(n_block + 1)) * SEQS)
                        v.tensor_copy(ranked[:, :, :, bass.ds((turn - start) * rounds, rounds)], tops[:, :, :, 0:rounds])\
                            .then_inc(tops_kept, 1)
                    score_out(u)
                    max_out(u)
                if last:
                    probs_out(UNITS - 1)
                    spread_out(UNITS - 1)

            def next_block(n):
                dve.wait_ge(tops_kept, share(n - 1)[1])
                finish_block(n, rounds_before(n + 1))
                if n + 1 < NP:
                    make_keys(n + 1)

            turns(dve, body, next_block)
            dve.wait_ge(fc_read, 7)
            v.tensor_tensor(fin[5], fin[3], fin[4], ALU.subtract).then_inc(logit_ready, 1)
            dve.wait_ge(exp_ready, 1)
            link(v.tensor_scalar(fin[7], fin[6], 1.0, None, ALU.add))
            v.reciprocal(fin[8], fin[7]).then_inc(out_ready, 1)

        @block.scalar
        def _(act):
            act.wait_ge(last_row_in, 16)
            nc.scalar.activation(last_rows[:], last_row[:].rearrange("p (o d) -> p o d", o=1).broadcast_to([P, T, D_ID]),
                                 ACT.Copy).then_inc(last_filled, 1)
            for k, (w, n) in enumerate(((bn1_w, 1), (bn2_w, 3))):
                act.wait_ge(bn_ready, n)
                nc.scalar.activation(w[:, 1], w[:, 0], ACT.Sqrt).then_inc(root_ready, 1)
            act.wait_ge(score_step, 2)
            nc.scalar.activation(fin[3], fin[2], ACT.Ln).then_inc(score_step, 1)
            for done, each in ((pre_read, PRES), (exps_ready, UNITS), (turned_read, BANKS), (pooled_copied, UNITS),
                               (pooled_read, UNITS)):
                act.sem_inc(done, each)

            def body(turn, n_block, first, last):
                def turn_out(u, after_three):
                    act.wait_ge(pre_ready, nth(turn, (u - 2 + 1) * NH - 1, PRES))
                    for k in range(TB):
                        n = min(TT, T - k * TT)
                        act.wait_ge(turned_ready, nth(turn, u * TB + k, BANKS))
                        src = turn_ring[k % TURN_RING][:, 0:n * P].rearrange("d (t b r) -> d t b r", t=n, b=GB)
                        dst = seq_t[u % SEQS][:].rearrange("d b (r t) -> d t b r", r=R)[:, k * TT:k * TT + n]
                        nc.scalar.activation(dst, src, ACT.Copy).then_inc(turned_read, 1)
                        if k == TB - 1:
                            after_three()

                def relu_out(u):
                    s, i = u % SEQS, u // SEQS
                    act.wait_ge(group_set, nth(turn, 2 * i + 1, UNITS))
                    act.wait_ge(score_ready, nth(turn, u - 2, UNITS))
                    for k in range(NH):
                        n = u * NH + k
                        act.wait_ge(pre_ready, nth(turn, n, PRES))
                        for j in range(2):
                            r = 2 * k + j
                            ins = nc.scalar.activation(hidden[s][:, r, :], pre[k % PRE_RING][:, j, 0:L], ACT.Relu,
                                                       bias=bias_g[i][:, r:r + 1])
                        ins.then_inc(pre_read, 1)

                def exp_out(u):
                    s = u % SEQS
                    act.wait_ge(max_ready, nth(turn, u, UNITS))
                    nc.scalar.activation(exps[s][:], logits[s][:], ACT.Exp, bias=neg_max[s][:, 0:1],
                                         accum_out=total[s][:]).then_inc(exps_ready, 1)

                def pool_copy(u):
                    act.wait_ge(pooled_ready, nth(turn, u, UNITS))
                    nc.scalar.activation(pooled_rows[:], pool_ps, ACT.Copy).then_inc(pooled_copied, 1)

                def fold_out(u):
                    act.wait_ge(folded, nth(turn, u, UNITS))
                    nc.scalar.activation(pooled_t[u % SEQS][:, bass.ds(group_of(turn, u) * GB, GB)],
                                         fold_ps, ACT.Copy).then_inc(pooled_read, 1)

                for u in range(UNITS):
                    behind = not (first and u == 0)
                    turn_out(u, (lambda: exp_out(u - 1)) if behind else (lambda: None))
                    relu_out(u)
                    if behind:
                        pool_copy(u - 1)
                        fold_out(u - 1)
                if last:
                    exp_out(UNITS - 1)
                    relu_1(PARTS[0], 1)
                    pool_copy(UNITS - 1)
                    fold_out(UNITS - 1)

            def relu_1(cols, n):
                act.wait_ge(bn_ready, 4)
                for c in range(2):
                    act.wait_ge(fc_ready, n + c)
                    nc.scalar.activation(h1[:, c, cols], turned[c][0:HC, cols], ACT.Relu, bias=bn1_w[:, 3, c:c + 1],
                                         scale=bn1_w[:, 2, c:c + 1]).then_inc(fc_read, 1)

            def relu_2(cols, n):
                act.wait_ge(fc_ready, n)
                nc.scalar.activation(h2[:, cols], fc2_ps[:, cols], ACT.Relu, bias=bn2_w[:, 3, 0:1],
                                     scale=bn2_w[:, 2, 0:1]).then_inc(fc_read, 1)

            turns(act, body)

            relu_2(PARTS[0], 3)
            relu_1(PARTS[1], 4)
            relu_2(PARTS[1], 6)
            act.wait_ge(fc_ready, 7)
            nc.scalar.activation(fin[4], misc_ps[:, 0:NP], ACT.Identity, bias=fc3_bias[:, 0:1]).then_inc(fc_read, 1)
            act.wait_ge(logit_ready, 1)
            nc.scalar.activation(fin[6], fin[5], ACT.Exp).then_inc(exp_ready, 1)

        @block.tensor
        def _(pe):
            mm = nc.tensor.matmul
            for done, each in ((rows_seen, UNITS), (hot_ready, HOTS), (turned_ready, BANKS), (pre_ready, PRES),
                               (score_ready, UNITS), (pooled_ready, UNITS), (folded, UNITS)):
                pe.sem_inc(done, each)
            pe.wait_ge(ident_set, 10)

            pe.wait_ge(one_gathered, 16 * 3 * NP)
            for n in range(NP):
                nc.tensor.transpose(turned[0][0:D, n * P:(n + 1) * P], cand_rows[:, n, :], ident[:])
                ins = nc.tensor.transpose(turned[1][0:D_USER, n * P:(n + 1) * P], user_rows[:, n, :], ident[:])
            ins.then_inc(head_turned, 1)
            pe.wait_ge(head_copied, 4)
            for r, q, b, part in PIECE:
                quad, part = slice(q * Q, (q + 1) * Q), slice(part * Q, (part + 1) * Q)
                mm(misc_ps[quad, r * (B // QB):(r + 1) * (B // QB)], w_tgt[:, part],
                   cand_t[:].rearrange("d (f b) -> d b f", b=QB)[:, b], start=True, stop=True)
                ins = mm(turned[0][quad, 2 * r:2 * r + 2], ident[0:D, part], b1_w2[:], start=True, stop=True)
            ins.then_inc(head_turned, 1)
            pe.wait_ge(head_copied, 4 + PIECES)
            pe.wait_ge(pool_cleared, 1)

            pe.wait_ge(cat_split, 2)

            def body(turn, n_block, first, last):
                def hot(u, chunks):
                    for c in chunks:
                        n, s = u * HOT_CHUNKS + c, u % SEQS
                        pe.wait_ge(hot_summed, nth(turn, n - 2, HOTS))
                        half = c // PER_HALF
                        pe.wait_ge(one_hot_ready, nth(turn, u * HALVES + half, BUILDS))
                        for t in range(HOT_TILES[s][c]):
                            column = (CHUNK_AT[s][c] - HALF_AT[s][half] + t) * P
                            for k in range(CK):
                                ins = mm(hot_ps[n % 2][:, t * D:(t + 1) * D], one_hot[s][half][:, k, column:column + P],
                                         cat_parts[:, k].rearrange("p k d -> p (k d)"), start=(k == 0), stop=(k == CK - 1))
                        ins.then_inc(hot_ready, 1)

                def turn_rows(u):
                    pe.wait_ge(gathered[u], (turn + 1) * (16 * (T + COLD[u % SEQS])))
                    pe.wait_ge(turned_read, nth(turn, u * TB - 1, BANKS))
                    pe.wait_ge(pre_read, nth(turn, u * NH - 1, PRES))
                    for k in range(TB):
                        if k >= TURN_RING:
                            pe.wait_ge(turned_read, nth(turn, u * TB + k - TURN_RING, BANKS))
                        for j in range(min(TT, T - k * TT)):
                            if k * TT + j - HOT_FROM in CHUNK_AT[u % SEQS]:
                                c = CHUNK_AT[u % SEQS].index(k * TT + j - HOT_FROM)
                                pe.wait_ge(hot_summed, nth(turn, u * HOT_CHUNKS + c, HOTS))
                            ins = nc.tensor.transpose(turn_ring[k % TURN_RING][:, j * P:(j + 1) * P], rows[u][:, k * TT + j, :],
                                                      ident[:])
                        ins.then_inc(turned_ready, 1)
                    pe.sem_inc(rows_seen, 1)

                def hide(u):
                    pe.wait_ge(turned_read, nth(turn, (u + 1) * TB - 1, BANKS))
                    pe.wait_ge(mix_ready, nth(turn, u // SEQS, UNITS // SEQS))
                    for k in range(NH):
                        n = u * NH + k
                        if k == PRE_RING - 1:
                            pe.wait_ge(score_read, nth(turn, u - 1, UNITS))
                        if k >= PRE_RING:
                            pe.wait_ge(pre_read, nth(turn, n - PRE_RING, PRES))
                        for j in range(2):
                            four, round_of_four = divmod(2 * k + j, PIECES)
                            for r, q, b, part in PIECE:
                                if r == round_of_four:
                                    b += four * QB
                                    ins = mm(pre[k % PRE_RING][q * Q:(q + 1) * Q, j, 0:L],
                                             mix[u // SEQS][:, b, part * Q:(part + 1) * Q], seq_t[u % SEQS][:, b, :],
                                             start=True, stop=True)
                        ins.then_inc(pre_ready, 1)

                def score(u):
                    pe.wait_ge(pre_read, nth(turn, (u + 1) * NH - 1, PRES))
                    pe.wait_ge(score_read, nth(turn, u - 1, UNITS))
                    for r in range(PIECES):
                        for q in range(NQ):
                            ins = mm(score_ps[q * Q:(q + 1) * Q, :], w2_q[:, r], hidden[u % SEQS][:, q * PIECES + r, :],
                                     start=(r == 0), stop=(r == PIECES - 1))
                    ins.then_inc(score_ready, 1)

                def pool_rows(u):
                    pe.wait_ge(pooled_read, nth(turn, u - 1, UNITS))
                    pe.wait_ge(spread_ready, nth(turn, u, UNITS))
                    for t in range(T):
                        q = t % NQ
                        ins = mm(pool_ps[q * Q:q * Q + GB, :], spread[u % SEQS][:, t, :], rows[u % UNITS][:, t, :],
                                 start=(t < NQ), stop=(t + NQ >= T))
                    ins.then_inc(pooled_ready, 1)

                def fold(u):
                    pe.wait_ge(pooled_copied, nth(turn, u, UNITS))
                    mm(fold_ps, pooled_rows[:], fold_sel[:], start=True, stop=True).then_inc(folded, 1)

                if first:
                    hot(0, range(HOT_CHUNKS))
                for u in range(UNITS):
                    behind = not (first and u == 0)
                    ahead = not (last and u == UNITS - 1)
                    turn_rows(u)
                    if ahead:
                        hot(u + 1, range(1))
                    hide(u)
                    if ahead:
                        hot(u + 1, range(1, HOT_CHUNKS - 1))
                    if behind:
                        pool_rows(u - 1)
                    if ahead:
                        hot(u + 1, range(HOT_CHUNKS - 1, HOT_CHUNKS))
                    score(u)
                    if behind:
                        fold(u - 1)
                if last:
                    pe.wait_ge(pooled_read, nth(turn, UNITS - SEQS - 1, UNITS))
                    pe.wait_ge(turned_read, nth(turn, BANKS - 1, BANKS))
                    fc_1(PARTS[0])
                    pool_rows(UNITS - 1)
                    fold(UNITS - 1)

            def fc_1(cols):
                for c in range(2):
                    half = slice(c * HC, (c + 1) * HC)
                    o = turned[c][0:HC, cols]
                    mm(o, fc1_m[:, half], misc_t[:, cols], start=True, stop=False)
                    mm(o, fc1_x[:, 0, half], cand_t[:, cols], start=False, stop=False)
                    mm(o, fc1_x[:, 1, half], pooled_t[0][:, cols], start=False, stop=False)
                    mm(o, fc1_x[:, 2, half], pooled_t[1][:, cols], start=False, stop=True).then_inc(fc_ready, 1)

            def fc_2(cols):
                for c in range(2):
                    ins = mm(fc2_ps[:, cols], fc2[:, c], h1[:, c, cols], start=(c == 0), stop=(c == 1))
                ins.then_inc(fc_ready, 1)

            turns(pe, body)

            pe.wait_ge(fc_read, 2)
            fc_2(PARTS[0])
            pe.wait_ge(pooled_read, UNITS + NG * SEQS)
            fc_1(PARTS[1])
            pe.wait_ge(fc_read, 5)
            fc_2(PARTS[1])
            pe.wait_ge(fc_read, 6)
            for n in range(NP):
                ins = mm(misc_ps[:, n:n + 1], h2[:, n * P:(n + 1) * P], fc3[:], start=True, stop=True)
            ins.then_inc(fc_ready, 1)


_INS = ['r_num_feat1', 'r_num_feat2', 'r_score', 'r_user_id', 'r_cand_item_id', 'r_cand_item_cat',
        'r_exp_item_id', 'r_exp_item_cat', 'r_ipv_item_id', 'r_ipv_item_cat',
        'L0_rec_emb_item_id', 'L0_rec_emb_item_cat', 'L0_rec_emb_user',
        'L0_rec_att_w1', 'L0_rec_att_b1', 'L0_rec_att_w2', 'L0_rec_att_b2',
        'L0_rec_fc1_w', 'L0_rec_fc1_b', 'L0_rec_bn1_g', 'L0_rec_bn1_b', 'L0_rec_bn1_m', 'L0_rec_bn1_v',
        'L0_rec_fc2_w', 'L0_rec_fc2_b', 'L0_rec_bn2_g', 'L0_rec_bn2_b', 'L0_rec_bn2_m', 'L0_rec_bn2_v',
        'L0_rec_fc3_w', 'L0_rec_fc3_b']
_OUTS = [((512, 1), 'float32')]


def kernel(**inputs):
    import numpy as _np
    import concourse.bacc as _bacc
    from concourse import mybir as _mybir
    from concourse.bass_utils import run_bass_kernel_spmd as _run

    nc = _bacc.Bacc("TRN2", target_bir_lowering=False, num_devices=1)
    arrays, args = {}, []
    for name in _INS:
        a = _np.ascontiguousarray(inputs[name])
        arrays[f"in_{name}_dram"] = a
        args.append(nc.dram_tensor(f"in_{name}_dram", a.shape, _mybir.dt.from_np(a.dtype), kind="ExternalInput").ap())
    for i, (shape, dtype) in enumerate(_OUTS):
        dt = _mybir.dt.from_np(_np.dtype(dtype))
        args.append(nc.dram_tensor(f"out_{i}_dram", shape, dt, kind="ExternalOutput").ap())
    recommend(nc, *args)
    r = _run(nc, [arrays], core_ids=[0])
    return r.results[0]["out_0_dram"]
```
